# Optimizing a Trainium2 kernel written in Bass

```python
import numpy as np
import jax
import jax.numpy as jnp

def _softmax(x, axis=-1):
    return jax.nn.softmax(x, axis=axis)

def _gelu(x):
    return jax.nn.gelu(x, approximate=True)

def _silu(x):
    return jax.nn.silu(x)

def _sigmoid(x):
    return jax.nn.sigmoid(x)

def _layernorm(x, axis=-1, eps=1e-05):
    m = jnp.mean(x, axis=axis, keepdims=True)
    v = jnp.var(x, axis=axis, keepdims=True)
    return (x - m) / jnp.sqrt(v + eps)

def _scatter_add(tgt, idx, src, axis=0):
    return tgt.at[idx].add(src)

def _segment_sum(src, seg, n):
    return jax.ops.segment_sum(src, seg, n)
kernel_name = 'mk_gnn_preln_d4_gnn_r8_eb4935'

def setup_inputs(seed: int=0):
    np.random.seed(seed)
    _w = jnp.asarray

    def _rec_inputs():
        import jax
        import jax.numpy as jnp
        _gk = jax.random.key(seed)
        x = -0.0009044 + 1 * jax.random.normal(jax.random.fold_in(_gk, 1), (12500, 16), jnp.float32)
        _s = jax.random.randint(jax.random.fold_in(_gk, 2), (200000,), 0, 12500, jnp.int32)
        _d = jax.random.randint(jax.random.fold_in(_gk, 3), (200000,), 0, 12500, jnp.int32)
        _loop = jnp.arange(12500, dtype=jnp.int32)
        src = jnp.concatenate([_s, _d, _loop])
        dst = jnp.concatenate([_d, _s, _loop])
        _o = jnp.argsort(dst, stable=True)
        src = src[_o]
        dst = dst[_o]
        edge_attr_8 = -5.3897e-05 + 0.999841 * jax.random.normal(jax.random.fold_in(_gk, 12), (412500, 8), jnp.float32)
        edge_weight = jax.random.uniform(jax.random.fold_in(_gk, 14), (412500,), jnp.float32, 0.0, 1)
        node_vec1 = -0.00472126 + 0.997171 * jax.random.normal(jax.random.fold_in(_gk, 15), (12500, 1), jnp.float32)
        return (x, src, dst, edge_attr_8, edge_weight, node_vec1)
    x, src, dst, edge_attr_8, edge_weight, node_vec1 = _rec_inputs()

    def _L0_gnn_setup():
        import jax, jax.numpy as jnp
        import numpy as np
        N_NODES = 12500
        N_EDGES = 400000
        D_NODE = 16
        D_EDGE = 8
        D_HIDDEN = 16
        key = jax.random.key(seed)
        ks = jax.random.split(key, 8)
        node_features = jax.random.normal(ks[0], (N_NODES, D_NODE), dtype=jnp.float32)
        edge_attr_e3nn = jax.random.normal(ks[1], (N_EDGES, D_EDGE), dtype=jnp.float32)
        node_attr_scalar_raw = jax.random.normal(ks[2], (N_NODES, 1), dtype=jnp.float32)
        W_msg_tp = jax.random.normal(ks[3], (D_NODE, D_EDGE, D_HIDDEN), dtype=jnp.float32)
        W_msg_lin = jax.random.normal(ks[4], (D_HIDDEN, D_HIDDEN), dtype=jnp.float32)
        W_upd_tp = jax.random.normal(ks[5], (D_NODE, D_HIDDEN, D_HIDDEN), dtype=jnp.float32)
        W_upd_lin = jax.random.normal(ks[6], (D_HIDDEN, D_NODE), dtype=jnp.float32)
        edge_index = jax.random.randint(ks[7], (2, N_EDGES), 0, N_NODES, dtype=jnp.int64)
        return {'node_features': node_features, 'edge_attr_e3nn': edge_attr_e3nn, 'node_attr_scalar_raw': node_attr_scalar_raw, 'W_msg_tp': W_msg_tp, 'W_msg_lin': W_msg_lin, 'W_upd_tp': W_upd_tp, 'W_upd_lin': W_upd_lin, 'edge_index': edge_index}
    _L0_gnn_all = _L0_gnn_setup()
    _L0_gnn_in = {k: v for k, v in _L0_gnn_all.items() if k in ('W_msg_tp', 'W_msg_lin', 'W_upd_tp', 'W_upd_lin')}
    del _L0_gnn_all

    def _L1_gnn_setup():
        import jax, jax.numpy as jnp
        import numpy as np
        N_NODES = 12500
        N_EDGES = 200000
        IN_C = 16
        OUT_C = 16
        N_EATTR = 8
        key = jax.random.key(seed)
        k1, k2, k3, k4 = jax.random.split(key, 4)
        x = jax.random.normal(k1, (N_NODES, IN_C), dtype=jnp.float32)
        edge_index = jax.random.randint(k2, (2, N_EDGES), 0, N_NODES, dtype=jnp.int64)
        edge_attr = jax.random.normal(k3, (N_EDGES, N_EATTR), dtype=jnp.float32)
        weight_matrix = jax.random.normal(k4, (N_EATTR, OUT_C, IN_C), dtype=jnp.float32) * 0.1
        bias = jnp.zeros((OUT_C,), dtype=jnp.float32)
        return {'x': x, 'edge_index': edge_index, 'edge_attr': edge_attr, 'weight_matrix': weight_matrix, 'bias': bias, 'num_nodes': N_NODES}
    _L1_gnn_all = _L1_gnn_setup()
    _L1_gnn_in = {k: v for k, v in _L1_gnn_all.items() if k in ('weight_matrix', 'bias')}
    del _L1_gnn_all

    def _L2_gnn_setup():
        import jax, jax.numpy as jnp
        import numpy as np
        N = 6250
        E = 100000
        S = 2
        D_NODE_IN, D_EDGE_IN, D, H, D_OUT = (16, 8, 64, 64, 16)
        LN_EPS = 1e-05

        def _mlp(x, w0, b0, w1, b1):
            return jax.nn.silu(x @ w0 + b0) @ w1 + b1

        def _ln(x, g, b):
            m = jnp.mean(x, axis=-1, keepdims=True)
            v = jnp.var(x, axis=-1, keepdims=True)
            return (x - m) * jax.lax.rsqrt(v + LN_EPS) * g + b
        key = jax.random.key(seed)
        ks = iter(jax.random.split(key, 40))
        p = lambda shape: jax.random.normal(next(ks), shape, dtype=jnp.float32) * 0.1
        inp = {'node_feat': jax.random.normal(next(ks), (N, D_NODE_IN), dtype=jnp.float32), 'edge_feat': jax.random.normal(next(ks), (E, D_EDGE_IN), dtype=jnp.float32), 'senders': jax.random.randint(next(ks), (E,), 0, N, dtype=jnp.int32), 'receivers': jax.random.randint(next(ks), (E,), 0, N, dtype=jnp.int32), 'node_enc_w0': p((D_NODE_IN, H)), 'node_enc_b0': p((H,)), 'node_enc_w1': p((H, D)), 'node_enc_b1': p((D,)), 'node_enc_g': jnp.ones((D,), jnp.float32), 'node_enc_beta': jnp.zeros((D,), jnp.float32), 'edge_enc_w0': p((D_EDGE_IN, H)), 'edge_enc_b0': p((H,)), 'edge_enc_w1': p((H, D)), 'edge_enc_b1': p((D,)), 'edge_enc_g': jnp.ones((D,), jnp.float32), 'edge_enc_beta': jnp.zeros((D,), jnp.float32), 'edge_blk_w0': p((S, 3 * D, H)), 'edge_blk_b0': p((S, H)), 'edge_blk_w1': p((S, H, D)), 'edge_blk_b1': p((S, D)), 'edge_blk_g': jnp.ones((S, D), jnp.float32), 'edge_blk_beta': jnp.zeros((S, D), jnp.float32), 'node_blk_w0': p((S, 2 * D, H)), 'node_blk_b0': p((S, H)), 'node_blk_w1': p((S, H, D)), 'node_blk_b1': p((S, D)), 'node_blk_g': jnp.ones((S, D), jnp.float32), 'node_blk_beta': jnp.zeros((S, D), jnp.float32), 'dec_w0': p((D, H)), 'dec_b0': p((H,)), 'dec_w1': p((H, D_OUT)), 'dec_b1': p((D_OUT,))}
        return inp
    _L2_gnn_all = _L2_gnn_setup()
    _L2_gnn_in = {k: v for k, v in _L2_gnn_all.items() if k in ('node_enc_w0', 'node_enc_b0', 'node_enc_w1', 'node_enc_b1', 'node_enc_g', 'node_enc_beta', 'edge_enc_w0', 'edge_enc_b0', 'edge_enc_w1', 'edge_enc_b1', 'edge_enc_g', 'edge_enc_beta', 'edge_blk_w0', 'edge_blk_b0', 'edge_blk_w1', 'edge_blk_b1', 'edge_blk_g', 'edge_blk_beta', 'node_blk_w0', 'node_blk_b0', 'node_blk_w1', 'node_blk_b1', 'node_blk_g', 'node_blk_beta', 'dec_w0', 'dec_b0', 'dec_w1', 'dec_b1')}
    del _L2_gnn_all

    def _L3_gnn_setup():
        import jax, jax.numpy as jnp
        import numpy as np
        N_NODES = 12500
        N_EDGES = 400000
        F_IN = 16
        F_HID = 32

        def _gcn_conv(x, row, col, edge_w, W, b, num_nodes):
            loop = jnp.arange(num_nodes)
            r = jnp.concatenate([row, loop])
            c = jnp.concatenate([col, loop])
            ew = jnp.concatenate([edge_w, jnp.ones((num_nodes,), dtype=edge_w.dtype)])
            deg = jax.ops.segment_sum(ew, c, num_segments=num_nodes)
            dis = jnp.where(deg > 0, jax.lax.rsqrt(deg), 0.0)
            norm = dis[r] * ew * dis[c]
            xw = x @ W.T
            msg = xw[r] * norm[:, None]
            out = jax.ops.segment_sum(msg, c, num_segments=num_nodes)
            return out + b
        key = jax.random.key(seed)
        ks = jax.random.split(key, 8)
        x = jax.random.normal(ks[0], (N_NODES, F_IN), dtype=jnp.float32)
        edge_index = jax.random.randint(ks[1], (2, N_EDGES), 0, N_NODES, dtype=jnp.int64)
        edge_w = jax.random.uniform(ks[2], (N_EDGES,), dtype=jnp.float32)
        W1 = jax.random.normal(ks[3], (F_HID, F_IN), dtype=jnp.float32) * 0.1
        b1 = jax.random.normal(ks[4], (F_HID,), dtype=jnp.float32) * 0.1
        W2 = jax.random.normal(ks[5], (F_IN, F_HID), dtype=jnp.float32) * 0.1
        b2 = jax.random.normal(ks[6], (F_IN,), dtype=jnp.float32) * 0.1
        return {'x': x, 'edge_index': edge_index, 'edge_w': edge_w, 'W1': W1, 'b1': b1, 'W2': W2, 'b2': b2, 'num_nodes': N_NODES}
    _L3_gnn_all = _L3_gnn_setup()
    _L3_gnn_in = {k: v for k, v in _L3_gnn_all.items() if k in ('W1', 'b1', 'W2', 'b2')}
    del _L3_gnn_all
    return {'x': x, 'src': src, 'dst': dst, 'edge_attr_8': edge_attr_8, 'edge_weight': edge_weight, 'node_vec1': node_vec1, 'L0_gnn_W_msg_tp': _L0_gnn_in['W_msg_tp'], 'L0_gnn_W_msg_lin': _L0_gnn_in['W_msg_lin'], 'L0_gnn_W_upd_tp': _L0_gnn_in['W_upd_tp'], 'L0_gnn_W_upd_lin': _L0_gnn_in['W_upd_lin'], 'L1_gnn_weight_matrix': _L1_gnn_in['weight_matrix'], 'L1_gnn_bias': _L1_gnn_in['bias'], 'L2_gnn_node_enc_w0': _L2_gnn_in['node_enc_w0'], 'L2_gnn_node_enc_b0': _L2_gnn_in['node_enc_b0'], 'L2_gnn_node_enc_w1': _L2_gnn_in['node_enc_w1'], 'L2_gnn_node_enc_b1': _L2_gnn_in['node_enc_b1'], 'L2_gnn_node_enc_g': _L2_gnn_in['node_enc_g'], 'L2_gnn_node_enc_beta': _L2_gnn_in['node_enc_beta'], 'L2_gnn_edge_enc_w0': _L2_gnn_in['edge_enc_w0'], 'L2_gnn_edge_enc_b0': _L2_gnn_in['edge_enc_b0'], 'L2_gnn_edge_enc_w1': _L2_gnn_in['edge_enc_w1'], 'L2_gnn_edge_enc_b1': _L2_gnn_in['edge_enc_b1'], 'L2_gnn_edge_enc_g': _L2_gnn_in['edge_enc_g'], 'L2_gnn_edge_enc_beta': _L2_gnn_in['edge_enc_beta'], 'L2_gnn_edge_blk_w0': _L2_gnn_in['edge_blk_w0'], 'L2_gnn_edge_blk_b0': _L2_gnn_in['edge_blk_b0'], 'L2_gnn_edge_blk_w1': _L2_gnn_in['edge_blk_w1'], 'L2_gnn_edge_blk_b1': _L2_gnn_in['edge_blk_b1'], 'L2_gnn_edge_blk_g': _L2_gnn_in['edge_blk_g'], 'L2_gnn_edge_blk_beta': _L2_gnn_in['edge_blk_beta'], 'L2_gnn_node_blk_w0': _L2_gnn_in['node_blk_w0'], 'L2_gnn_node_blk_b0': _L2_gnn_in['node_blk_b0'], 'L2_gnn_node_blk_w1': _L2_gnn_in['node_blk_w1'], 'L2_gnn_node_blk_b1': _L2_gnn_in['node_blk_b1'], 'L2_gnn_node_blk_g': _L2_gnn_in['node_blk_g'], 'L2_gnn_node_blk_beta': _L2_gnn_in['node_blk_beta'], 'L2_gnn_dec_w0': _L2_gnn_in['dec_w0'], 'L2_gnn_dec_b0': _L2_gnn_in['dec_b0'], 'L2_gnn_dec_w1': _L2_gnn_in['dec_w1'], 'L2_gnn_dec_b1': _L2_gnn_in['dec_b1'], 'L3_gnn_W1': _L3_gnn_in['W1'], 'L3_gnn_b1': _L3_gnn_in['b1'], 'L3_gnn_W2': _L3_gnn_in['W2'], 'L3_gnn_b2': _L3_gnn_in['b2']}

def reference(x, src, dst, edge_attr_8, edge_weight, node_vec1, L0_gnn_W_msg_tp, L0_gnn_W_msg_lin, L0_gnn_W_upd_tp, L0_gnn_W_upd_lin, L1_gnn_weight_matrix, L1_gnn_bias, L2_gnn_node_enc_w0, L2_gnn_node_enc_b0, L2_gnn_node_enc_w1, L2_gnn_node_enc_b1, L2_gnn_node_enc_g, L2_gnn_node_enc_beta, L2_gnn_edge_enc_w0, L2_gnn_edge_enc_b0, L2_gnn_edge_enc_w1, L2_gnn_edge_enc_b1, L2_gnn_edge_enc_g, L2_gnn_edge_enc_beta, L2_gnn_edge_blk_w0, L2_gnn_edge_blk_b0, L2_gnn_edge_blk_w1, L2_gnn_edge_blk_b1, L2_gnn_edge_blk_g, L2_gnn_edge_blk_beta, L2_gnn_node_blk_w0, L2_gnn_node_blk_b0, L2_gnn_node_blk_w1, L2_gnn_node_blk_b1, L2_gnn_node_blk_g, L2_gnn_node_blk_beta, L2_gnn_dec_w0, L2_gnn_dec_b0, L2_gnn_dec_w1, L2_gnn_dec_b1, L3_gnn_W1, L3_gnn_b1, L3_gnn_W2, L3_gnn_b2):
    import jax
    import jax.numpy as jnp

    def _L0_gnn_ref(node_features, edge_attr_e3nn, node_attr_scalar_raw, W_msg_tp, W_msg_lin, W_upd_tp, W_upd_lin, edge_index):
        import jax, jax.numpy as jnp
        import numpy as np
        N_NODES = 12500
        N_EDGES = 400000
        D_NODE = 16
        D_EDGE = 8
        D_HIDDEN = 16
        n_nodes = node_features.shape[0]
        row = edge_index[0]
        col = edge_index[1]
        norm_msg_tp = 1.0 / np.float32(np.sqrt(D_NODE * D_EDGE))
        norm_upd_tp = 1.0 / np.float32(np.sqrt(D_NODE * D_HIDDEN))
        norm_lin = 1.0 / np.float32(np.sqrt(D_HIDDEN))
        x_j = node_features[col]
        m = jnp.einsum('ei,ej,ijh->eh', x_j, edge_attr_e3nn, W_msg_tp) * norm_msg_tp
        m = jax.nn.silu(m)
        m = m @ W_msg_lin * norm_lin
        agg = jax.ops.segment_sum(m, row, num_segments=n_nodes)
        u = jnp.einsum('ni,nh,ihk->nk', node_features, agg, W_upd_tp) * norm_upd_tp
        u = jax.nn.silu(u)
        u = u @ W_upd_lin * norm_lin
        return node_features + u

    def _L1_gnn_ref(x, edge_index, edge_attr, weight_matrix, bias, num_nodes):
        import jax, jax.numpy as jnp
        import numpy as np
        N_NODES = 12500
        N_EDGES = 200000
        IN_C = 16
        OUT_C = 16
        N_EATTR = 8
        src = edge_index[0]
        dst = edge_index[1]
        x_j = x[src]
        msg = jnp.einsum('ea,aoi,ei->eo', edge_attr, weight_matrix, x_j)
        aggr = jax.ops.segment_sum(msg, dst, num_segments=num_nodes)
        return jax.nn.relu(aggr + bias)

    def _L2_gnn_ref(node_feat, edge_feat, senders, receivers, node_enc_w0, node_enc_b0, node_enc_w1, node_enc_b1, node_enc_g, node_enc_beta, edge_enc_w0, edge_enc_b0, edge_enc_w1, edge_enc_b1, edge_enc_g, edge_enc_beta, edge_blk_w0, edge_blk_b0, edge_blk_w1, edge_blk_b1, edge_blk_g, edge_blk_beta, node_blk_w0, node_blk_b0, node_blk_w1, node_blk_b1, node_blk_g, node_blk_beta, dec_w0, dec_b0, dec_w1, dec_b1):
        import jax, jax.numpy as jnp
        import numpy as np
        N = 6250
        E = 100000
        S = 2
        D_NODE_IN, D_EDGE_IN, D, H, D_OUT = (16, 8, 64, 64, 16)
        LN_EPS = 1e-05

        def _mlp(x, w0, b0, w1, b1):
            return jax.nn.silu(x @ w0 + b0) @ w1 + b1

        def _ln(x, g, b):
            m = jnp.mean(x, axis=-1, keepdims=True)
            v = jnp.var(x, axis=-1, keepdims=True)
            return (x - m) * jax.lax.rsqrt(v + LN_EPS) * g + b
        num_nodes = node_feat.shape[0]
        n = _ln(_mlp(node_feat, node_enc_w0, node_enc_b0, node_enc_w1, node_enc_b1), node_enc_g, node_enc_beta)
        e = _ln(_mlp(edge_feat, edge_enc_w0, edge_enc_b0, edge_enc_w1, edge_enc_b1), edge_enc_g, edge_enc_beta)
        for s in range(S):
            ce = jnp.concatenate([e, n[senders], n[receivers]], axis=-1)
            e = e + _ln(_mlp(ce, edge_blk_w0[s], edge_blk_b0[s], edge_blk_w1[s], edge_blk_b1[s]), edge_blk_g[s], edge_blk_beta[s])
            agg = jax.ops.segment_sum(e.astype(jnp.float32), receivers, num_segments=num_nodes)
            cn = jnp.concatenate([n, agg.astype(n.dtype)], axis=-1)
            n = n + _ln(_mlp(cn, node_blk_w0[s], node_blk_b0[s], node_blk_w1[s], node_blk_b1[s]), node_blk_g[s], node_blk_beta[s])
        return _mlp(n, dec_w0, dec_b0, dec_w1, dec_b1)

    def _L3_gnn_ref(x, edge_index, edge_w, W1, b1, W2, b2, num_nodes):
        import jax, jax.numpy as jnp
        import numpy as np
        N_NODES = 12500
        N_EDGES = 400000
        F_IN = 16
        F_HID = 32

        def _gcn_conv(x, row, col, edge_w, W, b, num_nodes):
            loop = jnp.arange(num_nodes)
            r = jnp.concatenate([row, loop])
            c = jnp.concatenate([col, loop])
            ew = jnp.concatenate([edge_w, jnp.ones((num_nodes,), dtype=edge_w.dtype)])
            deg = jax.ops.segment_sum(ew, c, num_segments=num_nodes)
            dis = jnp.where(deg > 0, jax.lax.rsqrt(deg), 0.0)
            norm = dis[r] * ew * dis[c]
            xw = x @ W.T
            msg = xw[r] * norm[:, None]
            out = jax.ops.segment_sum(msg, c, num_segments=num_nodes)
            return out + b
        row, col = (edge_index[0], edge_index[1])
        h = _gcn_conv(x, row, col, edge_w, W1, b1, num_nodes)
        h = jax.nn.relu(h)
        out = _gcn_conv(h, row, col, edge_w, W2, b2, num_nodes)
        return out
    edge_index = jnp.stack([src, dst])
    h = jnp.maximum(_layernorm(x, axis=-1), 0.0)
    x = x + _L0_gnn_ref(h, edge_attr_8, node_vec1, L0_gnn_W_msg_tp, L0_gnn_W_msg_lin, L0_gnn_W_upd_tp, L0_gnn_W_upd_lin, edge_index)
    h = jnp.maximum(_layernorm(x, axis=-1), 0.0)
    x = x + _L1_gnn_ref(h, edge_index, edge_attr_8, L1_gnn_weight_matrix, L1_gnn_bias, 12500)
    h = jnp.maximum(_layernorm(x, axis=-1), 0.0)
    x = x + _L2_gnn_ref(h, edge_attr_8, src, dst, L2_gnn_node_enc_w0, L2_gnn_node_enc_b0, L2_gnn_node_enc_w1, L2_gnn_node_enc_b1, L2_gnn_node_enc_g, L2_gnn_node_enc_beta, L2_gnn_edge_enc_w0, L2_gnn_edge_enc_b0, L2_gnn_edge_enc_w1, L2_gnn_edge_enc_b1, L2_gnn_edge_enc_g, L2_gnn_edge_enc_beta, L2_gnn_edge_blk_w0, L2_gnn_edge_blk_b0, L2_gnn_edge_blk_w1, L2_gnn_edge_blk_b1, L2_gnn_edge_blk_g, L2_gnn_edge_blk_beta, L2_gnn_node_blk_w0, L2_gnn_node_blk_b0, L2_gnn_node_blk_w1, L2_gnn_node_blk_b1, L2_gnn_node_blk_g, L2_gnn_node_blk_beta, L2_gnn_dec_w0, L2_gnn_dec_b0, L2_gnn_dec_w1, L2_gnn_dec_b1)
    h = jnp.maximum(_layernorm(x, axis=-1), 0.0)
    x = x + _L3_gnn_ref(h, edge_index, edge_weight, L3_gnn_W1, L3_gnn_b1, L3_gnn_W2, L3_gnn_b2, 12500)
    return x

_drawn_inputs = setup_inputs


def setup_inputs(seed=0):
    import zlib

    import numpy as np

    out = dict(_drawn_inputs(seed))
    spreads = {'L1_gnn_bias': (0.0, 0.596),
     'L2_gnn_node_enc_g': (1.0, 0.565),
     'L2_gnn_node_enc_beta': (0.0, 0.569),
     'L2_gnn_edge_enc_g': (1.0, 0.6),
     'L2_gnn_edge_enc_beta': (0.0, 0.527),
     'L2_gnn_edge_blk_g': (1.0, 0.6),
     'L2_gnn_edge_blk_beta': (0.0, 0.8),
     'L2_gnn_node_blk_g': (1.0, 0.6),
     'L2_gnn_node_blk_beta': (0.0, 0.533)}
    factors = {'edge_weight': 24.718,
     'L2_gnn_edge_enc_w0': 3.771,
     'L2_gnn_edge_blk_b0': 5.965,
     'L2_gnn_edge_blk_b1': 4.303,
     'L2_gnn_node_blk_b0': 64.0,
     'L2_gnn_node_blk_b1': 64.0,
     'L2_gnn_dec_b0': 8.0,
     'L2_gnn_dec_b1': 5.368,
     'L3_gnn_W1': 5.085,
     'L3_gnn_b1': 6.647,
     'L3_gnn_W2': 5.205,
     'L3_gnn_b2': 2.956,
     'L2_gnn_edge_enc_b0': 3.833}
    for name, (base, spread) in spreads.items():
        noise = np.random.default_rng([zlib.crc32(name.encode()), seed]).standard_normal(out[name].shape)
        drawn = base * np.exp(spread * noise) if base else spread * noise
        out[name] = jnp.asarray(drawn.astype(out[name].dtype))
    for name, factor in factors.items():
        out[name] = (out[name] * factor).astype(out[name].dtype)
    return out
```

```python
from contextlib import ExitStack

import numpy as np
import concourse.bass as bass
from concourse import mybir

F32 = mybir.dt.float32
BF16 = mybir.dt.bfloat16
I32 = mybir.dt.int32
ALU = mybir.AluOpType
ACT = mybir.ActivationFunctionType
AX = mybir.AxisListType

N = 12500
E = 412500
P = 125
WIN = 64
S = 6
UNITS = E // (P * S)
PAIRS = S // 2
C = 4
NODE_UNITS = N // (P * C)
ROWS = N + P
F = 16
A = 8
D = 64
EPS = 1e-5
RSQRT_STEPS = 12


class Chain:

    def __init__(self, sem, base, steps):
        self.sem, self.base, self.steps = sem, base, list(steps)
        assert len(set(self.steps)) == len(self.steps), self.steps
        self.n = len(self.steps)

    def at(self, step, i):
        return i * self.n + (self.base + self.steps.index(step) + 1)

    def end(self, i):
        return i * self.n + (self.base + self.n)

    def before(self, step, i):
        k = self.steps.index(step)
        assert k, step
        return i * self.n + (self.base + k)


def rsqrt_names(p):
    return [f"{p}_rsqrt{k}" for k in range(RSQRT_STEPS)]


def ln_names(p, centered):
    first = [] if centered else [f"{p}_sum", f"{p}_mean", f"{p}_center"]
    return first + [f"{p}_square", f"{p}_var"] + rsqrt_names(p) + [f"{p}_norm"]


def rolled(eng, n, body):
    body(0, True)
    with eng.Fori(1, n) as i:
        body(i, False)


def bc3(ap, shape):
    return ap.unsqueeze(2).broadcast_to(shape)


def gnn_kernel(nc, ins, out):
    ctx = ExitStack()
    with ctx:
        _gnn(nc, ctx, ins, out)


def _gnn(nc, ctx, ins, out):
    def sb(name, shape, dt=F32, at=None):
        return (at or ctx).enter_context(nc.sbuf_tensor(name, shape, dt))

    def sem(name):
        return ctx.enter_context(nc.semaphore(name))

    main = [sem("main_chain0"), sem("main_chain1")]
    dedup = [sem("dedup_chain0"), sem("dedup_chain1")]
    loaded = [sem("loaded0"), sem("loaded1")]
    scattered = [sem(f"scattered{t}") for t in range(S)]
    stored = [sem("stored0"), sem("stored1")]
    pool_tick = sem("pool_tick")
    sp_tick = sem("sp_tick")
    count = {}

    def base(s):
        return count.get(s.num, 0)

    def advance(s, by):
        count[s.num] = base(s) + by

    def dram(name, shape):
        return nc.dram_tensor(name, shape, F32).ap()

    y0 = dram("y0", [N, A * F])
    y1 = dram("y1", [N, A * F])
    h0_d = dram("h0", [N, F])
    x1_d, x2_d, x3_d = dram("x1", [N, F]), dram("x2", [N, F]), dram("x3", [N, F])
    n0_d, n1_d = dram("n0", [N, D]), dram("n1", [N, D])
    send_d = [dram("send0", [N, D]), dram("send1", [N, D])]
    recv_d = [dram("recv0", [N, D]), dram("recv1", [N, D])]
    dis_d = dram("dis", [N, 1])
    g1_d, g2_d = dram("g1", [N, F]), dram("g2", [N, F])
    edge_t = dram("edge_t", [UNITS, 2 * D, PAIRS * P])
    agg0 = [dram(f"agg0_{t}", [ROWS, F]) for t in range(S)]
    agg1 = [dram(f"agg1_{t}", [ROWS, F + 1]) for t in range(S)]
    agg2 = [dram(f"agg2_{t}", [ROWS, D]) for t in range(S)]
    agg3 = [dram(f"agg3_{t}", [ROWS, F]) for t in range(S)]
    agg4 = [dram(f"agg4_{t}", [ROWS, F]) for t in range(S)]

    ident = sb("ident", [P, P])
    earlier = sb("earlier", [P, P])
    spare_i = sb("spare_i", [P, 1], I32)
    spare = sb("spare", [P, 1])
    ones = sb("ones", [1, P])
    ones_col = sb("ones_col", [P, 1])
    w_msg = sb("w_msg", [C * F, C * A * F])
    w_msg_lin = sb("w_msg_lin", [C * F, C * F])
    w_upd = sb("w_upd", [C * F, C * F * F])
    w_upd_lin = sb("w_upd_lin", [C * F, C * F])
    w_conv = sb("w_conv", [C * F, C * A * F])
    conv_bias = sb("conv_bias", [P, F])
    w_nenc0 = sb("w_nenc0", [C * F, C * D])
    w_eenc0 = sb("w_eenc0", [S * A, S * D])
    w_gcn1 = sb("w_gcn1", [C * F, C * 32])
    w_gcn2 = sb("w_gcn2", [C * 32, C * F])
    gcn_b1 = sb("gcn_b1", [C * 32, 1])
    gcn_b2 = sb("gcn_b2", [P, F])
    w_dec1 = sb("w_dec1", [2 * D, 2 * F])
    dec_b1 = sb("dec_b1", [P, F])
    iota_row = sb("iota_row", [P, WIN])
    iota_col = sb("iota_col", [2 * D, 1])
    iota_i = sb("iota_i", [P, WIN], I32)
    iota_ci = sb("iota_ci", [2 * D, 1], I32)
    ones3 = sb("ones3", [3, P], BF16)
    row3 = {k: sb(f"row3_{k}", [3, S * D], BF16) for k in ("eenc1", "eblk1_0", "eblk1_1")}
    w_state = sb("w_state", [2 * D, 2 * D])
    col_state = sb("col_state", [2 * D, 1])
    both_bias = sb("both_bias", [P, D])
    disorder = sb("disorder", [1, 1], I32)
    sq = ["nenc1", "eenc1"] + [f"{w}{s}" for s in range(2) for w in
                               ("eblk_e", "eblk_s", "eblk_r", "eblk1", "nblk_n", "nblk_a", "nblk1")] + ["dec0"]
    W = {k: sb(f"w_{k}", [2 * D, 2 * D]) for k in sq}
    col = {k: sb(f"col_{k}", [2 * D, 1]) for k in ("nenc0", "eenc0", "nblk0_0", "nblk0_1", "dec0")}
    row = {k: sb(f"row_{k}", [1, S * D]) for k in ("nenc1", "eenc1", "eblk1_0", "eblk1_1", "nblk1_0", "nblk1_1",
                                                  "eblk0_0", "eblk0_1")}
    gb = {k: sb(f"gb_{k}", [P, 2, D]) for k in ("nenc", "eenc", "eblk_0", "eblk_1", "nblk_0", "nblk_1")}

    with ExitStack() as st:
        zero = sb("zero", [P, ROWS // P * D], F32, st)
        stage = {k: sb(f"stage_{k}", [2 * D, D], F32, st) for k in sq}
        stage_row = sb("stage_row", [1, len(row), D], F32, st)
        mean = sb("mean", [2 * D, len(sq)], F32, st)
        mean_row = sb("mean_row", [1, len(row)], F32, st)
        gain_col = sb("gain_col", [2 * D, 1], F32, st)
        bias_col = sb("bias_col", [2 * D, 1], F32, st)
        parts = {k: sb(f"parts_{k}", [1, 2, S * D], F32, st) for k in row3}
        parts16 = {k: sb(f"parts16_{k}", [1, 3, S * D], BF16, st) for k in row3}
        split = sem("split")
        placed = sem("placed")
        DP = 55 if UNITS // 2 % 55 == 0 else 1
        DR = UNITS // 2 // DP
        targets = sb("targets", [DP, DR, 2 * P * S], I32, st)
        first_target = sb("first_target", [DP, DR], F32, st)
        extent = sb("extent", [DP, 4, DR], F32, st)
        outside = sb("outside", [DP, 1], F32, st)
        ps_setup = st.enter_context(nc.psum_tensor("ps_setup", [2 * D, 512], F32))
        ordered, multiplied = sem("ordered"), sem("multiplied")
        cleared, weights, zeroed, wchain, consts = (sem(x) for x in ("cleared", "weights", "zeroed", "wchain", "consts"))
        small = [w_msg, w_msg_lin, w_upd, w_upd_lin, w_conv, w_nenc0, w_eenc0, w_gcn1, w_gcn2, w_dec1]
        square = {
            "nenc1": ins["L2_gnn_node_enc_w1"], "eenc1": ins["L2_gnn_edge_enc_w1"], "dec0": ins["L2_gnn_dec_w0"]}
        for s in range(2):
            w0, w1 = ins["L2_gnn_edge_blk_w0"], ins["L2_gnn_node_blk_w0"]
            square |= {f"eblk_e{s}": w0[s, 0:D, :], f"eblk_s{s}": w0[s, D:2 * D, :], f"eblk_r{s}": w0[s, 2 * D:3 * D, :],
                       f"eblk1{s}": ins["L2_gnn_edge_blk_w1"][s], f"nblk_n{s}": w1[s, 0:D, :],
                       f"nblk_a{s}": w1[s, D:2 * D, :], f"nblk1{s}": ins["L2_gnn_node_blk_w1"][s]}
        rows = {"nenc1": ins["L2_gnn_node_enc_b1"], "eenc1": ins["L2_gnn_edge_enc_b1"],
                "eblk1_0": ins["L2_gnn_edge_blk_b1"][0], "eblk1_1": ins["L2_gnn_edge_blk_b1"][1],
                "nblk1_0": ins["L2_gnn_node_blk_b1"][0], "nblk1_1": ins["L2_gnn_node_blk_b1"][1],
                "eblk0_0": ins["L2_gnn_edge_blk_b0"][0], "eblk0_1": ins["L2_gnn_edge_blk_b0"][1]}
        cols = {"nenc0": ins["L2_gnn_node_enc_b0"], "eenc0": ins["L2_gnn_edge_enc_b0"],
                "nblk0_0": ins["L2_gnn_node_blk_b0"][0], "nblk0_1": ins["L2_gnn_node_blk_b0"][1],
                "dec0": ins["L2_gnn_dec_b0"]}
        gbs = {"nenc": (ins["L2_gnn_node_enc_g"], ins["L2_gnn_node_enc_beta"]),
               "eenc": (ins["L2_gnn_edge_enc_g"], ins["L2_gnn_edge_enc_beta"])}
        for s in range(2):
            gbs[f"eblk_{s}"] = (ins["L2_gnn_edge_blk_g"][s], ins["L2_gnn_edge_blk_beta"][s])
            gbs[f"nblk_{s}"] = (ins["L2_gnn_node_blk_g"][s], ins["L2_gnn_node_blk_beta"][s])
        diagonals = []
        diagonals.append((w_msg, ins["L0_gnn_W_msg_tp"].rearrange("i j h -> i (j h)"), C))
        diagonals.append((w_msg_lin, ins["L0_gnn_W_msg_lin"], C))
        diagonals.append((w_upd, ins["L0_gnn_W_upd_tp"].rearrange("i h k -> i (h k)"), C))
        diagonals.append((w_upd_lin, ins["L0_gnn_W_upd_lin"], C))
        diagonals.append((w_nenc0, ins["L2_gnn_node_enc_w0"], C))
        diagonals.append((w_eenc0, ins["L2_gnn_edge_enc_w0"], S))
        diagonals.append((w_dec1, ins["L2_gnn_dec_w1"], 2))
        gcn_w1_t = ins["L3_gnn_W1"].rearrange("o i -> i o")
        gcn_w2_t = ins["L3_gnn_W2"].rearrange("o i -> i o")
        diagonals.append((w_gcn1, gcn_w1_t, C))
        diagonals.append((w_gcn2, gcn_w2_t, C))
        n_loads = [0]

        block = st.enter_context(nc.Block())

        @block.sync
        def _(sp):
            def load(dst, src):
                sp.dma_start(dst, src).then_inc(weights, 16)
                n_loads[0] += 1

            sp.wait_ge(cleared, 2)
            with nc.allow_non_contiguous_dma(reason="small weights, transposed once"):
                for dst, src, copies in diagonals:
                    k, m = src.shape
                    for t in range(copies):
                        load(dst[t * k:(t + 1) * k, t * m:(t + 1) * m], src)
                for t in range(C):
                    for a in range(A):
                        load(w_conv[t * F:(t + 1) * F, (t * A + a) * F:(t * A + a + 1) * F],
                             ins["L1_gnn_weight_matrix"][a].rearrange("o i -> i o"))
            for k, src in square.items():
                for half in range(2):
                    load(stage[k][half * D:(half + 1) * D, :], src)
            for n, k in enumerate(row):
                load(stage_row[:, n, :], rows[k].unsqueeze(0))
            with nc.allow_non_contiguous_dma(reason="biases as columns"):
                for k in col:
                    for half in range(2):
                        load(col[k][half * D:(half + 1) * D, :], cols[k].unsqueeze(1))
                for t in range(C):
                    load(gcn_b1[t * 32:(t + 1) * 32, :], ins["L3_gnn_b1"].unsqueeze(1))
            for k in gb:
                for n in range(2):
                    load(gb[k][:, n, :], gbs[k][n].unsqueeze(0).broadcast_to([P, D]))
            with nc.allow_non_contiguous_dma(reason="gain and bias as columns"):
                for half in range(2):
                    load(gain_col[half * D:(half + 1) * D, :], ins["L2_gnn_edge_enc_g"].unsqueeze(1))
                    load(bias_col[half * D:(half + 1) * D, :], ins["L2_gnn_edge_enc_beta"].unsqueeze(1))
            load(targets[:, :, :], ins["dst"].rearrange("(p r e) -> p r e", r=DR, e=2 * P * S))
            load(conv_bias[:, :], ins["L1_gnn_bias"].unsqueeze(0).broadcast_to([P, F]))
            load(gcn_b2[:, :], ins["L3_gnn_b2"].unsqueeze(0).broadcast_to([P, F]))
            load(dec_b1[:, :], ins["L2_gnn_dec_b1"].unsqueeze(0).broadcast_to([P, F]))

        @block.scalar
        def _(act):
            act.wait_ge(cleared, 2)
            n = 0
            for tables, width in ((agg0, F), (agg1, F + 1), (agg2, D), (agg3, F), (agg4, F)):
                for table in tables:
                    act.dma_start(table.rearrange("(p r) f -> p (r f)", p=P),
                                  zero[:, 0:ROWS // P * width]).then_inc(zeroed, 16)
                    n += 1
            act.wait_ge(split, 5 * len(row3))
            n_placed = 0
            for k in row3:
                for part in range(3):
                    act.dma_start(row3[k][part:part + 1, :], parts16[k][:, part, :]).then_inc(placed, 16)
                    n_placed += 1
            act.wait_ge(placed, 16 * n_placed)
            act.wait_ge(zeroed, 16 * n)

        @block.gpsimd
        def _(pool):
            pool.memset(ident[:, :], 0.0).then_inc(consts, 1)
            pool.memset(earlier[:, :], 1.0).then_inc(consts, 1)
            pool.memset(ones[:, :], 1.0).then_inc(consts, 1)
            pool.iota(spare_i[:, :], pattern=[[0, 1]], base=N, channel_multiplier=1).then_inc(consts, 1)
            pool.iota(iota_i[:, :], pattern=[[1, WIN]], base=0, channel_multiplier=0).then_inc(consts, 1)
            for half in range(2):
                pool.wait_ge(consts, 5 + half)
                pool.iota(iota_ci[half * D:(half + 1) * D, :], pattern=[[0, 1]], base=0, channel_multiplier=1).then_inc(consts, 1)
            pool.wait_ge(consts, 7)
            pool.memset(ones3[:, :], 1.0).then_inc(consts, 1)
            pool.memset(ones_col[:, :], 1.0).then_inc(consts, 1)
            pool.wait_ge(consts, 9)
            pool.tensor_copy(iota_row[:, :], iota_i[:, :]).then_inc(consts, 1)
            pool.tensor_copy(iota_col[:, :], iota_ci[:, :]).then_inc(consts, 1)
            pool.affine_select(out=ident[:, :], in_=ident[:, :], compare_op=ALU.not_equal, fill=1.0,
                               base=0, pattern=[[-1, P]], channel_multiplier=1).then_inc(consts, 1)
            pool.affine_select(out=earlier[:, :], in_=earlier[:, :], compare_op=ALU.is_gt, fill=0.0,
                               base=0, pattern=[[-1, P]], channel_multiplier=1).then_inc(consts, 1)
            pool.tensor_copy(spare[:, :], spare_i[:, :]).then_inc(consts, 1)
            pool.wait_ge(consts, 14)

        @block.vector
        def _(dve):
            dve.memset(zero[:, :], 0.0).then_inc(cleared, 1)
            for w in small:
                last = dve.memset(w[:, :], 0.0)
            last.then_inc(cleared, 1)
            for k in sq:
                last = dve.memset(W[k][:, :], 0.0)
            last.then_inc(wchain, 1)
            dve.wait_ge(weights, 16 * n_loads[0])
            dve.wait_ge(wchain, 1)
            centered = ["nenc1", "eenc1"] + [f"{w}1{s}" for s in range(2) for w in ("eblk", "nblk")]
            for n, k in enumerate(sq):
                last = dve.tensor_reduce(mean[:, n:n + 1], stage[k][:, :], axis=AX.X, op=ALU.add)
            last = dve.tensor_reduce(mean_row[:, :], stage_row[:, :, :], axis=AX.X, op=ALU.add)
            last.then_inc(wchain, 1)
            dve.wait_ge(wchain, 2)
            dve.tensor_scalar(mean[:, :], mean[:, :], -1.0 / D, None, ALU.mult).then_inc(wchain, 1)
            dve.tensor_scalar(mean_row[:, :], mean_row[:, :], -1.0 / D, None, ALU.mult).then_inc(wchain, 1)
            dve.wait_ge(wchain, 4)
            for n, k in enumerate(sq):
                for half in range(2):
                    q = slice(half * D, (half + 1) * D)
                    if k in centered:
                        last = dve.tensor_scalar(W[k][q, q], stage[k][q, :], mean[q, n:n + 1], None, ALU.add)
                    else:
                        last = dve.tensor_copy(W[k][q, q], stage[k][q, :])
            for n, k in enumerate(row):
                for t in range(S):
                    q = slice(t * D, (t + 1) * D)
                    if k.startswith("eblk0"):
                        last = dve.tensor_copy(row[k][:, q], stage_row[:, n, :])
                    else:
                        last = dve.tensor_scalar(row[k][:, q], stage_row[:, n, :], mean_row[:, n:n + 1], None, ALU.add)
            last.then_inc(wchain, 1)
            dve.wait_ge(wchain, 5)
            dve.tensor_scalar(w_state[:, :], W["eblk_e0"][:, :], gain_col[:, :], None, ALU.mult).then_inc(wchain, 1)
            dve.tensor_tensor(both_bias[:, :], gb["eenc"][:, 1, :], gb["eblk_0"][:, 1, :], ALU.add).then_inc(wchain, 1)
            dve.wait_ge(multiplied, 1)
            dve.tensor_copy(col_state[:, :], ps_setup[:, 0:1]).then_inc(wchain, 1)
            n = 0
            for k in row3:
                lo, hi = parts[k], parts16[k]
                for part in range(3):
                    frm = row[k][:, :] if part == 0 else lo[:, part - 1, :]
                    dve.tensor_copy(hi[:, part, :], frm).then_inc(split, 1)
                    n += 1
                    dve.wait_ge(split, n)
                    if part < 2:
                        dve.tensor_tensor(lo[:, part, :], frm, hi[:, part, :], ALU.subtract).then_inc(split, 1)
                        n += 1
                        dve.wait_ge(split, n)
            dve.tensor_copy(first_target[:, :], targets[:, :, 0]).then_inc(ordered, 1)
            dve.tensor_reduce(extent[:, 0, :], targets[:, :, :], axis=AX.X, op=ALU.max).then_inc(ordered, 1)
            dve.tensor_reduce(extent[:, 1, :], targets[:, :, :], axis=AX.X, op=ALU.min).then_inc(ordered, 1)
            dve.wait_ge(ordered, 3)
            dve.tensor_tensor(extent[:, 2, :], extent[:, 0, :], first_target[:, :], ALU.subtract).then_inc(ordered, 1)
            dve.tensor_tensor(extent[:, 3, :], first_target[:, :], extent[:, 1, :], ALU.subtract).then_inc(ordered, 1)
            dve.wait_ge(ordered, 5)
            dve.tensor_scalar(extent[:, 2, :], extent[:, 2, :], float(1 - WIN), 0.0, ALU.add, ALU.max).then_inc(ordered, 1)
            dve.tensor_scalar(extent[:, 3, :], extent[:, 3, :], 0.0, None, ALU.max).then_inc(ordered, 1)
            dve.wait_ge(ordered, 7)
            dve.tensor_reduce(outside[:, :], extent[:, 2:4, :], axis=AX.XY, op=ALU.max).then_inc(ordered, 1)
            dve.wait_ge(multiplied, 2)
            dve.tensor_scalar(disorder[:, :], ps_setup[0:1, 2:3], 1.0, None, ALU.min).then_inc(ordered, 1)
            dve.wait_ge(ordered, 9)

        @block.tensor
        def _(pe):
            pe.wait_ge(weights, 16 * n_loads[0])
            pe.wait_ge(wchain, 5)
            pe.matmul(ps_setup[:, 0:1], W["eblk_e0"][:, :], bias_col[:, :], start=True, stop=True).then_inc(multiplied, 1)
            pe.wait_ge(consts, 14)
            pe.wait_ge(ordered, 8)
            pe.wait_ge(wchain, 8)
            pe.matmul(ps_setup[0:1, 2:3], outside[:, :], ones_col[0:DP, :], start=True, stop=True).then_inc(multiplied, 1)

    def norm_stats(dve, chain, p, i, squares, width, n, v):
        dve.wait_ge(chain.sem, chain.at(f"{p}_square", i))
        dve.tensor_reduce(v[:, 1, 0:n], squares, axis=AX.X, op=ALU.add).then_inc(chain.sem, 1)
        dve.wait_ge(chain.sem, chain.at(f"{p}_var", i))
        dve.tensor_scalar(v[:, 1, 0:n], v[:, 1, 0:n], 1.0 / width, EPS, ALU.mult, ALU.add).then_inc(chain.sem, 1)
        newton(dve, chain, p, i, v[:, 1, 0:n], v[:, 0, 0:n], v[:, 2, 0:n])

    def newton(dve, chain, p, i, value, out_, t):
        names = rsqrt_names(p)

        dve.wait_ge(chain.sem, chain.at(names[0], i))
        dve.tensor_scalar(t.bitcast(I32), value.bitcast(I32), 1, None, ALU.logical_shift_right).then_inc(chain.sem, 1)
        dve.wait_ge(chain.sem, chain.at(names[1], i))
        dve.tensor_scalar(out_.bitcast(I32), t.bitcast(I32), -1.0, float(0x5F3759DF), ALU.mult, ALU.add).then_inc(chain.sem, 1)
        for r in range(3):
            dve.wait_ge(chain.sem, chain.at(names[2 + 3 * r], i))
            dve.scalar_tensor_tensor(out=t, in0=out_, scalar=-0.5, in1=value, op0=ALU.mult, op1=ALU.mult).then_inc(chain.sem, 1)
            dve.wait_ge(chain.sem, chain.at(names[3 + 3 * r], i))
            dve.tensor_tensor(t, t, out_, ALU.mult).then_inc(chain.sem, 1)
            dve.wait_ge(chain.sem, chain.at(names[4 + 3 * r], i))
            dve.scalar_tensor_tensor(out=out_, in0=t, scalar=1.5, in1=out_, op0=ALU.add, op1=ALU.mult).then_inc(chain.sem, 1)

    def edge_rows(ap):
        return ap.rearrange("(u p s) k -> u p (s k)", p=P, s=S)

    def node_rows(ap):
        return ap[0:N, :].rearrange("(u p c) k -> u p (c k)", p=P, c=C)

    attr_u = edge_rows(ins["edge_attr_8"])
    src_u = edge_rows(ins["src"].unsqueeze(1))
    dst_u = edge_rows(ins["dst"].unsqueeze(1))
    weight_u = edge_rows(ins["edge_weight"].unsqueeze(1))

    def edge_pass(name, tables, target, width, agg, kind, rnd=0):
        table_widths = [w for _, w, _ in tables]
        ends = {"src": src_u, "dst": dst_u}
        used = sorted({e for _, _, e in tables} | {target})
        mlp = kind in ("mlp0", "mlp1")
        takes_attr = kind in ("message", "conv", "mlp0")
        takes_weight = kind in ("conv", "gcn")
        from_table = "attr" if takes_attr else None

        dedup_steps = ["equal", "masked", "repeated", "to_spare", "if_repeated", "index"]
        if kind in ("message", "conv"):
            steps = ["product", "summed"] + (["silu"] if kind == "message" else ["weight"])
        elif kind == "gcn":
            steps = ["product"]
        else:
            steps = []
            if kind == "mlp0":
                steps += ["attr_turned", "attr_t", "hidden0", "act0", "out0"] + ln_names("enc", True) + \
                         ["enc_gain", "enc_bias", "state_turned", "state_t"]
            steps += ["hidden1", "act1", "out1"] + ln_names("upd", True) + ["upd_gain", "upd_bias"]
            if kind == "mlp0":
                steps += ["state_added", "next_turned", "next_t"]
        steps += ["merged", "merged_out"]

        with ExitStack() as st:
            J = {e: [sb(f"{name}_{e}{h}", [P, S], I32, st) for h in range(2)] for e in used}
            B = [sb(f"{name}_row{h}", [P, P * S], I32, st) for h in range(2)]
            G = [[sb(f"{name}_g{n}{h}", [P, S, w], F32, st) for h in range(2)] for n, w in enumerate(table_widths)]
            attr = [sb(f"{name}_attr{h}", [P, S * A], F32, st) for h in range(2)] if takes_attr else None
            wt = [sb(f"{name}_wt{h}", [P, S], F32, st) for h in range(2)] if takes_weight else None
            same = [sb(f"{name}_same{h}", [P, S, P], F32, st) for h in range(2)]
            masked = sb(f"{name}_masked", [P, S, P], F32, st)
            rep = sb(f"{name}_rep", [P, S], F32, st)
            alt = sb(f"{name}_alt", [P, S], F32, st)
            index = [sb(f"{name}_index{h}", [P, S], I32, st) for h in range(2)]
            V = [sb(f"{name}_v{h}", [P, S, width], F32, st) for h in range(2)]
            SV = [sb(f"{name}_sv{h}", [P, S, width], F32, st) for h in range(2)]
            if takes_attr and not mlp:
                prod = sb(f"{name}_prod", [P, S * A, F], F32, st)
                summed = sb(f"{name}_summed", [P, S, F], F32, st)
            if mlp:
                attr_t = sb(f"{name}_attr_t", [S * A, P], F32, st)
                act0 = sb(f"{name}_act0", [2 * D, PAIRS * P], F32, st)
                act1 = sb(f"{name}_act1", [2 * D, PAIRS * P], F32, st)
                squares = sb(f"{name}_squares", [P, S, D], F32, st)
                stat = sb(f"{name}_stat", [P, 3, 8], F32, st)
                state = sb(f"{name}_state", [P, S, D], F32, st)
                state_t = [sb(f"{name}_state_t{h}", [2 * D, PAIRS * P], F32, st) for h in range(2)]
                next_t = [sb(f"{name}_next_t{h}", [2 * D, PAIRS * P], F32, st) for h in range(2)]

            def ps(k):
                return st.enter_context(nc.psum_tensor(f"{name}_ps_{k}", [2 * D, 512], F32))

            ps_merged = ps("merged")
            if mlp:
                ps_attr, ps_h0, ps_o0, ps_st, ps_h1, ps_o1, ps_nt = [ps(k) for k in ("attr", "h0", "o0", "st", "h1", "o1", "nt")]

            gathered = [sem(f"{name}_gathered{h}") for h in range(2)]
            m = [Chain(main[h], base(main[h]), steps) for h in range(2)]
            d = [Chain(dedup[h], base(dedup[h]), dedup_steps) for h in range(2)]
            n_loads = len(used) + 1 + takes_attr + takes_weight + (kind == "mlp1")
            n_gathers = S * len(tables)
            consumed = "product" if not mlp else "hidden1"
            b_loaded = [base(x) for x in loaded]
            b_scattered = [base(x) for x in scattered]
            b_stored = [base(x) for x in stored]
            half = UNITS // 2

            def loads_of(h, i):
                return i * (16 * n_loads) + (b_loaded[h] + 16 * n_loads)

            def gathers_of(h, i):
                return i * (16 * n_gathers) + 16 * n_gathers

            def scatters_of(t, i, h, ago):
                return i * 32 + (b_scattered[t] + 16 * (h - ago + 1))

            def stores_of(h, i):
                return i * 16 + (b_stored[h] + 16)

            block = st.enter_context(nc.Block())

            @block.sync
            def _(sp):
                def store_state(i, h):
                    sp.wait_ge(m[h].sem, m[h].at("next_t", i))
                    sp.sem_inc(sp_tick, 1)
                    sp.dma_start(edge_t[bass.ds(i * 2 + h, 1), :, :].squeeze(0), next_t[h][:, :]).then_inc(stored[h], 16)

                def unit(i, h, first):
                    u = bass.ds(i * 2 + h, 1)
                    if not first:
                        sp.wait_ge(m[h].sem, m[h].end(i - 1))
                        sp.sem_inc(sp_tick, 1)
                        sp.wait_ge(d[h].sem, d[h].end(i - 1))
                        sp.sem_inc(sp_tick, 1)
                        sp.wait_ge(gathered[h], gathers_of(h, i - 1))
                        sp.sem_inc(sp_tick, 1)
                        if kind == "mlp0":
                            store_state(i - 1, h)
                    for e in used:
                        sp.dma_start(J[e][h][:, :], ends[e][u].squeeze(0)).then_inc(loaded[h], 16)
                    sp.dma_start(B[h][:, :], ends[target][u].rearrange("u p s -> u (p s)").broadcast_to([P, P * S]))\
                      .then_inc(loaded[h], 16)
                    if takes_attr:
                        sp.dma_start(attr[h][:, :], attr_u[u].squeeze(0)).then_inc(loaded[h], 16)
                    if takes_weight:
                        sp.dma_start(wt[h][:, :], weight_u[u].squeeze(0)).then_inc(loaded[h], 16)
                    if kind == "mlp1":
                        sp.dma_start(state_t[h][:, :], edge_t[u].squeeze(0)).then_inc(loaded[h], 16)

                def body(i, first):
                    for h in range(2):
                        unit(i, h, first)

                rolled(sp, half, body)
                if kind == "mlp0":
                    for h in range(2):
                        store_state(half - 1, h)
                    for h in range(2):
                        sp.wait_ge(stored[h], stores_of(h, half - 1))

            @block.gpsimd
            def _(pool):
                def gathers(i, h, first):
                    pool.wait_ge(loaded[h], loads_of(h, i))
                    pool.sem_inc(pool_tick, 1)
                    if not first:
                        pool.wait_ge(m[h].sem, m[h].at(consumed, i - 1))
                        pool.sem_inc(pool_tick, 1)
                    for n, (table, _, end) in enumerate(tables):
                        for t in range(S):
                            pool.indirect_dma_start(
                                G[n][h][:, t, :], None, table,
                                bass.IndirectOffsetOnAxis(ap=J[end][h][:, t:t + 1], axis=0),
                            ).then_inc(gathered[h], 16)

                def scatters(i, h, first):
                    pool.wait_ge(m[h].sem, m[h].at("merged_out", i))
                    pool.sem_inc(pool_tick, 1)
                    for t in range(S):
                        if not (first and h == 0):
                            pool.wait_ge(scattered[t], scatters_of(t, i, h, 1))
                            pool.sem_inc(pool_tick, 1)
                        pool.indirect_dma_start(
                            agg[t], bass.IndirectOffsetOnAxis(ap=index[h][:, t:t + 1], axis=0), SV[h][:, t, :], None,
                            compute_op=ALU.add).then_inc(scattered[t], 16)

                gathers(0, 0, True)

                def body(i, first, last=False):
                    gathers(i, 1, first)
                    scatters(i, 0, first)
                    if not last:
                        gathers(i + 1, 0, False)
                    scatters(i, 1, first)

                body(0, True)
                with pool.Fori(1, half - 1) as i:
                    body(i, False)
                body(half - 1, False, True)
                for t in range(S):
                    pool.wait_ge(scattered[t], scatters_of(t, half, 0, 1))

            @block.vector
            def _(dve):
                def targets(i, h, first):
                    q = d[h]
                    Jt = J[target][h]
                    dve.wait_ge(loaded[h], loads_of(h, i))
                    if not first or h == 1:
                        dve.wait_ge(d[1 - h].sem, d[1 - h].end(i - (1 - h)))
                    if not first:
                        dve.wait_ge(m[h].sem, m[h].at("merged", i - 1))
                    dve.tensor_tensor(same[h][:, :, :], bc3(Jt[:, :], [P, S, P]),
                                      B[h][:, :].rearrange("p (q s) -> p s q", s=S), ALU.is_equal).then_inc(q.sem, 1)
                    dve.wait_ge(q.sem, q.at("equal", i))
                    dve.tensor_tensor(masked[:, :, :], same[h][:, :, :],
                                      earlier[:, :].unsqueeze(1).broadcast_to([P, S, P]), ALU.mult).then_inc(q.sem, 1)
                    dve.wait_ge(q.sem, q.at("masked", i))
                    dve.tensor_reduce(rep[:, :], masked[:, :, :], axis=AX.X, op=ALU.max).then_inc(q.sem, 1)
                    dve.wait_ge(q.sem, q.at("repeated", i))
                    dve.tensor_scalar(alt[:, :], Jt[:, :], -1.0, spare[:, :], ALU.mult, ALU.add).then_inc(q.sem, 1)
                    dve.wait_ge(q.sem, q.at("to_spare", i))
                    dve.tensor_tensor(alt[:, :], alt[:, :], rep[:, :], ALU.mult).then_inc(q.sem, 1)
                    dve.wait_ge(q.sem, q.at("if_repeated", i))
                    if not first:
                        for t in range(S):
                            dve.wait_ge(scattered[t], scatters_of(t, i, h, 2))
                    dve.tensor_tensor(index[h][:, :], alt[:, :], Jt[:, :], ALU.add).then_inc(q.sem, 1)

                def body(i, first):
                    for h in range(2):
                        q = m[h]
                        targets(i, h, first)
                        if kind in ("message", "conv"):
                            dve.wait_ge(loaded[h], loads_of(h, i))
                            dve.wait_ge(gathered[h], gathers_of(h, i))
                            if not first or h == 1:
                                dve.wait_ge(m[1 - h].sem, m[1 - h].at("summed", i - (1 - h)))
                            dve.tensor_tensor(prod[:, :, :], G[0][h][:, :, :].rearrange("p s (a f) -> p (s a) f", f=F),
                                              bc3(attr[h][:, :], [P, S * A, F]), ALU.mult).then_inc(q.sem, 1)
                            dve.wait_ge(q.sem, q.at("product", i))
                            if kind == "message":
                                if not first or h == 1:
                                    dve.wait_ge(m[1 - h].sem, m[1 - h].at("silu", i - (1 - h)))
                                to = summed[:, :, :]
                            else:
                                if not first:
                                    dve.wait_ge(m[h].sem, m[h].at("merged", i - 1))
                                to = V[h][:, :, 0:F]
                            dve.tensor_reduce(to, prod[:, :, :].rearrange("p (s a) f -> p s f a", a=A), axis=AX.X,
                                              op=ALU.add).then_inc(q.sem, 1)
                            if kind == "conv":
                                dve.wait_ge(q.sem, q.at("summed", i))
                                dve.tensor_copy(V[h][:, :, F:F + 1], wt[h][:, :].unsqueeze(2)).then_inc(q.sem, 1)
                        if kind == "gcn":
                            dve.wait_ge(loaded[h], loads_of(h, i))
                            dve.wait_ge(gathered[h], gathers_of(h, i))
                            if not first:
                                dve.wait_ge(m[h].sem, m[h].at("merged", i - 1))
                            dve.tensor_tensor(V[h][:, :, :], G[0][h][:, :, :], bc3(wt[h][:, :], [P, S, F]),
                                              ALU.mult).then_inc(q.sem, 1)
                        if kind == "mlp0":
                            dve.wait_ge(q.sem, q.at("attr_turned", i))
                            dve.tensor_copy(attr_t[:, :], ps_attr[0:S * A, 0:P]).then_inc(q.sem, 1)
                            norm_stats(dve, q, "enc", i, squares[:, :, :], D, S, stat)
                            dve.wait_ge(q.sem, q.at(rsqrt_names("enc")[-1], i))
                            dve.tensor_tensor(state[:, :, :], ps_o0[0:P, 0:S * D].rearrange("p (s d) -> p s d", d=D),
                                              bc3(stat[:, 0, 0:S], [P, S, D]), ALU.mult).then_inc(q.sem, 1)
                            dve.wait_ge(q.sem, q.at("enc_norm", i))
                            dve.tensor_tensor(state[:, :, :], state[:, :, :],
                                              gb["eenc"][:, 0, :].unsqueeze(1).broadcast_to([P, S, D]), ALU.mult).then_inc(q.sem, 1)
                            dve.wait_ge(q.sem, q.at("enc_gain", i))
                            dve.tensor_tensor(state[:, :, :], state[:, :, :],
                                              gb["eenc"][:, 1, :].unsqueeze(1).broadcast_to([P, S, D]), ALU.add).then_inc(q.sem, 1)
                        if mlp:
                            norm_stats(dve, q, "upd", i, squares[:, :, :], D, S, stat)
                            if not first:
                                dve.wait_ge(m[h].sem, m[h].at("merged", i - 1))
                            dve.wait_ge(q.sem, q.at(rsqrt_names("upd")[-1], i))
                            dve.tensor_tensor(V[h][:, :, :], ps_o1[0:P, 0:S * D].rearrange("p (s d) -> p s d", d=D),
                                              bc3(stat[:, 0, 0:S], [P, S, D]), ALU.mult).then_inc(q.sem, 1)
                            dve.wait_ge(q.sem, q.at("upd_norm", i))
                            dve.tensor_tensor(V[h][:, :, :], V[h][:, :, :],
                                              gb[f"eblk_{rnd}"][:, 0, :].unsqueeze(1).broadcast_to([P, S, D]), ALU.mult).then_inc(q.sem, 1)
                            dve.wait_ge(q.sem, q.at("upd_gain", i))
                            dve.tensor_tensor(V[h][:, :, :], V[h][:, :, :],
                                              gb[f"eblk_{rnd}"][:, 1, :].unsqueeze(1).broadcast_to([P, S, D]), ALU.add).then_inc(q.sem, 1)
                        if kind == "mlp0":
                            dve.wait_ge(q.sem, q.at("upd_bias", i))
                            dve.tensor_tensor(V[h][:, :, :], V[h][:, :, :], state[:, :, :], ALU.add).then_inc(q.sem, 1)

                rolled(dve, half, body)

            @block.scalar
            def _(act):
                def body(i, first):
                    for h in range(2):
                        q = m[h]
                        if kind == "message":
                            act.wait_ge(q.sem, q.at("summed", i))
                            if not first:
                                act.wait_ge(m[h].sem, m[h].at("merged", i - 1))
                            act.activation(V[h][:, :, :], summed[:, :, :], ACT.Silu,
                                           scale=float(1 / np.float32(np.sqrt(F * A)))).then_inc(q.sem, 1)
                        if kind == "mlp0":
                            act.wait_ge(q.sem, q.at("hidden0", i))
                            act.activation(act0[:, :], ps_h0[:, 0:PAIRS * P], ACT.Silu, bias=col["eenc0"][:, :]).then_inc(q.sem, 1)
                            act.wait_ge(q.sem, q.at("out0", i))
                            act.activation(squares[:, :, :].rearrange("p s d -> p (s d)"), ps_o0[0:P, 0:S * D], ACT.Square).then_inc(q.sem, 1)
                            act.wait_ge(q.sem, q.at("state_turned", i))
                            act.activation(state_t[0][:, :], ps_st[:, 0:PAIRS * P], ACT.Copy).then_inc(q.sem, 1)
                        if mlp:
                            act.wait_ge(q.sem, q.at("hidden1", i))
                            act.activation(act1[:, :], ps_h1[:, 0:PAIRS * P], ACT.Silu).then_inc(q.sem, 1)
                            act.wait_ge(q.sem, q.at("out1", i))
                            act.activation(squares[:, :, :].rearrange("p s d -> p (s d)"), ps_o1[0:P, 0:S * D], ACT.Square).then_inc(q.sem, 1)
                        if kind == "mlp0":
                            act.wait_ge(q.sem, q.at("next_turned", i))
                            if not first:
                                act.wait_ge(stored[h], stores_of(h, i - 1))
                            act.activation(next_t[h][:, :], ps_nt[:, 0:PAIRS * P], ACT.Copy).then_inc(q.sem, 1)
                        act.wait_ge(q.sem, q.at("merged", i))
                        act.wait_ge(d[h].sem, d[h].at("index", i))
                        act.activation(SV[h][:, :, :].rearrange("p s w -> p (s w)"), ps_merged[0:P, 0:S * width], ACT.Copy).then_inc(q.sem, 1)

                rolled(act, half, body)

            @block.tensor
            def _(pe):
                def body(i, first):
                    for h in range(2):
                        q = m[h]
                        if kind == "mlp0":
                            pe.wait_ge(loaded[h], loads_of(h, i))
                            if not first or h == 1:
                                pe.wait_ge(m[1 - h].sem, m[1 - h].end(i - (1 - h)))
                            pe.matmul(ps_attr[0:S * A, 0:P], attr[h][:, :], ident[:, :], start=True, stop=True).then_inc(q.sem, 1)
                            pe.wait_ge(q.sem, q.at("attr_t", i))
                            for k in range(PAIRS):
                                last = pe.matmul(ps_h0[:, k * P:(k + 1) * P], w_eenc0[:, k * 2 * D:(k + 1) * 2 * D],
                                                 attr_t[:, :], start=True, stop=True)
                            last.then_inc(q.sem, 1)
                            pe.wait_ge(q.sem, q.at("act0", i))
                            pe.matmul(ps_o0[0:P, 0:S * D], ones[:, :], row["eenc1"][:, :], start=True, stop=False)
                            for k in range(PAIRS):
                                last = pe.matmul(ps_o0[0:P, k * 2 * D:(k + 1) * 2 * D], act0[:, k * P:(k + 1) * P],
                                                 W["eenc1"][:, :], start=False, stop=k == PAIRS - 1)
                            last.then_inc(q.sem, 1)
                            pe.wait_ge(q.sem, q.at("enc_bias", i))
                            for k in range(PAIRS):
                                last = pe.matmul(ps_st[:, k * P:(k + 1) * P],
                                                 state[:, 2 * k:2 * k + 2, :].rearrange("p s d -> p (s d)"), ident[:, :],
                                                 start=True, stop=True)
                            last.then_inc(q.sem, 1)
                            pe.wait_ge(q.sem, q.at("state_t", i))
                        elif mlp:
                            pe.wait_ge(loaded[h], loads_of(h, i))
                            if not first or h == 1:
                                pe.wait_ge(m[1 - h].sem, m[1 - h].end(i - (1 - h)))
                        if mlp:
                            pe.wait_ge(gathered[h], gathers_of(h, i))
                            pe.matmul(ps_h1[:, 0:PAIRS * P], W[f"eblk_e{rnd}"][:, :],
                                      state_t[0 if kind == "mlp0" else h][:, :], start=True, stop=False)
                            for n in range(2):
                                for k in range(PAIRS):
                                    last = pe.matmul(ps_h1[:, k * P:(k + 1) * P],
                                                     G[n][h][:, 2 * k:2 * k + 2, :].rearrange("p s d -> p (s d)"),
                                                     ident[:, :], start=False, stop=n == 1 and k == PAIRS - 1)
                            last.then_inc(q.sem, 1)
                            pe.wait_ge(q.sem, q.at("act1", i))
                            pe.matmul(ps_o1[0:P, 0:S * D], ones[:, :], row[f"eblk1_{rnd}"][:, :], start=True, stop=False)
                            for k in range(PAIRS):
                                last = pe.matmul(ps_o1[0:P, k * 2 * D:(k + 1) * 2 * D], act1[:, k * P:(k + 1) * P],
                                                 W[f"eblk1{rnd}"][:, :], start=False, stop=k == PAIRS - 1)
                            last.then_inc(q.sem, 1)
                        if kind == "mlp0":
                            pe.wait_ge(q.sem, q.at("state_added", i))
                            for k in range(PAIRS):
                                last = pe.matmul(ps_nt[:, k * P:(k + 1) * P],
                                                 V[h][:, 2 * k:2 * k + 2, :].rearrange("p s d -> p (s d)"), ident[:, :],
                                                 start=True, stop=True)
                            last.then_inc(q.sem, 1)
                        pe.wait_ge(q.sem, q.before("merged", i))
                        pe.wait_ge(d[h].sem, d[h].at("equal", i))
                        if not first or h == 1:
                            pe.wait_ge(m[1 - h].sem, m[1 - h].end(i - (1 - h)))
                        for t in range(S):
                            last = pe.matmul(ps_merged[0:P, t * width:(t + 1) * width], same[h][:, t, :], V[h][:, t, :],
                                             start=True, stop=True)
                        last.then_inc(q.sem, 1)

                rolled(pe, half, body)

        for h in range(2):
            advance(main[h], m[h].n * half)
            advance(dedup[h], d[h].n * half)
            advance(loaded[h], 16 * n_loads * half)
            if kind == "mlp0":
                advance(stored[h], 16 * half)
        for t in range(S):
            advance(scattered[t], 16 * UNITS)

    def node_pass(name, loads, stores, steps, dve_body, act_body, pe_body, bufs):
        q = Chain(main[0], base(main[0]), steps)
        b_loaded, b_stored = base(loaded[0]), base(stored[0])

        def ready(step, i):
            if step == q.steps[0]:
                return loaded[0], i * (16 * len(loads)) + (b_loaded + 16 * len(loads))
            return q.sem, q.before(step, i)

        block = bufs.enter_context(nc.Block())

        @block.sync
        def _(sp):
            def body(i, first):
                if not first:
                    sp.wait_ge(q.sem, q.end(i - 1))
                    sp.sem_inc(sp_tick, 1)
                    sp.wait_ge(stored[0], i * (16 * len(stores)) + b_stored)
                    sp.sem_inc(sp_tick, 1)
                u = bass.ds(i, 1)
                for tile, rows_ in loads:
                    sp.dma_start(tile, rows_[u].squeeze(0)).then_inc(loaded[0], 16)
                for rows_, tile, step in stores:
                    sp.wait_ge(q.sem, q.at(step, i))
                    sp.sem_inc(sp_tick, 1)
                    sp.dma_start(rows_[u].squeeze(0), tile).then_inc(stored[0], 16)

            rolled(sp, NODE_UNITS, body)
            sp.wait_ge(stored[0], b_stored + 16 * len(stores) * NODE_UNITS)

        @block.vector
        def _(dve):
            rolled(dve, NODE_UNITS, lambda i, first: dve_body(dve, q, ready, i))

        if act_body is not None:
            @block.scalar
            def _(act):
                rolled(act, NODE_UNITS, lambda i, first: act_body(act, q, ready, i))

        if pe_body is not None:
            @block.tensor
            def _(pe):
                rolled(pe, NODE_UNITS, lambda i, first: pe_body(pe, q, ready, i))

        advance(main[0], q.n * NODE_UNITS)
        advance(loaded[0], 16 * len(loads) * NODE_UNITS)
        advance(stored[0], 16 * len(stores) * NODE_UNITS)

    def ln_relu(dve, q, ready, p, i, x, centered, squares, v, h):
        dve.wait_ge(*ready(f"{p}_sum", i))
        dve.tensor_reduce(v[:, 1, 0:C], x, axis=AX.X, op=ALU.add).then_inc(q.sem, 1)
        dve.wait_ge(*ready(f"{p}_mean", i))
        dve.tensor_scalar(v[:, 1, 0:C], v[:, 1, 0:C], -1.0 / F, None, ALU.mult).then_inc(q.sem, 1)
        dve.wait_ge(*ready(f"{p}_center", i))
        dve.tensor_tensor(centered, x, bc3(v[:, 1, 0:C], [P, C, F]), ALU.add).then_inc(q.sem, 1)
        dve.wait_ge(*ready(f"{p}_square", i))
        dve.tensor_tensor(squares, centered, centered, ALU.mult).then_inc(q.sem, 1)
        norm_stats(dve, q, p, i, squares, F, C, v)
        dve.wait_ge(*ready(f"{p}_norm", i))
        dve.scalar_tensor_tensor(out=h, in0=centered, scalar=0.0, in1=bc3(v[:, 0, 0:C], [P, C, F]),
                                 op0=ALU.max, op1=ALU.mult).then_inc(q.sem, 1)

    def ln_affine(dve, q, ready, p, i, x_ps, squares, v, k, o):
        norm_stats(dve, q, p, i, squares, D, C, v)
        dve.wait_ge(*ready(f"{p}_norm", i))
        dve.tensor_tensor(o, x_ps[0:P, 0:C * D].rearrange("p (c d) -> p c d", d=D), bc3(v[:, 0, 0:C], [P, C, D]),
                          ALU.mult).then_inc(q.sem, 1)
        dve.wait_ge(*ready(f"{p}_gain", i))
        dve.tensor_tensor(o, o, gb[k][:, 0, :].unsqueeze(1).broadcast_to([P, C, D]), ALU.mult).then_inc(q.sem, 1)
        dve.wait_ge(*ready(f"{p}_bias", i))
        dve.tensor_tensor(o, o, gb[k][:, 1, :].unsqueeze(1).broadcast_to([P, C, D]), ALU.add).then_inc(q.sem, 1)

    def flat(ap):
        return ap.rearrange("p a b -> p (a b)")

    def tables_of(agg, tile, width):
        return [(tile[:, t, :], node_rows(agg[t])) for t in range(S)]

    def turn_pairs(pe, ps_, frm):
        for k in range(C // 2):
            last = pe.matmul(ps_[:, k * P:(k + 1) * P], flat(frm[:, 2 * k:2 * k + 2, :]), ident[:, :], start=True, stop=True)
        return last

    def by_node(pe, ps_, turned, w, width, bias=None):
        if bias is not None:
            pe.matmul(ps_[0:P, 0:C * width], ones[:, :], bias[:, 0:C * width], start=True, stop=False)
        for k in range(C // 2):
            last = pe.matmul(ps_[0:P, k * 2 * width:(k + 1) * 2 * width], turned[:, k * P:(k + 1) * P], w,
                             start=bias is None, stop=bias is None or k == C // 2 - 1)
        return last

    TW = C * F
    NORM_UPD = float(1 / np.float32(np.sqrt(F * F)))
    NORM_LIN = float(1 / np.float32(np.sqrt(F)))

    def pass_scope(name, tiles, banks):
        st = ExitStack()
        t = {k: sb(f"{name}_{k}", shape, F32, st) for k, shape in tiles.items()}
        p = {k: st.enter_context(nc.psum_tensor(f"{name}_ps_{k}", [2 * D, 512], F32)) for k in banks}
        return st, t, p


    st, t, ps = pass_scope("n0", dict(x=[P, C, F], c=[P, C, F], sq=[P, C, F], v=[P, 3, 8], h=[P, C, F], ht=[TW, P],
                                      y=[P, 512]), ["t", "y"])
    with st:
        def n0_dve(dve, q, ready, i, t=t):
            ln_relu(dve, q, ready, "x", i, t["x"][:, :, :], t["c"][:, :, :], t["sq"][:, :, :], t["v"], t["h"][:, :, :])

        def n0_act(act, q, ready, i, t=t, ps=ps):
            act.wait_ge(*ready("h_t", i))
            act.activation(t["ht"][:, :], ps["t"][0:TW, 0:P], ACT.Copy).then_inc(q.sem, 1)
            act.wait_ge(*ready("y_out", i))
            act.activation(t["y"][:, :], ps["y"][0:P, :], ACT.Copy).then_inc(q.sem, 1)

        def n0_pe(pe, q, ready, i, t=t, ps=ps):
            pe.wait_ge(*ready("h_turned", i))
            pe.matmul(ps["t"][0:TW, 0:P], flat(t["h"][:, :, :]), ident[:, :], start=True, stop=True).then_inc(q.sem, 1)
            pe.wait_ge(*ready("y", i))
            pe.matmul(ps["y"][0:P, :], t["ht"][:, :], w_msg[:, :], start=True, stop=True).then_inc(q.sem, 1)

        node_pass("n0", [(flat(t["x"][:, :, :]), node_rows(ins["x"]))],
                  [(node_rows(h0_d), flat(t["h"][:, :, :]), "x_norm"), (node_rows(y0), t["y"][:, :], "y_out")],
                  ln_names("x", False) + ["h_turned", "h_t", "y", "y_out"], n0_dve, n0_act, n0_pe, st)

    edge_pass("e0", [(y0, A * F, "dst")], "src", F, agg0, "message")

    st, t, ps = pass_scope("n1", dict(x=[P, C, F], h0=[P, C, F], tab=[P, S, C * F], ag=[P, TW], agt=[TW, P], al=[P, C, F],
                                      h0t=[TW, P], prod=[P, C * F, F], u=[P, C, F], us=[P, C, F], ust=[TW, P],
                                      x1=[P, C, F], c=[P, C, F], sq=[P, C, F], v=[P, 3, 8], h=[P, C, F], ht=[TW, P],
                                      y=[P, 512]), ["agt", "al", "h0t", "up0", "up1", "ut", "ul", "y"])
    with st:
        def n1_dve(dve, q, ready, i, t=t, ps=ps):
            dve.wait_ge(*ready("agg_sum", i))
            dve.tensor_reduce(t["ag"][:, :], t["tab"][:, :, :].rearrange("p t x -> p x t"), axis=AX.X, op=ALU.add).then_inc(q.sem, 1)
            dve.wait_ge(*ready("upd_prod", i))
            for b in range(2):
                last = dve.tensor_tensor(t["prod"][:, b * 32:(b + 1) * 32, :],
                                         ps[f"up{b}"][0:P, :].rearrange("p (a f) -> p a f", f=F),
                                         bc3(flat(t["al"][:, 2 * b:2 * b + 2, :]), [P, 32, F]), ALU.mult)
            last.then_inc(q.sem, 1)
            dve.wait_ge(*ready("upd_sum", i))
            dve.tensor_reduce(t["u"][:, :, :], t["prod"][:, :, :].rearrange("p (c h) k -> p c k h", c=C), axis=AX.X,
                              op=ALU.add).then_inc(q.sem, 1)
            dve.wait_ge(*ready("x_upd", i))
            dve.scalar_tensor_tensor(out=flat(t["x1"][:, :, :]), in0=ps["ul"][0:P, 0:TW], scalar=NORM_LIN,
                                     in1=flat(t["h0"][:, :, :]), op0=ALU.mult, op1=ALU.add).then_inc(q.sem, 1)
            dve.wait_ge(*ready("x_new", i))
            dve.tensor_tensor(t["x1"][:, :, :], t["x1"][:, :, :], t["x"][:, :, :], ALU.add).then_inc(q.sem, 1)
            ln_relu(dve, q, ready, "x", i, t["x1"][:, :, :], t["c"][:, :, :], t["sq"][:, :, :], t["v"], t["h"][:, :, :])

        def n1_act(act, q, ready, i, t=t, ps=ps):
            act.wait_ge(*ready("agg_t", i))
            act.activation(t["agt"][:, :], ps["agt"][0:TW, 0:P], ACT.Copy).then_inc(q.sem, 1)
            act.wait_ge(*ready("agg_scaled", i))
            act.activation(flat(t["al"][:, :, :]), ps["al"][0:P, 0:TW], ACT.Copy, scale=NORM_LIN).then_inc(q.sem, 1)
            act.wait_ge(*ready("h0_t", i))
            act.activation(t["h0t"][:, :], ps["h0t"][0:TW, 0:P], ACT.Copy).then_inc(q.sem, 1)
            act.wait_ge(*ready("upd_silu", i))
            act.activation(t["us"][:, :, :], t["u"][:, :, :], ACT.Silu, scale=NORM_UPD).then_inc(q.sem, 1)
            act.wait_ge(*ready("u_t", i))
            act.activation(t["ust"][:, :], ps["ut"][0:TW, 0:P], ACT.Copy).then_inc(q.sem, 1)
            act.wait_ge(*ready("h_t", i))
            act.activation(t["ht"][:, :], ps["agt"][0:TW, 0:P], ACT.Copy).then_inc(q.sem, 1)
            act.wait_ge(*ready("y_out", i))
            act.activation(t["y"][:, :], ps["y"][0:P, :], ACT.Copy).then_inc(q.sem, 1)

        def n1_pe(pe, q, ready, i, t=t, ps=ps):
            pe.wait_ge(*ready("agg_turned", i))
            pe.matmul(ps["agt"][0:TW, 0:P], t["ag"][:, :], ident[:, :], start=True, stop=True).then_inc(q.sem, 1)
            pe.wait_ge(*ready("agg_lin", i))
            pe.matmul(ps["al"][0:P, 0:TW], t["agt"][:, :], w_msg_lin[:, :], start=True, stop=True).then_inc(q.sem, 1)
            pe.wait_ge(*ready("h0_turned", i))
            pe.matmul(ps["h0t"][0:TW, 0:P], flat(t["h0"][:, :, :]), ident[:, :], start=True, stop=True).then_inc(q.sem, 1)
            pe.wait_ge(*ready("upd", i))
            for b in range(2):
                last = pe.matmul(ps[f"up{b}"][0:P, :], t["h0t"][:, :], w_upd[:, b * 512:(b + 1) * 512], start=True, stop=True)
            last.then_inc(q.sem, 1)
            pe.wait_ge(*ready("u_turned", i))
            pe.matmul(ps["ut"][0:TW, 0:P], flat(t["us"][:, :, :]), ident[:, :], start=True, stop=True).then_inc(q.sem, 1)
            pe.wait_ge(*ready("u_lin", i))
            pe.matmul(ps["ul"][0:P, 0:TW], t["ust"][:, :], w_upd_lin[:, :], start=True, stop=True).then_inc(q.sem, 1)
            pe.wait_ge(*ready("h_turned", i))
            pe.matmul(ps["agt"][0:TW, 0:P], flat(t["h"][:, :, :]), ident[:, :], start=True, stop=True).then_inc(q.sem, 1)
            pe.wait_ge(*ready("y", i))
            pe.matmul(ps["y"][0:P, :], t["ht"][:, :], w_conv[:, :], start=True, stop=True).then_inc(q.sem, 1)

        node_pass("n1", [(flat(t["x"][:, :, :]), node_rows(ins["x"])), (flat(t["h0"][:, :, :]), node_rows(h0_d))]
                  + tables_of(agg0, t["tab"], F),
                  [(node_rows(x1_d), flat(t["x1"][:, :, :]), "x_new"), (node_rows(y1), t["y"][:, :], "y_out")],
                  ["agg_sum", "agg_turned", "agg_t", "agg_lin", "agg_scaled", "h0_turned", "h0_t", "upd", "upd_prod",
                   "upd_sum", "upd_silu", "u_turned", "u_t", "u_lin", "x_upd", "x_new"]
                  + ln_names("x", False) + ["h_turned", "h_t", "y", "y_out"], n1_dve, n1_act, n1_pe, st)

    edge_pass("e1", [(y1, A * F, "src")], "dst", F + 1, agg1, "conv")

    send_recv = ["node_turned", "node_t", "send", "send_out", "recv", "recv_out"]

    def send_recv_act(act, q, ready, i, t, ps):
        act.wait_ge(*ready("node_t", i))
        act.activation(t["nt"][:, :], ps["nt"][:, 0:2 * P], ACT.Copy).then_inc(q.sem, 1)
        act.wait_ge(*ready("send_out", i))
        act.activation(flat(t["send"][:, :, :]), ps["send"][0:P, 0:C * D], ACT.Copy).then_inc(q.sem, 1)
        act.wait_ge(*ready("recv_out", i))
        act.activation(flat(t["recv"][:, :, :]), ps["recv"][0:P, 0:C * D], ACT.Copy).then_inc(q.sem, 1)

    def send_recv_pe(pe, q, ready, i, t, ps, r, node):
        pe.wait_ge(*ready("node_turned", i))
        turn_pairs(pe, ps["nt"], t[node]).then_inc(q.sem, 1)
        pe.wait_ge(*ready("send", i))
        by_node(pe, ps["send"], t["nt"], W[f"eblk_s{r}"][:, :], D).then_inc(q.sem, 1)
        pe.wait_ge(*ready("recv", i))
        by_node(pe, ps["recv"], t["nt"], W[f"eblk_r{r}"][:, :], D, row[f"eblk0_{r}"]).then_inc(q.sem, 1)

    st, t, ps = pass_scope("n2", dict(x=[P, C, F], tab=[P, S, C * (F + 1)], ag=[P, C, F + 1], cv=[P, C, F], deg=[P, 8],
                                      dis=[P, 8], tmp=[P, 8], pos=[P, 8], x2=[P, C, F], c=[P, C, F], sq=[P, C, F],
                                      v=[P, 3, 8], h=[P, C, F], ht=[TW, P], a=[2 * D, 2 * P], sqd=[P, C, D],
                                      n=[P, C, D], nt=[2 * D, 2 * P], send=[P, C, D], recv=[P, C, D]),
                           ["ht", "a", "o", "nt", "send", "recv"])
    with st:
        def n2_dve(dve, q, ready, i, t=t, ps=ps):
            dve.wait_ge(*ready("agg_sum", i))
            dve.tensor_reduce(flat(t["ag"][:, :, :]), t["tab"][:, :, :].rearrange("p t x -> p x t"), axis=AX.X, op=ALU.add).then_inc(q.sem, 1)
            dve.wait_ge(*ready("conv_bias", i))
            dve.tensor_tensor(t["cv"][:, :, :], t["ag"][:, :, 0:F], conv_bias[:, :].unsqueeze(1).broadcast_to([P, C, F]),
                              ALU.add).then_inc(q.sem, 1)
            dve.wait_ge(*ready("x_new", i))
            dve.scalar_tensor_tensor(out=t["x2"][:, :, :], in0=t["cv"][:, :, :], scalar=0.0, in1=t["x"][:, :, :],
                                     op0=ALU.max, op1=ALU.add).then_inc(q.sem, 1)
            deg = t["deg"][:, 0:C]
            dve.wait_ge(*ready("degree", i))
            dve.tensor_scalar(deg, t["ag"][:, :, F], 1.0, None, ALU.add).then_inc(q.sem, 1)
            dve.wait_ge(*ready("degree_positive", i))
            dve.tensor_scalar(t["pos"][:, 0:C], deg, 0.0, None, ALU.is_gt).then_inc(q.sem, 1)
            dve.wait_ge(*ready("dis_rsqrt0", i))
            dve.tensor_scalar(deg, deg, 1e-30, None, ALU.max).then_inc(q.sem, 1)
            newton(dve, q, "dis", i, deg, t["dis"][:, 0:C], t["tmp"][:, 0:C])
            dve.wait_ge(*ready("dis", i))
            dve.tensor_tensor(t["dis"][:, 0:C], t["dis"][:, 0:C], t["pos"][:, 0:C], ALU.mult).then_inc(q.sem, 1)
            ln_relu(dve, q, ready, "x", i, t["x2"][:, :, :], t["c"][:, :, :], t["sq"][:, :, :], t["v"], t["h"][:, :, :])
            ln_affine(dve, q, ready, "enc", i, ps["o"], t["sqd"][:, :, :], t["v"], "nenc", t["n"][:, :, :])

        def n2_act(act, q, ready, i, t=t, ps=ps):
            act.wait_ge(*ready("h_t", i))
            act.activation(t["ht"][:, :], ps["ht"][0:TW, 0:P], ACT.Copy).then_inc(q.sem, 1)
            act.wait_ge(*ready("act", i))
            act.activation(t["a"][:, :], ps["a"][:, 0:2 * P], ACT.Silu, bias=col["nenc0"][:, :]).then_inc(q.sem, 1)
            act.wait_ge(*ready("enc_square", i))
            act.activation(flat(t["sqd"][:, :, :]), ps["o"][0:P, 0:C * D], ACT.Square).then_inc(q.sem, 1)
            send_recv_act(act, q, ready, i, t, ps)

        def n2_pe(pe, q, ready, i, t=t, ps=ps):
            pe.wait_ge(*ready("h_turned", i))
            pe.matmul(ps["ht"][0:TW, 0:P], flat(t["h"][:, :, :]), ident[:, :], start=True, stop=True).then_inc(q.sem, 1)
            pe.wait_ge(*ready("hidden", i))
            for k in range(2):
                last = pe.matmul(ps["a"][:, k * P:(k + 1) * P], w_nenc0[:, k * 2 * D:(k + 1) * 2 * D], t["ht"][:, :],
                                 start=True, stop=True)
            last.then_inc(q.sem, 1)
            pe.wait_ge(*ready("out", i))
            by_node(pe, ps["o"], t["a"], W["nenc1"][:, :], D, row["nenc1"]).then_inc(q.sem, 1)
            send_recv_pe(pe, q, ready, i, t, ps, 0, "n")

        node_pass("n2", [(flat(t["x"][:, :, :]), node_rows(x1_d))] + tables_of(agg1, t["tab"], F + 1),
                  [(node_rows(x2_d), flat(t["x2"][:, :, :]), "x_new"), (node_rows(dis_d), t["dis"][:, 0:C], "dis"),
                   (node_rows(n0_d), flat(t["n"][:, :, :]), "enc_bias"),
                   (node_rows(send_d[0]), flat(t["send"][:, :, :]), "send_out"),
                   (node_rows(recv_d[0]), flat(t["recv"][:, :, :]), "recv_out")],
                  ["agg_sum", "conv_bias", "x_new", "degree", "degree_positive"] + rsqrt_names("dis") + ["dis"]
                  + ln_names("x", False) + ["h_turned", "h_t", "hidden", "act", "out"] + ln_names("enc", True)
                  + ["enc_gain", "enc_bias"] + send_recv, n2_dve, n2_act, n2_pe, st)

    edge_pass("e2", [(send_d[0], D, "src"), (recv_d[0], D, "dst")], "dst", D, agg2, "mlp0", 0)

    node_update = ["agg_sum", "prev_turned", "prev_t", "agg_turned", "agg_t", "hidden", "act", "out"] \
        + ln_names("upd", True) + ["upd_gain", "upd_bias", "node_new"]

    def node_update_dve(dve, q, ready, i, t, ps, r):
        dve.wait_ge(*ready("agg_sum", i))
        dve.tensor_reduce(flat(t["ag"][:, :, :]), t["tab"][:, :, :].rearrange("p t x -> p x t"), axis=AX.X, op=ALU.add).then_inc(q.sem, 1)
        ln_affine(dve, q, ready, "upd", i, ps["o"], t["sqd"][:, :, :], t["v"], f"nblk_{r}", t["n"][:, :, :])
        dve.wait_ge(*ready("node_new", i))
        dve.tensor_tensor(t["n"][:, :, :], t["n"][:, :, :], t["prev"][:, :, :], ALU.add).then_inc(q.sem, 1)

    def node_update_act(act, q, ready, i, t, ps, r):
        act.wait_ge(*ready("prev_t", i))
        act.activation(t["pt"][:, :], ps["nt"][:, 0:2 * P], ACT.Copy).then_inc(q.sem, 1)
        act.wait_ge(*ready("agg_t", i))
        act.activation(t["agt"][:, :], ps["agt"][:, 0:2 * P], ACT.Copy).then_inc(q.sem, 1)
        act.wait_ge(*ready("act", i))
        act.activation(t["a"][:, :], ps["a"][:, 0:2 * P], ACT.Silu, bias=col[f"nblk0_{r}"][:, :]).then_inc(q.sem, 1)
        act.wait_ge(*ready("upd_square", i))
        act.activation(flat(t["sqd"][:, :, :]), ps["o"][0:P, 0:C * D], ACT.Square).then_inc(q.sem, 1)

    def node_update_pe(pe, q, ready, i, t, ps, r):
        pe.wait_ge(*ready("prev_turned", i))
        turn_pairs(pe, ps["nt"], t["prev"]).then_inc(q.sem, 1)
        pe.wait_ge(*ready("agg_turned", i))
        turn_pairs(pe, ps["agt"], t["ag"]).then_inc(q.sem, 1)
        pe.wait_ge(*ready("hidden", i))
        pe.matmul(ps["a"][:, 0:2 * P], W[f"nblk_n{r}"][:, :], t["pt"][:, :], start=True, stop=False)
        pe.matmul(ps["a"][:, 0:2 * P], W[f"nblk_a{r}"][:, :], t["agt"][:, :], start=False, stop=True).then_inc(q.sem, 1)
        pe.wait_ge(*ready("out", i))
        by_node(pe, ps["o"], t["a"], W[f"nblk1{r}"][:, :], D, row[f"nblk1_{r}"]).then_inc(q.sem, 1)

    node_tiles = dict(prev=[P, C, D], tab=[P, S, C * D], ag=[P, C, D], pt=[2 * D, 2 * P], agt=[2 * D, 2 * P],
                      a=[2 * D, 2 * P], sqd=[P, C, D], v=[P, 3, 8], n=[P, C, D], nt=[2 * D, 2 * P])

    st, t, ps = pass_scope("n3", node_tiles | dict(send=[P, C, D], recv=[P, C, D]), ["nt", "agt", "a", "o", "send", "recv"])
    with st:
        def n3_dve(dve, q, ready, i, t=t, ps=ps):
            node_update_dve(dve, q, ready, i, t, ps, 0)

        def n3_act(act, q, ready, i, t=t, ps=ps):
            node_update_act(act, q, ready, i, t, ps, 0)
            send_recv_act(act, q, ready, i, t, ps)

        def n3_pe(pe, q, ready, i, t=t, ps=ps):
            node_update_pe(pe, q, ready, i, t, ps, 0)
            send_recv_pe(pe, q, ready, i, t, ps, 1, "n")

        node_pass("n3", [(flat(t["prev"][:, :, :]), node_rows(n0_d))] + tables_of(agg2, t["tab"], D),
                  [(node_rows(n1_d), flat(t["n"][:, :, :]), "node_new"),
                   (node_rows(send_d[1]), flat(t["send"][:, :, :]), "send_out"),
                   (node_rows(recv_d[1]), flat(t["recv"][:, :, :]), "recv_out")],
                  node_update + send_recv, n3_dve, n3_act, n3_pe, st)

    edge_pass("e3", [(send_d[1], D, "src"), (recv_d[1], D, "dst")], "dst", D, agg2, "mlp1", 1)

    st, t, ps = pass_scope("n4", node_tiles | dict(x=[P, C, F], dis=[P, 8], a2=[2 * D, 2 * P], x3=[P, C, F], c=[P, C, F],
                                                   sq=[P, C, F], h=[P, C, F], g=[P, C, F]),
                           ["nt", "agt", "a", "o", "a2", "dec"])
    with st:
        def n4_dve(dve, q, ready, i, t=t, ps=ps):
            node_update_dve(dve, q, ready, i, t, ps, 1)
            dve.wait_ge(*ready("dec_bias", i))
            dve.tensor_tensor(t["x3"][:, :, :], ps["dec"][0:P, 0:TW].rearrange("p (c f) -> p c f", f=F),
                              dec_b1[:, :].unsqueeze(1).broadcast_to([P, C, F]), ALU.add).then_inc(q.sem, 1)
            dve.wait_ge(*ready("x_new", i))
            dve.tensor_tensor(t["x3"][:, :, :], t["x3"][:, :, :], t["x"][:, :, :], ALU.add).then_inc(q.sem, 1)
            ln_relu(dve, q, ready, "x", i, t["x3"][:, :, :], t["c"][:, :, :], t["sq"][:, :, :], t["v"], t["h"][:, :, :])
            dve.wait_ge(*ready("h_dis", i))
            dve.tensor_tensor(t["g"][:, :, :], t["h"][:, :, :], bc3(t["dis"][:, 0:C], [P, C, F]), ALU.mult).then_inc(q.sem, 1)

        def n4_act(act, q, ready, i, t=t, ps=ps):
            node_update_act(act, q, ready, i, t, ps, 1)
            act.wait_ge(*ready("node_t", i))
            act.activation(t["nt"][:, :], ps["nt"][:, 0:2 * P], ACT.Copy).then_inc(q.sem, 1)
            act.wait_ge(*ready("dec_act", i))
            act.activation(t["a2"][:, :], ps["a2"][:, 0:2 * P], ACT.Silu, bias=col["dec0"][:, :]).then_inc(q.sem, 1)

        def n4_pe(pe, q, ready, i, t=t, ps=ps):
            node_update_pe(pe, q, ready, i, t, ps, 1)
            pe.wait_ge(*ready("node_turned", i))
            turn_pairs(pe, ps["nt"], t["n"]).then_inc(q.sem, 1)
            pe.wait_ge(*ready("dec_hidden", i))
            pe.matmul(ps["a2"][:, 0:2 * P], W["dec0"][:, :], t["nt"][:, :], start=True, stop=True).then_inc(q.sem, 1)
            pe.wait_ge(*ready("dec", i))
            by_node(pe, ps["dec"], t["a2"], w_dec1[:, :], F).then_inc(q.sem, 1)

        node_pass("n4", [(flat(t["prev"][:, :, :]), node_rows(n1_d)), (flat(t["x"][:, :, :]), node_rows(x2_d)),
                         (t["dis"][:, 0:C], node_rows(dis_d))] + tables_of(agg2, t["tab"], D),
                  [(node_rows(x3_d), flat(t["x3"][:, :, :]), "x_new"), (node_rows(g1_d), flat(t["g"][:, :, :]), "h_dis")],
                  node_update + ["node_turned", "node_t", "dec_hidden", "dec_act", "dec", "dec_bias", "x_new"]
                  + ln_names("x", False) + ["h_dis"], n4_dve, n4_act, n4_pe, st)

    edge_pass("e4", [(g1_d, F, "src")], "dst", F, agg3, "gcn")

    def own_loop(dve, q, ready, i, t):
        dve.wait_ge(*ready("own", i))
        dve.tensor_tensor(flat(t["s"][:, :, :]), flat(t["s"][:, :, :]), flat(t["g"][:, :, :]), ALU.add).then_inc(q.sem, 1)
        dve.wait_ge(*ready("s_dis", i))
        dve.tensor_tensor(t["s"][:, :, :], t["s"][:, :, :], bc3(t["dis"][:, 0:C], [P, C, F]), ALU.mult).then_inc(q.sem, 1)

    st, t, ps = pass_scope("n5", dict(tab=[P, S, TW], s=[P, C, F], g=[P, C, F], dis=[P, 8], sT=[TW, P], a=[2 * TW, P],
                                      o=[P, C, F]), ["s", "a", "o"])
    with st:
        def n5_dve(dve, q, ready, i, t=t, ps=ps):
            dve.wait_ge(*ready("agg_sum", i))
            dve.tensor_reduce(flat(t["s"][:, :, :]), t["tab"][:, :, :].rearrange("p t x -> p x t"), axis=AX.X, op=ALU.add).then_inc(q.sem, 1)
            own_loop(dve, q, ready, i, t)
            dve.wait_ge(*ready("o_dis", i))
            dve.tensor_tensor(t["o"][:, :, :], ps["o"][0:P, 0:TW].rearrange("p (c f) -> p c f", f=F),
                              bc3(t["dis"][:, 0:C], [P, C, F]), ALU.mult).then_inc(q.sem, 1)

        def n5_act(act, q, ready, i, t=t, ps=ps):
            act.wait_ge(*ready("s_t", i))
            act.activation(t["sT"][:, :], ps["s"][0:TW, 0:P], ACT.Copy).then_inc(q.sem, 1)
            act.wait_ge(*ready("act", i))
            act.activation(t["a"][:, :], ps["a"][:, 0:P], ACT.Relu, bias=gcn_b1[:, :]).then_inc(q.sem, 1)

        def n5_pe(pe, q, ready, i, t=t, ps=ps):
            pe.wait_ge(*ready("s_turned", i))
            pe.matmul(ps["s"][0:TW, 0:P], flat(t["s"][:, :, :]), ident[:, :], start=True, stop=True).then_inc(q.sem, 1)
            pe.wait_ge(*ready("hidden", i))
            pe.matmul(ps["a"][:, 0:P], w_gcn1[:, :], t["sT"][:, :], start=True, stop=True).then_inc(q.sem, 1)
            pe.wait_ge(*ready("out", i))
            pe.matmul(ps["o"][0:P, 0:TW], t["a"][:, :], w_gcn2[:, :], start=True, stop=True).then_inc(q.sem, 1)

        node_pass("n5", [(flat(t["g"][:, :, :]), node_rows(g1_d)), (t["dis"][:, 0:C], node_rows(dis_d))]
                  + tables_of(agg3, t["tab"], F),
                  [(node_rows(g2_d), flat(t["o"][:, :, :]), "o_dis")],
                  ["agg_sum", "own", "s_dis", "s_turned", "s_t", "hidden", "act", "out", "o_dis"], n5_dve, n5_act, n5_pe, st)

    edge_pass("e5", [(g2_d, F, "src")], "dst", F, agg4, "gcn")

    st, t, ps = pass_scope("n6", dict(tab=[P, S, TW], s=[P, C, F], g=[P, C, F], dis=[P, 8], x=[P, C, F], o=[P, C, F]), [])
    with st:
        def n6_dve(dve, q, ready, i, t=t, ps=ps):
            dve.wait_ge(*ready("agg_sum", i))
            dve.tensor_reduce(flat(t["s"][:, :, :]), t["tab"][:, :, :].rearrange("p t x -> p x t"), axis=AX.X, op=ALU.add).then_inc(q.sem, 1)
            own_loop(dve, q, ready, i, t)
            dve.wait_ge(*ready("s_bias", i))
            dve.tensor_tensor(t["s"][:, :, :], t["s"][:, :, :], gcn_b2[:, :].unsqueeze(1).broadcast_to([P, C, F]),
                              ALU.add).then_inc(q.sem, 1)
            dve.wait_ge(*ready("x_new", i))
            dve.tensor_tensor(t["o"][:, :, :], t["s"][:, :, :], t["x"][:, :, :], ALU.add).then_inc(q.sem, 1)

        node_pass("n6", [(flat(t["g"][:, :, :]), node_rows(g2_d)), (t["dis"][:, 0:C], node_rows(dis_d)),
                         (flat(t["x"][:, :, :]), node_rows(x3_d))] + tables_of(agg4, t["tab"], F),
                  [(node_rows(out), flat(t["o"][:, :, :]), "x_new")],
                  ["agg_sum", "own", "s_dis", "s_bias", "x_new"], n6_dve, None, None, st)


def kernel(**inputs):
    import concourse.bacc as bacc
    from concourse.bass_utils import run_bass_kernel_spmd

    nc = bacc.Bacc("TRN2", target_bir_lowering=False, num_devices=1)
    arrays, aps = {}, {}
    for name, value in inputs.items():
        value = np.ascontiguousarray(value)
        arrays[f"in_{name}"] = value
        aps[name] = nc.dram_tensor(f"in_{name}", value.shape, mybir.dt.from_np(value.dtype), kind="ExternalInput").ap()
    out = nc.dram_tensor("out_0", (N, F), F32, kind="ExternalOutput").ap()
    gnn_kernel(nc, aps, out)
    result = run_bass_kernel_spmd(nc, [arrays], core_ids=[0])
    return result.results[0]["out_0"]
```

```python
from contextlib import ExitStack

import numpy as np
import concourse.bass as bass
from concourse import mybir

F32 = mybir.dt.float32
BF16 = mybir.dt.bfloat16
I32 = mybir.dt.int32
ALU = mybir.AluOpType
ACT = mybir.ActivationFunctionType
AX = mybir.AxisListType

N = 12500
E = 412500
P = 125
WIN = 64
S = 6
UNITS = E // (P * S)
PAIRS = S // 2
C = 4
NODE_UNITS = N // (P * C)
ROWS = N + P
F = 16
A = 8
D = 64
EPS = 1e-5
RSQRT_STEPS = 12


class Chain:

    def __init__(self, sem, base, steps):
        self.sem, self.base, self.steps = sem, base, list(steps)
        assert len(set(self.steps)) == len(self.steps), self.steps
        self.n = len(self.steps)

    def at(self, step, i):
        return i * self.n + (self.base + self.steps.index(step) + 1)

    def end(self, i):
        return i * self.n + (self.base + self.n)

    def before(self, step, i):
        k = self.steps.index(step)
        assert k, step
        return i * self.n + (self.base + k)


def rsqrt_names(p):
    return [f"{p}_rsqrt{k}" for k in range(RSQRT_STEPS)]


def ln_names(p, centered):
    first = [] if centered else [f"{p}_sum", f"{p}_mean", f"{p}_center"]
    return first + [f"{p}_square", f"{p}_var"] + rsqrt_names(p) + [f"{p}_norm"]


def rolled(eng, n, body):
    body(0, True)
    with eng.Fori(1, n) as i:
        body(i, False)


def in_duos(eng, n, body, ahead=False):
    assert n % 2 and n > 6
    for d in range(3):
        body(d, d % 2, d, False)
    with eng.Fori(1, n // 2 - ahead) as j:
        body(j * 2 + 1, 1, 2, False)
        body(j * 2 + 2, 0, 2, False)
    if ahead:
        body(n - 2, 1, 2, False)
        body(n - 1, 0, 2, True)


def bc3(ap, shape):
    return ap.unsqueeze(2).broadcast_to(shape)


def gnn_kernel(nc, ins, out):
    ctx = ExitStack()
    with ctx:
        _gnn(nc, ctx, ins, out)


def _gnn(nc, ctx, ins, out):
    def sb(name, shape, dt=F32, at=None):
        return (at or ctx).enter_context(nc.sbuf_tensor(name, shape, dt))

    def sem(name):
        return ctx.enter_context(nc.semaphore(name))

    main = [sem("main_chain0"), sem("main_chain1")]
    dedup = [sem("dedup_chain0"), sem("dedup_chain1")]
    loaded = [sem("loaded0"), sem("loaded1")]
    scattered = [sem(f"scattered{t}") for t in range(S)]
    stored = [sem("stored0"), sem("stored1")]
    pool_tick = sem("pool_tick")
    sp_tick = sem("sp_tick")
    node_chain, node_loaded, node_stored = sem("node_chain"), sem("node_loaded"), sem("node_stored")
    half_chain = [sem("half_chain0"), sem("half_chain1")]
    back_chain = [sem("back_chain0"), sem("back_chain1")]
    window_chain = sem("window_chain")
    merge_chain = sem("merge_chain")
    stat_chain = sem("stat_chain")
    full_chain = [sem("full_chain0"), sem("full_chain1")]
    duo_loaded = [sem("duo_loaded0"), sem("duo_loaded1")]
    duo_stored = [sem("duo_stored0"), sem("duo_stored1")]
    duo_added = sem("duo_added")
    count = {}

    def base(s):
        return count.get(s.num, 0)

    def advance(s, by):
        count[s.num] = base(s) + by

    def dram(name, shape):
        return nc.dram_tensor(name, shape, F32).ap()

    y0 = dram("y0", [N, A * F])
    y1 = dram("y1", [N, A * F])
    h0_d = dram("h0", [N, F])
    x1_d, x2_d, x3_d = dram("x1", [N, F]), dram("x2", [N, F]), dram("x3", [N, F])
    n0_d, n1_d = dram("n0", [N, D]), dram("n1", [N, D])
    send_d = [dram("send0", [N, D]), dram("send1", [N, D])]
    recv_d = [dram("recv0", [ROWS, D]), dram("recv1", [ROWS, D])]
    dis_d = dram("dis", [N, 1])
    g1_d, g2_d = dram("g1", [N, F]), dram("g2", [N, F])
    edge_t = dram("edge_t", [UNITS, 2 * D, PAIRS * P])
    agg0 = [dram(f"agg0_{t}", [ROWS, F]) for t in range(S)]
    agg1 = [dram(f"agg1_{t}", [ROWS, F + 1]) for t in range(S)]
    agg2 = [dram(f"agg2_{t}", [ROWS, D]) for t in range(S)]
    agg3 = [dram(f"agg3_{t}", [ROWS, F]) for t in range(S)]
    agg4 = [dram(f"agg4_{t}", [ROWS, F]) for t in range(S)]

    ident = sb("ident", [P, P])
    earlier = sb("earlier", [P, P])
    spare_i = sb("spare_i", [P, 1], I32)
    spare = sb("spare", [P, 1])
    ones = sb("ones", [1, P])
    ones_col = sb("ones_col", [P, 1])
    w_msg = sb("w_msg", [C * F, C * A * F])
    w_msg_lin = sb("w_msg_lin", [C * F, C * F])
    w_upd = sb("w_upd", [C * F, C * F * F])
    w_upd_lin = sb("w_upd_lin", [C * F, C * F])
    w_conv = sb("w_conv", [C * F, C * A * F])
    conv_bias = sb("conv_bias", [P, F])
    w_nenc0 = sb("w_nenc0", [C * F, C * D])
    w_eenc0 = sb("w_eenc0", [S * A, S * D])
    w_gcn1 = sb("w_gcn1", [C * F, C * 32])
    w_gcn2 = sb("w_gcn2", [C * 32, C * F])
    gcn_b1 = sb("gcn_b1", [C * 32, 1])
    gcn_b2 = sb("gcn_b2", [P, F])
    w_dec1 = sb("w_dec1", [2 * D, 2 * F])
    dec_b1 = sb("dec_b1", [P, F])
    iota_row = sb("iota_row", [P, WIN])
    iota_col = sb("iota_col", [2 * D, 1])
    iota_i = sb("iota_i", [P, WIN], I32)
    iota_ci = sb("iota_ci", [2 * D, 1], I32)
    ones3 = sb("ones3", [3, P], BF16)
    row3 = {k: sb(f"row3_{k}", [3, S * D], BF16) for k in ("eenc1", "eblk1_0", "eblk1_1")}
    w_state = sb("w_state", [2 * D, 2 * D])
    col_state = sb("col_state", [2 * D, 1])
    both_bias = sb("both_bias", [P, D])
    disorder = sb("disorder", [1, 1], I32)
    sq = ["nenc1", "eenc1"] + [f"{w}{s}" for s in range(2) for w in
                               ("eblk_e", "eblk_s", "eblk_r", "eblk1", "nblk_n", "nblk_a", "nblk1")] + ["dec0"]
    W = {k: sb(f"w_{k}", [2 * D, 2 * D]) for k in sq}
    col = {k: sb(f"col_{k}", [2 * D, 1]) for k in ("nenc0", "eenc0", "nblk0_0", "nblk0_1", "dec0")}
    row = {k: sb(f"row_{k}", [1, S * D]) for k in ("nenc1", "eenc1", "eblk1_0", "eblk1_1", "nblk1_0", "nblk1_1",
                                                  "eblk0_0", "eblk0_1")}
    gb = {k: sb(f"gb_{k}", [P, 2, D]) for k in ("nenc", "eenc", "eblk_0", "eblk_1", "nblk_0", "nblk_1")}

    with ExitStack() as st:
        zero = sb("zero", [P, ROWS // P * D], F32, st)
        stage = {k: sb(f"stage_{k}", [2 * D, D], F32, st) for k in sq}
        stage_row = sb("stage_row", [1, len(row), D], F32, st)
        mean = sb("mean", [2 * D, len(sq)], F32, st)
        mean_row = sb("mean_row", [1, len(row)], F32, st)
        gain_col = sb("gain_col", [2 * D, 1], F32, st)
        bias_col = sb("bias_col", [2 * D, 1], F32, st)
        parts = {k: sb(f"parts_{k}", [1, 2, S * D], F32, st) for k in row3}
        parts16 = {k: sb(f"parts16_{k}", [1, 3, S * D], BF16, st) for k in row3}
        split = sem("split")
        placed = sem("placed")
        DP = max(k for k in range(1, P + 1) if UNITS // 2 % k == 0)
        DR = UNITS // 2 // DP
        targets = sb("targets", [DP, DR, 2 * P * S], I32, st)
        first_target = sb("first_target", [DP, DR], F32, st)
        extent = sb("extent", [DP, 4, DR], F32, st)
        outside = sb("outside", [DP, 1], F32, st)
        ps_setup = st.enter_context(nc.psum_tensor("ps_setup", [2 * D, 512], F32))
        ordered, multiplied = sem("ordered"), sem("multiplied")
        cleared, weights, zeroed, wchain, consts = (sem(x) for x in ("cleared", "weights", "zeroed", "wchain", "consts"))
        small = [w_msg, w_msg_lin, w_upd, w_upd_lin, w_conv, w_nenc0, w_eenc0, w_gcn1, w_gcn2, w_dec1]
        square = {
            "nenc1": ins["L2_gnn_node_enc_w1"], "eenc1": ins["L2_gnn_edge_enc_w1"], "dec0": ins["L2_gnn_dec_w0"]}
        for s in range(2):
            w0, w1 = ins["L2_gnn_edge_blk_w0"], ins["L2_gnn_node_blk_w0"]
            square |= {f"eblk_e{s}": w0[s, 0:D, :], f"eblk_s{s}": w0[s, D:2 * D, :], f"eblk_r{s}": w0[s, 2 * D:3 * D, :],
                       f"eblk1{s}": ins["L2_gnn_edge_blk_w1"][s], f"nblk_n{s}": w1[s, 0:D, :],
                       f"nblk_a{s}": w1[s, D:2 * D, :], f"nblk1{s}": ins["L2_gnn_node_blk_w1"][s]}
        rows = {"nenc1": ins["L2_gnn_node_enc_b1"], "eenc1": ins["L2_gnn_edge_enc_b1"],
                "eblk1_0": ins["L2_gnn_edge_blk_b1"][0], "eblk1_1": ins["L2_gnn_edge_blk_b1"][1],
                "nblk1_0": ins["L2_gnn_node_blk_b1"][0], "nblk1_1": ins["L2_gnn_node_blk_b1"][1],
                "eblk0_0": ins["L2_gnn_edge_blk_b0"][0], "eblk0_1": ins["L2_gnn_edge_blk_b0"][1]}
        cols = {"nenc0": ins["L2_gnn_node_enc_b0"], "eenc0": ins["L2_gnn_edge_enc_b0"],
                "nblk0_0": ins["L2_gnn_node_blk_b0"][0], "nblk0_1": ins["L2_gnn_node_blk_b0"][1],
                "dec0": ins["L2_gnn_dec_b0"]}
        gbs = {"nenc": (ins["L2_gnn_node_enc_g"], ins["L2_gnn_node_enc_beta"]),
               "eenc": (ins["L2_gnn_edge_enc_g"], ins["L2_gnn_edge_enc_beta"])}
        for s in range(2):
            gbs[f"eblk_{s}"] = (ins["L2_gnn_edge_blk_g"][s], ins["L2_gnn_edge_blk_beta"][s])
            gbs[f"nblk_{s}"] = (ins["L2_gnn_node_blk_g"][s], ins["L2_gnn_node_blk_beta"][s])
        diagonals = []
        diagonals.append((w_msg, ins["L0_gnn_W_msg_tp"].rearrange("i j h -> i (j h)"), C))
        diagonals.append((w_msg_lin, ins["L0_gnn_W_msg_lin"], C))
        diagonals.append((w_upd, ins["L0_gnn_W_upd_tp"].rearrange("i h k -> i (h k)"), C))
        diagonals.append((w_upd_lin, ins["L0_gnn_W_upd_lin"], C))
        diagonals.append((w_nenc0, ins["L2_gnn_node_enc_w0"], C))
        diagonals.append((w_eenc0, ins["L2_gnn_edge_enc_w0"], S))
        diagonals.append((w_dec1, ins["L2_gnn_dec_w1"], 2))
        gcn_w1_t = ins["L3_gnn_W1"].rearrange("o i -> i o")
        gcn_w2_t = ins["L3_gnn_W2"].rearrange("o i -> i o")
        diagonals.append((w_gcn1, gcn_w1_t, C))
        diagonals.append((w_gcn2, gcn_w2_t, C))
        n_loads = [0]

        block = st.enter_context(nc.Block())

        @block.sync
        def _(sp):
            def load(dst, src):
                sp.dma_start(dst, src).then_inc(weights, 16)
                n_loads[0] += 1

            sp.wait_ge(cleared, 2)
            with nc.allow_non_contiguous_dma(reason="small weights, transposed once"):
                for dst, src, copies in diagonals:
                    k, m = src.shape
                    for t in range(copies):
                        load(dst[t * k:(t + 1) * k, t * m:(t + 1) * m], src)
                for t in range(C):
                    for a in range(A):
                        load(w_conv[t * F:(t + 1) * F, (t * A + a) * F:(t * A + a + 1) * F],
                             ins["L1_gnn_weight_matrix"][a].rearrange("o i -> i o"))
            for k, src in square.items():
                for half in range(2):
                    load(stage[k][half * D:(half + 1) * D, :], src)
            for n, k in enumerate(row):
                load(stage_row[:, n, :], rows[k].unsqueeze(0))
            with nc.allow_non_contiguous_dma(reason="biases as columns"):
                for k in col:
                    for half in range(2):
                        load(col[k][half * D:(half + 1) * D, :], cols[k].unsqueeze(1))
                for t in range(C):
                    load(gcn_b1[t * 32:(t + 1) * 32, :], ins["L3_gnn_b1"].unsqueeze(1))
            for k in gb:
                for n in range(2):
                    load(gb[k][:, n, :], gbs[k][n].unsqueeze(0).broadcast_to([P, D]))
            with nc.allow_non_contiguous_dma(reason="gain and bias as columns"):
                for half in range(2):
                    load(gain_col[half * D:(half + 1) * D, :], ins["L2_gnn_edge_enc_g"].unsqueeze(1))
                    load(bias_col[half * D:(half + 1) * D, :], ins["L2_gnn_edge_enc_beta"].unsqueeze(1))
            load(targets[:, :, :], ins["dst"].rearrange("(p r e) -> p r e", r=DR, e=2 * P * S))
            load(conv_bias[:, :], ins["L1_gnn_bias"].unsqueeze(0).broadcast_to([P, F]))
            load(gcn_b2[:, :], ins["L3_gnn_b2"].unsqueeze(0).broadcast_to([P, F]))
            load(dec_b1[:, :], ins["L2_gnn_dec_b1"].unsqueeze(0).broadcast_to([P, F]))

        @block.scalar
        def _(act):
            act.wait_ge(cleared, 2)
            n = 0
            for tables, width in ((agg0, F), (agg1, F + 1), (agg2, D), (agg3, F), (agg4, F)):
                for table in tables:
                    act.dma_start(table.rearrange("(p r) f -> p (r f)", p=P),
                                  zero[:, 0:ROWS // P * width]).then_inc(zeroed, 16)
                    n += 1
            for table in recv_d:
                act.dma_start(table[N:ROWS, :], zero[:, 0:D]).then_inc(zeroed, 16)
                n += 1
            act.wait_ge(split, 5 * len(row3))
            n_placed = 0
            for k in row3:
                for part in range(3):
                    act.dma_start(row3[k][part:part + 1, :], parts16[k][:, part, :]).then_inc(placed, 16)
                    n_placed += 1
            act.wait_ge(placed, 16 * n_placed)
            act.wait_ge(zeroed, 16 * n)

        @block.gpsimd
        def _(pool):
            pool.memset(ident[:, :], 0.0).then_inc(consts, 1)
            pool.memset(earlier[:, :], 1.0).then_inc(consts, 1)
            pool.memset(ones[:, :], 1.0).then_inc(consts, 1)
            pool.iota(spare_i[:, :], pattern=[[0, 1]], base=N, channel_multiplier=1).then_inc(consts, 1)
            pool.iota(iota_i[:, :], pattern=[[1, WIN]], base=0, channel_multiplier=0).then_inc(consts, 1)
            for half in range(2):
                pool.wait_ge(consts, 5 + half)
                pool.iota(iota_ci[half * D:(half + 1) * D, :], pattern=[[0, 1]], base=0, channel_multiplier=1).then_inc(consts, 1)
            pool.wait_ge(consts, 7)
            pool.memset(ones3[:, :], 1.0).then_inc(consts, 1)
            pool.memset(ones_col[:, :], 1.0).then_inc(consts, 1)
            pool.wait_ge(consts, 9)
            pool.tensor_copy(iota_row[:, :], iota_i[:, :]).then_inc(consts, 1)
            pool.tensor_copy(iota_col[:, :], iota_ci[:, :]).then_inc(consts, 1)
            pool.affine_select(out=ident[:, :], in_=ident[:, :], compare_op=ALU.not_equal, fill=1.0,
                               base=0, pattern=[[-1, P]], channel_multiplier=1).then_inc(consts, 1)
            pool.affine_select(out=earlier[:, :], in_=earlier[:, :], compare_op=ALU.is_gt, fill=0.0,
                               base=0, pattern=[[-1, P]], channel_multiplier=1).then_inc(consts, 1)
            pool.tensor_copy(spare[:, :], spare_i[:, :]).then_inc(consts, 1)
            pool.wait_ge(consts, 14)

        @block.vector
        def _(dve):
            dve.memset(zero[:, :], 0.0).then_inc(cleared, 1)
            for w in small:
                last = dve.memset(w[:, :], 0.0)
            last.then_inc(cleared, 1)
            for k in sq:
                last = dve.memset(W[k][:, :], 0.0)
            last.then_inc(wchain, 1)
            dve.wait_ge(weights, 16 * n_loads[0])
            dve.wait_ge(wchain, 1)
            centered = ["nenc1", "eenc1"] + [f"{w}1{s}" for s in range(2) for w in ("eblk", "nblk")]
            for n, k in enumerate(sq):
                last = dve.tensor_reduce(mean[:, n:n + 1], stage[k][:, :], axis=AX.X, op=ALU.add)
            last = dve.tensor_reduce(mean_row[:, :], stage_row[:, :, :], axis=AX.X, op=ALU.add)
            last.then_inc(wchain, 1)
            dve.wait_ge(wchain, 2)
            dve.tensor_scalar(mean[:, :], mean[:, :], -1.0 / D, None, ALU.mult).then_inc(wchain, 1)
            dve.tensor_scalar(mean_row[:, :], mean_row[:, :], -1.0 / D, None, ALU.mult).then_inc(wchain, 1)
            dve.wait_ge(wchain, 4)
            for n, k in enumerate(sq):
                for half in range(2):
                    q = slice(half * D, (half + 1) * D)
                    if k in centered:
                        last = dve.tensor_scalar(W[k][q, q], stage[k][q, :], mean[q, n:n + 1], None, ALU.add)
                    else:
                        last = dve.tensor_copy(W[k][q, q], stage[k][q, :])
            for n, k in enumerate(row):
                for t in range(S):
                    q = slice(t * D, (t + 1) * D)
                    if k.startswith("eblk0"):
                        last = dve.tensor_copy(row[k][:, q], stage_row[:, n, :])
                    else:
                        last = dve.tensor_scalar(row[k][:, q], stage_row[:, n, :], mean_row[:, n:n + 1], None, ALU.add)
            last.then_inc(wchain, 1)
            dve.wait_ge(wchain, 5)
            dve.tensor_scalar(w_state[:, :], W["eblk_e0"][:, :], gain_col[:, :], None, ALU.mult).then_inc(wchain, 1)
            dve.tensor_tensor(both_bias[:, :], gb["eenc"][:, 1, :], gb["eblk_0"][:, 1, :], ALU.add).then_inc(wchain, 1)
            dve.wait_ge(multiplied, 1)
            dve.tensor_copy(col_state[:, :], ps_setup[:, 0:1]).then_inc(wchain, 1)
            n = 0
            for k in row3:
                lo, hi = parts[k], parts16[k]
                for part in range(3):
                    frm = row[k][:, :] if part == 0 else lo[:, part - 1, :]
                    dve.tensor_copy(hi[:, part, :], frm).then_inc(split, 1)
                    n += 1
                    dve.wait_ge(split, n)
                    if part < 2:
                        dve.tensor_tensor(lo[:, part, :], frm, hi[:, part, :], ALU.subtract).then_inc(split, 1)
                        n += 1
                        dve.wait_ge(split, n)
            dve.tensor_copy(first_target[:, :], targets[:, :, 0]).then_inc(ordered, 1)
            dve.tensor_reduce(extent[:, 0, :], targets[:, :, :], axis=AX.X, op=ALU.max).then_inc(ordered, 1)
            dve.tensor_reduce(extent[:, 1, :], targets[:, :, :], axis=AX.X, op=ALU.min).then_inc(ordered, 1)
            dve.wait_ge(ordered, 3)
            dve.tensor_tensor(extent[:, 2, :], extent[:, 0, :], first_target[:, :], ALU.subtract).then_inc(ordered, 1)
            dve.tensor_tensor(extent[:, 3, :], first_target[:, :], extent[:, 1, :], ALU.subtract).then_inc(ordered, 1)
            dve.wait_ge(ordered, 5)
            dve.tensor_scalar(extent[:, 2, :], extent[:, 2, :], float(1 - WIN), 0.0, ALU.add, ALU.max).then_inc(ordered, 1)
            dve.tensor_scalar(extent[:, 3, :], extent[:, 3, :], 0.0, None, ALU.max).then_inc(ordered, 1)
            dve.wait_ge(ordered, 7)
            dve.tensor_reduce(outside[:, :], extent[:, 2:4, :], axis=AX.XY, op=ALU.max).then_inc(ordered, 1)
            dve.wait_ge(multiplied, 2)
            dve.tensor_scalar(disorder[:, :], ps_setup[0:1, 2:3], 1.0, None, ALU.min).then_inc(ordered, 1)
            dve.wait_ge(ordered, 9)

        @block.tensor
        def _(pe):
            pe.wait_ge(weights, 16 * n_loads[0])
            pe.wait_ge(wchain, 5)
            pe.matmul(ps_setup[:, 0:1], W["eblk_e0"][:, :], bias_col[:, :], start=True, stop=True).then_inc(multiplied, 1)
            pe.wait_ge(consts, 14)
            pe.wait_ge(ordered, 8)
            pe.wait_ge(wchain, 8)
            pe.matmul(ps_setup[0:1, 2:3], outside[:, :], ones_col[0:DP, :], start=True, stop=True).then_inc(multiplied, 1)

    def norm_stats(dve, chain, p, i, squares, width, n, v):
        dve.wait_ge(chain.sem, chain.at(f"{p}_square", i))
        dve.tensor_reduce(v[:, 1, 0:n], squares, axis=AX.X, op=ALU.add).then_inc(chain.sem, 1)
        dve.wait_ge(chain.sem, chain.at(f"{p}_var", i))
        dve.tensor_scalar(v[:, 1, 0:n], v[:, 1, 0:n], 1.0 / width, EPS, ALU.mult, ALU.add).then_inc(chain.sem, 1)
        newton(dve, chain, p, i, v[:, 1, 0:n], v[:, 0, 0:n], v[:, 2, 0:n])

    def newton(dve, chain, p, i, value, out_, t):
        names = rsqrt_names(p)

        dve.wait_ge(chain.sem, chain.at(names[0], i))
        dve.tensor_scalar(t.bitcast(I32), value.bitcast(I32), 1, None, ALU.logical_shift_right).then_inc(chain.sem, 1)
        dve.wait_ge(chain.sem, chain.at(names[1], i))
        dve.tensor_scalar(out_.bitcast(I32), t.bitcast(I32), -1.0, float(0x5F3759DF), ALU.mult, ALU.add).then_inc(chain.sem, 1)
        for r in range(3):
            dve.wait_ge(chain.sem, chain.at(names[2 + 3 * r], i))
            dve.scalar_tensor_tensor(out=t, in0=out_, scalar=-0.5, in1=value, op0=ALU.mult, op1=ALU.mult).then_inc(chain.sem, 1)
            dve.wait_ge(chain.sem, chain.at(names[3 + 3 * r], i))
            dve.tensor_tensor(t, t, out_, ALU.mult).then_inc(chain.sem, 1)
            dve.wait_ge(chain.sem, chain.at(names[4 + 3 * r], i))
            dve.scalar_tensor_tensor(out=out_, in0=t, scalar=1.5, in1=out_, op0=ALU.add, op1=ALU.mult).then_inc(chain.sem, 1)

    def edge_rows(ap):
        return ap.rearrange("(u p s) k -> u p (s k)", p=P, s=S)

    def node_rows(ap):
        return ap[0:N, :].rearrange("(u p c) k -> u p (c k)", p=P, c=C)

    attr_u = edge_rows(ins["edge_attr_8"])
    src_u = edge_rows(ins["src"].unsqueeze(1))
    dst_u = edge_rows(ins["dst"].unsqueeze(1))
    weight_u = edge_rows(ins["edge_weight"].unsqueeze(1))

    DUO = 2 * P * S
    DUOS = UNITS // 2
    src_d = ins["src"].rearrange("(d h p s) -> d p h s", h=2, p=P, s=S)
    dst_d = ins["dst"].rearrange("(d h p s) -> d p h s", h=2, p=P, s=S)
    weight_d = ins["edge_weight"].rearrange("(d h p s) -> d p h s", h=2, p=P, s=S)
    attr_d = ins["edge_attr_8"].rearrange("(d h p s) k -> d p h (s k)", h=2, p=P, s=S)
    edge_t_d = edge_t.rearrange("(d h) p n -> d p h n", h=2)
    dst_duo = ins["dst"].rearrange("(d e) -> d e", e=DUO)

    def windowed_pass(st, name, tables, width, agg, kind, gathered, into):
        conv = kind == "conv"
        steps = ["product", "summed", "weight"] if conv else ["product"]
        q = [Chain(half_chain[h], base(half_chain[h]), steps) for h in range(2)]
        g = Chain(merge_chain, base(merge_chain), ["merged", "merged_out"])
        w = Chain(window_chain, base(window_chain), ["row", "pick0", "pick1"])
        b_loaded = [base(x) for x in duo_loaded]
        b_added = base(duo_added)
        n_loads = 4 + conv

        def tiles(k, shape, dt=F32, n=2):
            return [sb(f"{name}_w_{k}{x}", shape, dt, st) for x in range(n)]

        Jsrc, Jdst = tiles("src", [P, 2, S], I32), tiles("dst", [P, 2, S], I32)
        first = tiles("first", [2 * D, 1], I32)
        G = tiles("g", [P, S, tables[0][1]], F32, 4)
        attr = tiles("attr", [P, 2, S * A]) if conv else None
        wt = tiles("wt", [P, 2, S])
        row_ids = tiles("row_ids", [P, WIN])
        pick = tiles("pick", [P, S, WIN], F32, 4)
        merged = tiles("merged", [WIN, width])
        V = tiles("v", [P, S, width], F32, 4)
        prod = tiles("prod", [P, S * A, F]) if conv else None

        for h in range(2):
            advance(half_chain[h], q[h].n * DUOS)
        advance(merge_chain, 2 * DUOS)
        advance(window_chain, w.n * DUOS)
        advance(duo_added, 16 * DUOS)
        for x in range(2):
            advance(duo_loaded[x], 16 * n_loads * (DUOS // 2 + 1 - x))

        def by_parity(d, x, each, b):
            if isinstance(d, int):
                return (d // 2 + 1) * each + b
            return (d - x) * (each // 2) + (each + b)

        def loads_of(d, x):
            return by_parity(d, x, 16 * n_loads, b_loaded[x])

        def gathers_of(d, x):
            return by_parity(d, x, 16 * S, 0)

        def adds_to(d):
            return d * 16 + b_added

        def sync(sp):
            def body(d, x, before, last):
                if before >= 2:
                    for h in range(2):
                        sp.wait_ge(q[h].sem, q[h].end(d - 2))
                        sp.sem_inc(sp_tick, 1)
                u = bass.ds(d, 1)
                sp.dma_start(Jsrc[x][:, :, :], src_d[u].squeeze(0)).then_inc(duo_loaded[x], 16)
                sp.dma_start(Jdst[x][:, :, :], dst_d[u].squeeze(0)).then_inc(duo_loaded[x], 16)
                sp.dma_start(first[x][:, :], dst_duo[u, 0:1].broadcast_to([2 * D, 1])).then_inc(duo_loaded[x], 16)
                sp.dma_start(wt[x][:, :, :], weight_d[u].squeeze(0)).then_inc(duo_loaded[x], 16)
                if conv:
                    sp.dma_start(attr[x][:, :, :], attr_d[u].squeeze(0)).then_inc(duo_loaded[x], 16)

            in_duos(sp, DUOS, body)

        def gpsimd(pool):
            def gathers(d, x, before):
                pool.wait_ge(duo_loaded[x], loads_of(d, x))
                pool.sem_inc(pool_tick, 1)
                for h in range(2):
                    if before >= 2:
                        pool.wait_ge(q[h].sem, q[h].at("product", d - 2))
                        pool.sem_inc(pool_tick, 1)
                    for t in range(S):
                        pool.indirect_dma_start(
                            G[2 * x + h][:, t, :], None, tables[0][0],
                            bass.IndirectOffsetOnAxis(ap=Jsrc[x][:, h, t:t + 1], axis=0),
                        ).then_inc(gathered[2 * x + h], 16)

            def body(d, x, before, last):
                if not last:
                    gathers(d + 1, 1 - x, before + 1)
                pool.wait_ge(g.sem, g.at("merged_out", d))
                pool.sem_inc(pool_tick, 1)
                if before:
                    pool.wait_ge(duo_added, adds_to(d))
                    pool.sem_inc(pool_tick, 1)
                at = pool.value_load(dst_duo[bass.ds(d, 1), 0:1], min_val=0, max_val=N - 1)
                pool.dma_start(agg[bass.ds(at, WIN), :], merged[x][:, :], accum_op=ALU.add).then_inc(duo_added, 16)

            gathers(0, 0, 0)
            in_duos(pool, DUOS, body, ahead=True)
            pool.wait_ge(duo_added, adds_to(DUOS))

        def vector(dve):
            def body(d, x, before, last):
                dve.wait_ge(duo_loaded[x], loads_of(d, x))
                if before:
                    dve.wait_ge(w.sem, w.end(d - 1))
                dve.tensor_tensor(row_ids[x][:, :], iota_row[:, :], first[x][0:P, :].broadcast_to([P, WIN]), ALU.add).then_inc(w.sem, 1)
                dve.wait_ge(w.sem, w.at("row", d))
                if before >= 2:
                    dve.wait_ge(g.sem, g.at("merged", d - 2))
                for h in range(2):
                    dve.tensor_tensor(pick[2 * x + h][:, :, :], bc3(Jdst[x][:, h, :], [P, S, WIN]),
                                      row_ids[x][:, :].unsqueeze(1).broadcast_to([P, S, WIN]), ALU.is_equal).then_inc(w.sem, 1)
                dve.wait_ge(w.sem, w.end(d))
                for h in range(2):
                    k = 2 * x + h
                    dve.wait_ge(gathered[k], gathers_of(d, x))
                    if conv:
                        if before:
                            dve.wait_ge(q[h].sem, q[h].end(d - 1))
                        dve.tensor_tensor(prod[h][:, :, :], G[k][:, :, :].rearrange("p s (a f) -> p (s a) f", f=F),
                                          bc3(attr[x][:, h, :], [P, S * A, F]), ALU.mult).then_inc(q[h].sem, 1)
                    else:
                        dve.tensor_tensor(V[k][:, :, :], G[k][:, :, :], bc3(wt[x][:, h, :], [P, S, F]),
                                          ALU.mult).then_inc(q[h].sem, 1)
                if conv:
                    for h in range(2):
                        dve.wait_ge(q[h].sem, q[h].at("product", d))
                        dve.tensor_reduce(V[2 * x + h][:, :, 0:F], prod[h][:, :, :].rearrange("p (s a) f -> p s f a", a=A),
                                          axis=AX.X, op=ALU.add).then_inc(q[h].sem, 1)
                    for h in range(2):
                        dve.wait_ge(q[h].sem, q[h].at("summed", d))
                        dve.tensor_copy(V[2 * x + h][:, :, F:F + 1], wt[x][:, h, :].unsqueeze(2)).then_inc(q[h].sem, 1)

            in_duos(dve, DUOS, body)

        def scalar(act):
            def body(d, x, before, last):
                act.wait_ge(g.sem, g.at("merged", d))
                if before >= 2:
                    act.wait_ge(duo_added, adds_to(d - 1))
                act.activation(merged[x][:, :], into[0:WIN, 0:width], ACT.Copy).then_inc(g.sem, 1)

            in_duos(act, DUOS, body)

        def tensor(pe):
            def body(d, x, before, last):
                pe.wait_ge(w.sem, w.at("pick1", d))
                if before:
                    pe.wait_ge(g.sem, g.end(d - 1))
                for h in range(2):
                    pe.wait_ge(q[h].sem, q[h].end(d))
                    for t in range(S):
                        mm = pe.matmul(into[0:WIN, 0:width], pick[2 * x + h][:, t, :], V[2 * x + h][:, t, :],
                                       start=h == 0 and t == 0, stop=h == 1 and t == S - 1)
                mm.then_inc(g.sem, 1)

            in_duos(pe, DUOS, body)

        return dict(sync=sync, gpsimd=gpsimd, vector=vector, scalar=scalar, tensor=tensor)

    def windowed_mlp(st, name, tables, agg, rnd, gathered, banks):
        enc = rnd == 0
        update = ["hidden1", "act1", "out1", "upd_square"]
        rest = ["upd_var", "upd_norm", "upd_gain", "values"]
        if enc:
            front_steps = ["attr_turned", "attr_t", "hidden0", "act0", "out0", "enc_square", "enc_var", "enc_norm",
                           "state_turned", "state_t"]
            back_steps = update + rest + ["next_turned", "next_t"]
        else:
            front_steps, back_steps = update, rest
        a = [Chain(half_chain[h], base(half_chain[h]), front_steps) for h in range(2)]
        b = [Chain(back_chain[h], base(back_chain[h]), back_steps) for h in range(2)]
        up = b if enc else a
        w = Chain(window_chain, base(window_chain), ["row", "pick0", "pick1", "col", "spread0", "spread1"])
        r = Chain(stat_chain, base(stat_chain), rsqrt_names("dev"))
        f = [Chain(full_chain[h], base(full_chain[h]), ["full_gain", "full_bias"]) for h in range(2)]
        g = Chain(merge_chain, base(merge_chain), ["merged", "merged_out"])
        b_loaded = [base(x) for x in duo_loaded]
        b_stored = [base(x) for x in duo_stored]
        b_added = base(duo_added)
        n_loads = 7

        def tiles(k, shape, dt=F32, n=2):
            return [sb(f"{name}_w_{k}{x}", shape, dt, st) for x in range(n)]

        Jsrc, Jdst = tiles("src", [P, 2, S], I32), tiles("dst", [P, 2, S], I32)
        first = tiles("first", [2 * D, 1], I32)
        G = tiles("g", [P, S, D], F32, 4)
        row_ids, col_ids = tiles("row_ids", [P, WIN]), tiles("col_ids", [2 * D, 1])
        trow = tiles("row", [2 * D, DUO], I32)
        pick = tiles("pick", [P, S, WIN], F32, 4)
        spread = tiles("spread", [2 * D, PAIRS, P], F32, 4)
        window = tiles("window", [2 * D, 2 * D])
        merged = tiles("merged", [WIN, D])
        act1 = tiles("act1", [2 * D, PAIRS * P])
        sq1 = tiles("sq1", [P, S, D], F32, 4)
        stat = tiles("stat", [P, 3, 4 * S], F32, 1)[0]
        V = tiles("v", [P, S, D], F32, 4)
        if enc:
            attr = tiles("attr", [P, 2, S * A])
            attr_t, act0 = tiles("attr_t", [S * A, P]), tiles("act0", [2 * D, PAIRS * P])
            sq0, unit, change = tiles("sq0", [P, S, D]), tiles("unit", [P, S, D]), tiles("change", [P, S, D])
            state_t, next_t = tiles("state_t", [2 * D, PAIRS * P]), tiles("next_t", [2 * D, PAIRS * P])
            O0, H0, H1, O1 = banks[0:2], banks[2:4], banks[4:6], banks[6:8]
            into = O1[0]
        else:
            state2 = tiles("state", [2 * D, 2, PAIRS * P])
            H1, O4, into = banks[0:2], banks[2:6], banks[6]

        for h in range(2):
            advance(half_chain[h], a[h].n * DUOS)
            advance(back_chain[h], b[h].n * DUOS)
            if enc:
                advance(full_chain[h], 2 * DUOS)
                advance(duo_stored[h], 16 * DUOS)
        advance(window_chain, w.n * DUOS)
        advance(merge_chain, 2 * DUOS)
        advance(duo_added, 16 * DUOS)
        advance(stat_chain, r.n * (DUOS + 1))
        for x in range(2):
            advance(duo_loaded[x], 16 * n_loads * (DUOS // 2 + 1 - x))

        def by_parity(d, x, each, start):
            if isinstance(d, int):
                return (d // 2 + 1) * each + start
            return (d - x) * (each // 2) + (each + start)

        def loads_of(d, x):
            return by_parity(d, x, 16 * n_loads, b_loaded[x])

        def gathers_of(d, x):
            return by_parity(d, x, 16 * S, 0)

        def adds_to(d):
            return d * 16 + b_added

        def three(bank):
            return bank[0:P, 0:S * D].rearrange("p (s d) -> p s d", d=D)

        def out1_bank(x, h):
            return O1[h] if enc else O4[2 * x + h]

        def sync(sp):
            sp.wait_ge(cleared_windows[name], 2)

            def body(d, x, before, last):
                if before >= 2:
                    for h in range(2):
                        sp.wait_ge(up[h].sem, up[h].at("hidden1", d - 2))
                        sp.sem_inc(sp_tick, 1)
                u = bass.ds(d, 1)
                if enc:
                    sp.dma_start(attr[x][:, :, :], attr_d[u].squeeze(0)).then_inc(duo_loaded[x], 16)
                else:
                    sp.dma_start(state2[x][:, :, :], edge_t_d[u].squeeze(0)).then_inc(duo_loaded[x], 16)
                sp.dma_start(first[x][:, :], dst_duo[u, 0:1].broadcast_to([2 * D, 1])).then_inc(duo_loaded[x], 16)
                sp.dma_start(Jsrc[x][:, :, :], src_d[u].squeeze(0)).then_inc(duo_loaded[x], 16)
                sp.dma_start(Jdst[x][:, :, :], dst_d[u].squeeze(0)).then_inc(duo_loaded[x], 16)
                sp.dma_start(trow[x][:, :], dst_duo[u, :].broadcast_to([2 * D, DUO])).then_inc(duo_loaded[x], 16)
                at = sp.value_load(dst_duo[u, 0:1], min_val=0, max_val=N - 1)
                for h in range(2):
                    sp.dma_start(window[x][h * D:h * D + WIN, h * D:(h + 1) * D], tables[1][0][bass.ds(at, WIN), :])\
                      .then_inc(duo_loaded[x], 16)

            in_duos(sp, DUOS, body)

        def gpsimd(pool):
            def gathers(d, x, before):
                pool.wait_ge(duo_loaded[x], loads_of(d, x))
                pool.sem_inc(pool_tick, 1)
                for h in range(2):
                    if before >= 2:
                        pool.wait_ge(up[h].sem, up[h].at("hidden1", d - 2))
                        pool.sem_inc(pool_tick, 1)
                    for t in range(S):
                        pool.indirect_dma_start(
                            G[2 * x + h][:, t, :], None, tables[0][0],
                            bass.IndirectOffsetOnAxis(ap=Jsrc[x][:, h, t:t + 1], axis=0),
                        ).then_inc(gathered[2 * x + h], 16)

            def add(d, x, before):
                pool.wait_ge(g.sem, g.at("merged_out", d))
                pool.sem_inc(pool_tick, 1)
                if before:
                    pool.wait_ge(duo_added, adds_to(d))
                    pool.sem_inc(pool_tick, 1)
                at = pool.value_load(dst_duo[bass.ds(d, 1), 0:1], min_val=0, max_val=N - 1)
                pool.dma_start(agg[bass.ds(at, WIN), :], merged[x][:, :], accum_op=ALU.add).then_inc(duo_added, 16)

            def body(d, x, before, last):
                if not last:
                    gathers(d + 1, 1 - x, before + 1)
                if before:
                    add(d - 1, 1 - x, before - 1)

            gathers(0, 0, 0)
            in_duos(pool, DUOS, body, ahead=True)
            add(DUOS - 1, 0, 2)
            pool.wait_ge(duo_added, adds_to(DUOS))

        def vector(dve):
            for x in range(2):
                dve.memset(window[x][:, :], 0.0).then_inc(cleared_windows[name], 1)
            dve.memset(stat[:, :, :], 1.0).then_inc(cleared_windows[name], 1)
            dve.wait_ge(cleared_windows[name], 3)

            def body(d, x, before, last, front=True):
                y = 1 - x
                if front:
                    dve.wait_ge(duo_loaded[x], loads_of(d, x))
                    if before:
                        dve.wait_ge(w.sem, w.end(d - 1))
                    dve.tensor_tensor(row_ids[x][:, :], iota_row[:, :], first[x][0:P, :].broadcast_to([P, WIN]), ALU.add).then_inc(w.sem, 1)
                    dve.wait_ge(w.sem, w.at("row", d))
                    if before >= 2:
                        dve.wait_ge(g.sem, g.at("merged", d - 2))
                    for h in range(2):
                        dve.tensor_tensor(pick[2 * x + h][:, :, :], bc3(Jdst[x][:, h, :], [P, S, WIN]),
                                          row_ids[x][:, :].unsqueeze(1).broadcast_to([P, S, WIN]), ALU.is_equal).then_inc(w.sem, 1)
                    dve.tensor_tensor(col_ids[x][:, :], iota_col[:, :], first[x][:, :], ALU.add).then_inc(w.sem, 1)
                    dve.wait_ge(w.sem, w.at("col", d))
                    for h in range(2):
                        targets_ = trow[x][:, h * P * S:(h + 1) * P * S].rearrange("p (q k two) -> p two k q", two=2, k=PAIRS)
                        if before >= 2:
                            dve.wait_ge(up[h].sem, up[h].at("hidden1", d - 2))
                        dve.tensor_scalar(spread[2 * x + h][0:D, :, :], targets_[0:D, 0], col_ids[x][0:D, :], None, ALU.is_equal)
                        dve.tensor_scalar(spread[2 * x + h][D:2 * D, :, :], targets_[D:2 * D, 1], col_ids[x][D:2 * D, :], None,
                                          ALU.is_equal).then_inc(w.sem, 1)
                if enc and before:
                    for h in range(2):
                        dve.wait_ge(a[h].sem, a[h].at("enc_norm", d - 1))
                if before >= 2:
                    for h in range(2):
                        dve.wait_ge(b[h].sem, b[h].at("upd_norm", d - 2))
                if before:
                    for h in range(2):
                        dve.wait_ge(up[h].sem, up[h].at("upd_square", d - 1))
                        dve.tensor_reduce(stat[:, 1, (2 + h) * S:(3 + h) * S], sq1[2 * y + h][:, :, :], axis=AX.X, op=ALU.add).then_inc(b[h].sem, 1)
                if enc and front:
                    for h in range(2):
                        dve.wait_ge(a[h].sem, a[h].at("enc_square", d))
                        dve.tensor_reduce(stat[:, 1, h * S:(h + 1) * S], sq0[h][:, :, :], axis=AX.X, op=ALU.add).then_inc(a[h].sem, 1)
                    for h in range(2):
                        dve.wait_ge(a[h].sem, a[h].at("enc_var", d))
                if before:
                    for h in range(2):
                        dve.wait_ge(b[h].sem, b[h].at("upd_var", d - 1))
                if before:
                    dve.wait_ge(r.sem, r.end(d - 1))
                dve.tensor_scalar(stat[:, 1, :], stat[:, 1, :], 1.0 / D, EPS, ALU.mult, ALU.add).then_inc(r.sem, 1)
                newton(dve, r, "dev", d, stat[:, 1, :], stat[:, 0, :], stat[:, 2, :])
                dve.wait_ge(r.sem, r.end(d))
                if enc and front:
                    for h in range(2):
                        if before:
                            dve.wait_ge(f[h].sem, f[h].at("full_gain", d - 1))
                        dve.tensor_tensor(unit[h][:, :, :], three(O0[h]), bc3(stat[:, 0, h * S:(h + 1) * S], [P, S, D]),
                                          ALU.mult).then_inc(a[h].sem, 1)
                if before:
                    to = change if enc else [V[0], V[1]]
                    if not enc and before >= 2:
                        dve.wait_ge(g.sem, g.at("merged", d - 2))
                    for h in range(2):
                        dve.tensor_tensor(to[h][:, :, :], three(out1_bank(y, h)), bc3(stat[:, 0, (2 + h) * S:(3 + h) * S], [P, S, D]),
                                          ALU.mult).then_inc(b[h].sem, 1)
                    for h in range(2):
                        dve.wait_ge(b[h].sem, b[h].at("upd_norm", d - 1))
                        dve.tensor_tensor(to[h][:, :, :], to[h][:, :, :],
                                          gb[f"eblk_{rnd}"][:, 0, :].unsqueeze(1).broadcast_to([P, S, D]), ALU.mult).then_inc(b[h].sem, 1)
                    for h in range(2):
                        dve.wait_ge(b[h].sem, b[h].at("upd_gain", d - 1))
                        if enc:
                            dve.wait_ge(f[h].sem, f[h].at("full_bias", d - 1))
                            dve.tensor_tensor(V[2 * y + h][:, :, :], V[2 * y + h][:, :, :], to[h][:, :, :], ALU.add).then_inc(b[h].sem, 1)
                        else:
                            dve.tensor_tensor(to[h][:, :, :], to[h][:, :, :],
                                              gb[f"eblk_{rnd}"][:, 1, :].unsqueeze(1).broadcast_to([P, S, D]), ALU.add).then_inc(b[h].sem, 1)
                if enc and front:
                    if before >= 2:
                        dve.wait_ge(g.sem, g.at("merged", d - 2))
                    for h in range(2):
                        dve.wait_ge(a[h].sem, a[h].at("enc_norm", d))
                        dve.tensor_tensor(V[2 * x + h][:, :, :], unit[h][:, :, :],
                                          gb["eenc"][:, 0, :].unsqueeze(1).broadcast_to([P, S, D]), ALU.mult).then_inc(f[h].sem, 1)
                    for h in range(2):
                        dve.wait_ge(f[h].sem, f[h].at("full_gain", d))
                        dve.tensor_tensor(V[2 * x + h][:, :, :], V[2 * x + h][:, :, :],
                                          both_bias[:, :].unsqueeze(1).broadcast_to([P, S, D]), ALU.add).then_inc(f[h].sem, 1)

            in_duos(dve, DUOS, body)
            body(DUOS, 1, 2, True, front=False)

        def scalar(act):
            def body(d, x, before, last, front=True):
                y = 1 - x
                if enc and front:
                    for h in range(2):
                        act.wait_ge(a[h].sem, a[h].at("attr_turned", d))
                        act.activation(attr_t[h][:, :], O0[h][0:S * A, 0:P], ACT.Copy).then_inc(a[h].sem, 1)
                if enc and before or not enc and front:
                    for h in range(2):
                        act.wait_ge(up[h].sem, up[h].at("hidden1", d - 1 if enc else d))
                        act.activation(act1[h][:, :], H1[h][:, 0:PAIRS * P], ACT.Silu,
                                       bias=col_state[:, :] if enc else 0.0).then_inc(up[h].sem, 1)
                if enc and front:
                    for h in range(2):
                        act.wait_ge(a[h].sem, a[h].at("hidden0", d))
                        act.activation(act0[h][:, :], H0[h][:, 0:PAIRS * P], ACT.Silu, bias=col["eenc0"][:, :]).then_inc(a[h].sem, 1)
                if enc and before:
                    for h in range(2):
                        act.wait_ge(b[h].sem, b[h].at("out1", d - 1))
                        act.activation(sq1[2 * y + h][:, :, :], three(O1[h]), ACT.Square).then_inc(b[h].sem, 1)
                if not enc and front:
                    for h in range(2):
                        act.wait_ge(a[h].sem, a[h].at("out1", d))
                        if before >= 2:
                            act.wait_ge(b[h].sem, b[h].at("upd_var", d - 2))
                        act.activation(sq1[2 * x + h][:, :, :], three(O4[2 * x + h]), ACT.Square).then_inc(a[h].sem, 1)
                if enc and front:
                    for h in range(2):
                        act.wait_ge(a[h].sem, a[h].at("out0", d))
                        act.activation(sq0[h][:, :, :], three(O0[h]), ACT.Square).then_inc(a[h].sem, 1)
                    for h in range(2):
                        act.wait_ge(a[h].sem, a[h].at("state_turned", d))
                        act.activation(state_t[h][:, :], H0[h][:, 0:PAIRS * P], ACT.Copy).then_inc(a[h].sem, 1)
                if enc and before:
                    for h in range(2):
                        act.wait_ge(b[h].sem, b[h].at("next_turned", d - 1))
                        if before >= 2:
                            act.wait_ge(duo_stored[h], (d - 1) * 16 + b_stored[h])
                        act.activation(next_t[h][:, :], H1[h][:, 0:PAIRS * P], ACT.Copy).then_inc(b[h].sem, 1)
                    for h in range(2):
                        act.wait_ge(b[h].sem, b[h].at("next_t", d - 1))
                        act.dma_start(edge_t[bass.ds(d * 2 - 2 + h, 1), :, :].squeeze(0), next_t[h][:, :]).then_inc(duo_stored[h], 16)
                if before:
                    act.wait_ge(g.sem, g.at("merged", d - 1))
                    if before >= 2:
                        act.wait_ge(duo_added, adds_to(d - 2))
                    act.activation(merged[y][:, :], into[0:WIN, 0:D], ACT.Copy).then_inc(g.sem, 1)

            in_duos(act, DUOS, body)
            body(DUOS, 1, 2, True, front=False)
            if enc:
                for h in range(2):
                    act.wait_ge(duo_stored[h], 16 * DUOS + b_stored[h])

        def tensor(pe):
            def hidden1(d, x, before):
                for h in range(2):
                    k4 = 2 * x + h
                    if before:
                        pe.wait_ge(up[h].sem, up[h].end(d - 1))
                    if enc:
                        pe.wait_ge(a[h].sem, a[h].at("state_t", d))
                        pe.matmul(H1[h][:, 0:PAIRS * P], w_state[:, :], state_t[h][:, :], start=True, stop=False)
                    else:
                        pe.wait_ge(duo_loaded[x], loads_of(d, x))
                        pe.matmul(H1[h][:, 0:PAIRS * P], W[f"eblk_e{rnd}"][:, :], state2[x][:, h, :], start=True, stop=False)
                    pe.wait_ge(gathered[k4], gathers_of(d, x))
                    pe.wait_ge(w.sem, w.at(f"spread{h}", d))
                    for k in range(PAIRS):
                        pe.matmul(H1[h][:, k * P:(k + 1) * P], flat2(G[k4][:, 2 * k:2 * k + 2, :]), ident[:, :],
                                  start=False, stop=False)
                    pe.matmul(H1[h][:, 0:PAIRS * P], window[x][:, :], spread[k4][:, :, :].rearrange("p k q -> p (k q)"),
                              start=False, stop=True).then_inc(up[h].sem, 1)

            def out1(d, x, before):
                for h in range(2):
                    pe.wait_ge(up[h].sem, up[h].at("act1", d))
                    if enc and before and h == 0:
                        pe.wait_ge(g.sem, g.end(d - 1))
                    o = out1_bank(x, h)
                    pe.matmul(o[0:P, 0:S * D], ones3[:, :], row3[f"eblk1_{rnd}"][:, :], start=True, stop=False)
                    for k in range(PAIRS):
                        mm = pe.matmul(o[0:P, k * 2 * D:(k + 1) * 2 * D], act1[h][:, k * P:(k + 1) * P],
                                       W[f"eblk1{rnd}"][:, :], start=False, stop=k == PAIRS - 1)
                    mm.then_inc(up[h].sem, 1)

            def body(d, x, before, last, front=True):
                y = 1 - x
                if enc and front:
                    for h in range(2):
                        pe.wait_ge(duo_loaded[x], loads_of(d, x))
                        if before:
                            pe.wait_ge(a[h].sem, a[h].end(d - 1))
                        pe.matmul(O0[h][0:S * A, 0:P], attr[x][:, h, :], ident[:, :], start=True, stop=True).then_inc(a[h].sem, 1)
                if enc and before:
                    hidden1(d - 1, y, before - 1)
                if not enc and front:
                    hidden1(d, x, before)
                if enc and front:
                    for h in range(2):
                        pe.wait_ge(a[h].sem, a[h].at("attr_t", d))
                        for k in range(PAIRS):
                            mm = pe.matmul(H0[h][:, k * P:(k + 1) * P], w_eenc0[:, k * 2 * D:(k + 1) * 2 * D],
                                           attr_t[h][:, :], start=True, stop=True)
                        mm.then_inc(a[h].sem, 1)
                if enc and before:
                    out1(d - 1, y, before - 1)
                if not enc and front:
                    out1(d, x, before)
                if enc and front:
                    for h in range(2):
                        pe.wait_ge(a[h].sem, a[h].at("act0", d))
                        pe.matmul(O0[h][0:P, 0:S * D], ones3[:, :], row3["eenc1"][:, :], start=True, stop=False)
                        for k in range(PAIRS):
                            mm = pe.matmul(O0[h][0:P, k * 2 * D:(k + 1) * 2 * D], act0[h][:, k * P:(k + 1) * P],
                                           W["eenc1"][:, :], start=False, stop=k == PAIRS - 1)
                        mm.then_inc(a[h].sem, 1)
                    for h in range(2):
                        pe.wait_ge(a[h].sem, a[h].at("enc_norm", d))
                        for k in range(PAIRS):
                            mm = pe.matmul(H0[h][:, k * P:(k + 1) * P], flat2(unit[h][:, 2 * k:2 * k + 2, :]), ident[:, :],
                                           start=True, stop=True)
                        mm.then_inc(a[h].sem, 1)
                if before:
                    v = [V[2 * y + h] if enc else V[h] for h in range(2)]
                    if enc:
                        for h in range(2):
                            pe.wait_ge(b[h].sem, b[h].at("values", d - 1))
                            for k in range(PAIRS):
                                mm = pe.matmul(H1[h][:, k * P:(k + 1) * P], flat2(v[h][:, 2 * k:2 * k + 2, :]), ident[:, :],
                                               start=True, stop=True)
                            mm.then_inc(b[h].sem, 1)
                    if before >= 2:
                        pe.wait_ge(g.sem, g.end(d - 2))
                    for h in range(2):
                        pe.wait_ge(b[h].sem, b[h].at("values", d - 1))
                        for t in range(S):
                            mm = pe.matmul(into[0:WIN, 0:D], pick[2 * y + h][:, t, :], v[h][:, t, :],
                                           start=h == 0 and t == 0, stop=h == 1 and t == S - 1)
                    mm.then_inc(g.sem, 1)

            in_duos(pe, DUOS, body)
            body(DUOS, 1, 2, True, front=False)

        return dict(sync=sync, gpsimd=gpsimd, vector=vector, scalar=scalar, tensor=tensor)

    def flat2(ap):
        return ap.rearrange("p a b -> p (a b)")

    cleared_windows = {"e2": sem("cleared_windows0"), "e3": sem("cleared_windows1")}

    def edge_pass(name, tables, target, width, agg, kind, rnd=0):
        table_widths = [w for _, w, _ in tables]
        ends = {"src": src_u, "dst": dst_u}
        used = sorted({e for _, _, e in tables} | {target})
        mlp = kind in ("mlp0", "mlp1")
        takes_attr = kind in ("message", "conv", "mlp0")
        takes_weight = kind in ("conv", "gcn")
        from_table = "attr" if takes_attr else None

        dedup_steps = ["equal", "masked", "repeated", "to_spare", "if_repeated", "index"]
        if kind in ("message", "conv"):
            steps = ["product", "summed"] + (["silu"] if kind == "message" else ["weight"])
        elif kind == "gcn":
            steps = ["product"]
        else:
            steps = []
            if kind == "mlp0":
                steps += ["attr_turned", "attr_t", "hidden0", "act0", "out0"] + ln_names("enc", True) + \
                         ["enc_gain", "enc_bias", "state_turned", "state_t"]
            steps += ["hidden1", "act1", "out1"] + ln_names("upd", True) + ["upd_gain", "upd_bias"]
            if kind == "mlp0":
                steps += ["state_added", "next_turned", "next_t"]
        steps += ["merged", "merged_out"]

        with ExitStack() as st:
            J = {e: [sb(f"{name}_{e}{h}", [P, S], I32, st) for h in range(2)] for e in used}
            B = [sb(f"{name}_row{h}", [P, P * S], I32, st) for h in range(2)]
            G = [[sb(f"{name}_g{n}{h}", [P, S, w], F32, st) for h in range(2)] for n, w in enumerate(table_widths)]
            attr = [sb(f"{name}_attr{h}", [P, S * A], F32, st) for h in range(2)] if takes_attr else None
            wt = [sb(f"{name}_wt{h}", [P, S], F32, st) for h in range(2)] if takes_weight else None
            same = [sb(f"{name}_same{h}", [P, S, P], F32, st) for h in range(2)]
            masked = sb(f"{name}_masked", [P, S, P], F32, st)
            rep = sb(f"{name}_rep", [P, S], F32, st)
            alt = sb(f"{name}_alt", [P, S], F32, st)
            index = [sb(f"{name}_index{h}", [P, S], I32, st) for h in range(2)]
            V = [sb(f"{name}_v{h}", [P, S, width], F32, st) for h in range(2)]
            SV = [sb(f"{name}_sv{h}", [P, S, width], F32, st) for h in range(2)]
            if takes_attr and not mlp:
                prod = sb(f"{name}_prod", [P, S * A, F], F32, st)
                summed = sb(f"{name}_summed", [P, S, F], F32, st)
            if mlp:
                attr_t = sb(f"{name}_attr_t", [S * A, P], F32, st)
                act0 = sb(f"{name}_act0", [2 * D, PAIRS * P], F32, st)
                act1 = sb(f"{name}_act1", [2 * D, PAIRS * P], F32, st)
                squares = sb(f"{name}_squares", [P, S, D], F32, st)
                stat = sb(f"{name}_stat", [P, 3, 8], F32, st)
                state = sb(f"{name}_state", [P, S, D], F32, st)
                state_t = [sb(f"{name}_state_t{h}", [2 * D, PAIRS * P], F32, st) for h in range(2)]
                next_t = [sb(f"{name}_next_t{h}", [2 * D, PAIRS * P], F32, st) for h in range(2)]

            def ps(k):
                return st.enter_context(nc.psum_tensor(f"{name}_ps_{k}", [2 * D, 512], F32))

            ps_merged = ps("merged")
            if mlp:
                ps_attr, ps_h0, ps_o0, ps_st, ps_h1, ps_o1, ps_nt = [ps(k) for k in ("attr", "h0", "o0", "st", "h1", "o1", "nt")]

            gathered = [sem(f"{name}_gathered{h}") for h in range(4)]
            m = [Chain(main[h], base(main[h]), steps) for h in range(2)]
            d = [Chain(dedup[h], base(dedup[h]), dedup_steps) for h in range(2)]
            n_loads = len(used) + 1 + takes_attr + takes_weight + (kind == "mlp1")
            n_gathers = S * len(tables)
            consumed = "product" if not mlp else "hidden1"
            b_loaded = [base(x) for x in loaded]
            b_scattered = [base(x) for x in scattered]
            b_stored = [base(x) for x in stored]
            half = UNITS // 2

            def loads_of(h, i):
                return i * (16 * n_loads) + (b_loaded[h] + 16 * n_loads)

            def gathers_of(h, i):
                return i * (16 * n_gathers) + 16 * n_gathers

            def scatters_of(t, i, h, ago):
                return i * 32 + (b_scattered[t] + 16 * (h - ago + 1))

            def stores_of(h, i):
                return i * 16 + (b_stored[h] + 16)

            windowed = None
            if mlp:
                windowed = windowed_mlp(st, name, tables, agg[0], rnd, gathered,
                                        [ps_h0, ps_attr, ps_h1, ps_merged, ps_o0, ps_o1, ps_st, ps_nt])
            elif kind != "message":
                windowed = windowed_pass(st, name, tables, width, agg[0], kind, gathered, ps_merged)

            def either(eng, engine, general):
                if windowed is None:
                    return general()
                unordered = eng.value_load(disorder[0:1, 0:1], min_val=0, max_val=1)
                with eng.If_eq(eng.to_reg(unordered), 0):
                    windowed[engine](eng)
                with eng.Else():
                    general()

            block = st.enter_context(nc.Block())

            @block.sync
            def _(sp):
                def store_state(i, h):
                    sp.wait_ge(m[h].sem, m[h].at("next_t", i))
                    sp.sem_inc(sp_tick, 1)
                    sp.dma_start(edge_t[bass.ds(i * 2 + h, 1), :, :].squeeze(0), next_t[h][:, :]).then_inc(stored[h], 16)

                def unit(i, h, first):
                    u = bass.ds(i * 2 + h, 1)
                    if not first:
                        sp.wait_ge(m[h].sem, m[h].end(i - 1))
                        sp.sem_inc(sp_tick, 1)
                        sp.wait_ge(d[h].sem, d[h].end(i - 1))
                        sp.sem_inc(sp_tick, 1)
                        sp.wait_ge(gathered[h], gathers_of(h, i - 1))
                        sp.sem_inc(sp_tick, 1)
                        if kind == "mlp0":
                            store_state(i - 1, h)
                    for e in used:
                        sp.dma_start(J[e][h][:, :], ends[e][u].squeeze(0)).then_inc(loaded[h], 16)
                    sp.dma_start(B[h][:, :], ends[target][u].rearrange("u p s -> u (p s)").broadcast_to([P, P * S]))\
                      .then_inc(loaded[h], 16)
                    if takes_attr:
                        sp.dma_start(attr[h][:, :], attr_u[u].squeeze(0)).then_inc(loaded[h], 16)
                    if takes_weight:
                        sp.dma_start(wt[h][:, :], weight_u[u].squeeze(0)).then_inc(loaded[h], 16)
                    if kind == "mlp1":
                        sp.dma_start(state_t[h][:, :], edge_t[u].squeeze(0)).then_inc(loaded[h], 16)

                def body(i, first):
                    for h in range(2):
                        unit(i, h, first)

                def general():
                    rolled(sp, half, body)
                    if kind == "mlp0":
                        for h in range(2):
                            store_state(half - 1, h)
                        for h in range(2):
                            sp.wait_ge(stored[h], stores_of(h, half - 1))

                either(sp, "sync", general)

            @block.gpsimd
            def _(pool):
                def gathers(i, h, first):
                    pool.wait_ge(loaded[h], loads_of(h, i))
                    pool.sem_inc(pool_tick, 1)
                    if not first:
                        pool.wait_ge(m[h].sem, m[h].at(consumed, i - 1))
                        pool.sem_inc(pool_tick, 1)
                    for n, (table, _, end) in enumerate(tables):
                        for t in range(S):
                            pool.indirect_dma_start(
                                G[n][h][:, t, :], None, table,
                                bass.IndirectOffsetOnAxis(ap=J[end][h][:, t:t + 1], axis=0),
                            ).then_inc(gathered[h], 16)

                def scatters(i, h, first):
                    pool.wait_ge(m[h].sem, m[h].at("merged_out", i))
                    pool.sem_inc(pool_tick, 1)
                    for t in range(S):
                        if not (first and h == 0):
                            pool.wait_ge(scattered[t], scatters_of(t, i, h, 1))
                            pool.sem_inc(pool_tick, 1)
                        pool.indirect_dma_start(
                            agg[t], bass.IndirectOffsetOnAxis(ap=index[h][:, t:t + 1], axis=0), SV[h][:, t, :], None,
                            compute_op=ALU.add).then_inc(scattered[t], 16)

                def general():
                    gathers(0, 0, True)

                    def body(i, first, last=False):
                        gathers(i, 1, first)
                        scatters(i, 0, first)
                        if not last:
                            gathers(i + 1, 0, False)
                        scatters(i, 1, first)

                    body(0, True)
                    with pool.Fori(1, half - 1) as i:
                        body(i, False)
                    body(half - 1, False, True)
                    for t in range(S):
                        pool.wait_ge(scattered[t], scatters_of(t, half, 0, 1))

                either(pool, "gpsimd", general)

            @block.vector
            def _(dve):
                def targets(i, h, first):
                    q = d[h]
                    Jt = J[target][h]
                    dve.wait_ge(loaded[h], loads_of(h, i))
                    if not first or h == 1:
                        dve.wait_ge(d[1 - h].sem, d[1 - h].end(i - (1 - h)))
                    if not first:
                        dve.wait_ge(m[h].sem, m[h].at("merged", i - 1))
                    dve.tensor_tensor(same[h][:, :, :], bc3(Jt[:, :], [P, S, P]),
                                      B[h][:, :].rearrange("p (q s) -> p s q", s=S), ALU.is_equal).then_inc(q.sem, 1)
                    dve.wait_ge(q.sem, q.at("equal", i))
                    dve.tensor_tensor(masked[:, :, :], same[h][:, :, :],
                                      earlier[:, :].unsqueeze(1).broadcast_to([P, S, P]), ALU.mult).then_inc(q.sem, 1)
                    dve.wait_ge(q.sem, q.at("masked", i))
                    dve.tensor_reduce(rep[:, :], masked[:, :, :], axis=AX.X, op=ALU.max).then_inc(q.sem, 1)
                    dve.wait_ge(q.sem, q.at("repeated", i))
                    dve.tensor_scalar(alt[:, :], Jt[:, :], -1.0, spare[:, :], ALU.mult, ALU.add).then_inc(q.sem, 1)
                    dve.wait_ge(q.sem, q.at("to_spare", i))
                    dve.tensor_tensor(alt[:, :], alt[:, :], rep[:, :], ALU.mult).then_inc(q.sem, 1)
                    dve.wait_ge(q.sem, q.at("if_repeated", i))
                    if not first:
                        for t in range(S):
                            dve.wait_ge(scattered[t], scatters_of(t, i, h, 2))
                    dve.tensor_tensor(index[h][:, :], alt[:, :], Jt[:, :], ALU.add).then_inc(q.sem, 1)

                def body(i, first):
                    for h in range(2):
                        q = m[h]
                        targets(i, h, first)
                        if kind in ("message", "conv"):
                            dve.wait_ge(loaded[h], loads_of(h, i))
                            dve.wait_ge(gathered[h], gathers_of(h, i))
                            if not first or h == 1:
                                dve.wait_ge(m[1 - h].sem, m[1 - h].at("summed", i - (1 - h)))
                            dve.tensor_tensor(prod[:, :, :], G[0][h][:, :, :].rearrange("p s (a f) -> p (s a) f", f=F),
                                              bc3(attr[h][:, :], [P, S * A, F]), ALU.mult).then_inc(q.sem, 1)
                            dve.wait_ge(q.sem, q.at("product", i))
                            if kind == "message":
                                if not first or h == 1:
                                    dve.wait_ge(m[1 - h].sem, m[1 - h].at("silu", i - (1 - h)))
                                to = summed[:, :, :]
                            else:
                                if not first:
                                    dve.wait_ge(m[h].sem, m[h].at("merged", i - 1))
                                to = V[h][:, :, 0:F]
                            dve.tensor_reduce(to, prod[:, :, :].rearrange("p (s a) f -> p s f a", a=A), axis=AX.X,
                                              op=ALU.add).then_inc(q.sem, 1)
                            if kind == "conv":
                                dve.wait_ge(q.sem, q.at("summed", i))
                                dve.tensor_copy(V[h][:, :, F:F + 1], wt[h][:, :].unsqueeze(2)).then_inc(q.sem, 1)
                        if kind == "gcn":
                            dve.wait_ge(loaded[h], loads_of(h, i))
                            dve.wait_ge(gathered[h], gathers_of(h, i))
                            if not first:
                                dve.wait_ge(m[h].sem, m[h].at("merged", i - 1))
                            dve.tensor_tensor(V[h][:, :, :], G[0][h][:, :, :], bc3(wt[h][:, :], [P, S, F]),
                                              ALU.mult).then_inc(q.sem, 1)
                        if kind == "mlp0":
                            dve.wait_ge(q.sem, q.at("attr_turned", i))
                            dve.tensor_copy(attr_t[:, :], ps_attr[0:S * A, 0:P]).then_inc(q.sem, 1)
                            norm_stats(dve, q, "enc", i, squares[:, :, :], D, S, stat)
                            dve.wait_ge(q.sem, q.at(rsqrt_names("enc")[-1], i))
                            dve.tensor_tensor(state[:, :, :], ps_o0[0:P, 0:S * D].rearrange("p (s d) -> p s d", d=D),
                                              bc3(stat[:, 0, 0:S], [P, S, D]), ALU.mult).then_inc(q.sem, 1)
                            dve.wait_ge(q.sem, q.at("enc_norm", i))
                            dve.tensor_tensor(state[:, :, :], state[:, :, :],
                                              gb["eenc"][:, 0, :].unsqueeze(1).broadcast_to([P, S, D]), ALU.mult).then_inc(q.sem, 1)
                            dve.wait_ge(q.sem, q.at("enc_gain", i))
                            dve.tensor_tensor(state[:, :, :], state[:, :, :],
                                              gb["eenc"][:, 1, :].unsqueeze(1).broadcast_to([P, S, D]), ALU.add).then_inc(q.sem, 1)
                        if mlp:
                            norm_stats(dve, q, "upd", i, squares[:, :, :], D, S, stat)
                            if not first:
                                dve.wait_ge(m[h].sem, m[h].at("merged", i - 1))
                            dve.wait_ge(q.sem, q.at(rsqrt_names("upd")[-1], i))
                            dve.tensor_tensor(V[h][:, :, :], ps_o1[0:P, 0:S * D].rearrange("p (s d) -> p s d", d=D),
                                              bc3(stat[:, 0, 0:S], [P, S, D]), ALU.mult).then_inc(q.sem, 1)
                            dve.wait_ge(q.sem, q.at("upd_norm", i))
                            dve.tensor_tensor(V[h][:, :, :], V[h][:, :, :],
                                              gb[f"eblk_{rnd}"][:, 0, :].unsqueeze(1).broadcast_to([P, S, D]), ALU.mult).then_inc(q.sem, 1)
                            dve.wait_ge(q.sem, q.at("upd_gain", i))
                            dve.tensor_tensor(V[h][:, :, :], V[h][:, :, :],
                                              gb[f"eblk_{rnd}"][:, 1, :].unsqueeze(1).broadcast_to([P, S, D]), ALU.add).then_inc(q.sem, 1)
                        if kind == "mlp0":
                            dve.wait_ge(q.sem, q.at("upd_bias", i))
                            dve.tensor_tensor(V[h][:, :, :], V[h][:, :, :], state[:, :, :], ALU.add).then_inc(q.sem, 1)

                def general():
                    rolled(dve, half, body)

                either(dve, "vector", general)

            @block.scalar
            def _(act):
                def body(i, first):
                    for h in range(2):
                        q = m[h]
                        if kind == "message":
                            act.wait_ge(q.sem, q.at("summed", i))
                            if not first:
                                act.wait_ge(m[h].sem, m[h].at("merged", i - 1))
                            act.activation(V[h][:, :, :], summed[:, :, :], ACT.Silu,
                                           scale=float(1 / np.float32(np.sqrt(F * A)))).then_inc(q.sem, 1)
                        if kind == "mlp0":
                            act.wait_ge(q.sem, q.at("hidden0", i))
                            act.activation(act0[:, :], ps_h0[:, 0:PAIRS * P], ACT.Silu, bias=col["eenc0"][:, :]).then_inc(q.sem, 1)
                            act.wait_ge(q.sem, q.at("out0", i))
                            act.activation(squares[:, :, :].rearrange("p s d -> p (s d)"), ps_o0[0:P, 0:S * D], ACT.Square).then_inc(q.sem, 1)
                            act.wait_ge(q.sem, q.at("state_turned", i))
                            act.activation(state_t[0][:, :], ps_st[:, 0:PAIRS * P], ACT.Copy).then_inc(q.sem, 1)
                        if mlp:
                            act.wait_ge(q.sem, q.at("hidden1", i))
                            act.activation(act1[:, :], ps_h1[:, 0:PAIRS * P], ACT.Silu).then_inc(q.sem, 1)
                            act.wait_ge(q.sem, q.at("out1", i))
                            act.activation(squares[:, :, :].rearrange("p s d -> p (s d)"), ps_o1[0:P, 0:S * D], ACT.Square).then_inc(q.sem, 1)
                        if kind == "mlp0":
                            act.wait_ge(q.sem, q.at("next_turned", i))
                            if not first:
                                act.wait_ge(stored[h], stores_of(h, i - 1))
                            act.activation(next_t[h][:, :], ps_nt[:, 0:PAIRS * P], ACT.Copy).then_inc(q.sem, 1)
                        act.wait_ge(q.sem, q.at("merged", i))
                        act.wait_ge(d[h].sem, d[h].at("index", i))
                        act.activation(SV[h][:, :, :].rearrange("p s w -> p (s w)"), ps_merged[0:P, 0:S * width], ACT.Copy).then_inc(q.sem, 1)

                def general():
                    rolled(act, half, body)

                either(act, "scalar", general)

            @block.tensor
            def _(pe):
                def body(i, first):
                    for h in range(2):
                        q = m[h]
                        if kind == "mlp0":
                            pe.wait_ge(loaded[h], loads_of(h, i))
                            if not first or h == 1:
                                pe.wait_ge(m[1 - h].sem, m[1 - h].end(i - (1 - h)))
                            pe.matmul(ps_attr[0:S * A, 0:P], attr[h][:, :], ident[:, :], start=True, stop=True).then_inc(q.sem, 1)
                            pe.wait_ge(q.sem, q.at("attr_t", i))
                            for k in range(PAIRS):
                                last = pe.matmul(ps_h0[:, k * P:(k + 1) * P], w_eenc0[:, k * 2 * D:(k + 1) * 2 * D],
                                                 attr_t[:, :], start=True, stop=True)
                            last.then_inc(q.sem, 1)
                            pe.wait_ge(q.sem, q.at("act0", i))
                            pe.matmul(ps_o0[0:P, 0:S * D], ones[:, :], row["eenc1"][:, :], start=True, stop=False)
                            for k in range(PAIRS):
                                last = pe.matmul(ps_o0[0:P, k * 2 * D:(k + 1) * 2 * D], act0[:, k * P:(k + 1) * P],
                                                 W["eenc1"][:, :], start=False, stop=k == PAIRS - 1)
                            last.then_inc(q.sem, 1)
                            pe.wait_ge(q.sem, q.at("enc_bias", i))
                            for k in range(PAIRS):
                                last = pe.matmul(ps_st[:, k * P:(k + 1) * P],
                                                 state[:, 2 * k:2 * k + 2, :].rearrange("p s d -> p (s d)"), ident[:, :],
                                                 start=True, stop=True)
                            last.then_inc(q.sem, 1)
                            pe.wait_ge(q.sem, q.at("state_t", i))
                        elif mlp:
                            pe.wait_ge(loaded[h], loads_of(h, i))
                            if not first or h == 1:
                                pe.wait_ge(m[1 - h].sem, m[1 - h].end(i - (1 - h)))
                        if mlp:
                            pe.wait_ge(gathered[h], gathers_of(h, i))
                            pe.matmul(ps_h1[:, 0:PAIRS * P], W[f"eblk_e{rnd}"][:, :],
                                      state_t[0 if kind == "mlp0" else h][:, :], start=True, stop=False)
                            for n in range(2):
                                for k in range(PAIRS):
                                    last = pe.matmul(ps_h1[:, k * P:(k + 1) * P],
                                                     G[n][h][:, 2 * k:2 * k + 2, :].rearrange("p s d -> p (s d)"),
                                                     ident[:, :], start=False, stop=n == 1 and k == PAIRS - 1)
                            last.then_inc(q.sem, 1)
                            pe.wait_ge(q.sem, q.at("act1", i))
                            pe.matmul(ps_o1[0:P, 0:S * D], ones[:, :], row[f"eblk1_{rnd}"][:, :], start=True, stop=False)
                            for k in range(PAIRS):
                                last = pe.matmul(ps_o1[0:P, k * 2 * D:(k + 1) * 2 * D], act1[:, k * P:(k + 1) * P],
                                                 W[f"eblk1{rnd}"][:, :], start=False, stop=k == PAIRS - 1)
                            last.then_inc(q.sem, 1)
                        if kind == "mlp0":
                            pe.wait_ge(q.sem, q.at("state_added", i))
                            for k in range(PAIRS):
                                last = pe.matmul(ps_nt[:, k * P:(k + 1) * P],
                                                 V[h][:, 2 * k:2 * k + 2, :].rearrange("p s d -> p (s d)"), ident[:, :],
                                                 start=True, stop=True)
                            last.then_inc(q.sem, 1)
                        pe.wait_ge(q.sem, q.before("merged", i))
                        pe.wait_ge(d[h].sem, d[h].at("equal", i))
                        if not first or h == 1:
                            pe.wait_ge(m[1 - h].sem, m[1 - h].end(i - (1 - h)))
                        for t in range(S):
                            last = pe.matmul(ps_merged[0:P, t * width:(t + 1) * width], same[h][:, t, :], V[h][:, t, :],
                                             start=True, stop=True)
                        last.then_inc(q.sem, 1)

                def general():
                    rolled(pe, half, body)

                either(pe, "tensor", general)

        for h in range(2):
            advance(main[h], m[h].n * half)
            advance(dedup[h], d[h].n * half)
            advance(loaded[h], 16 * n_loads * half)
            if kind == "mlp0":
                advance(stored[h], 16 * half)
        for t in range(S):
            advance(scattered[t], 16 * UNITS)

    def node_pass(name, loads, stores, steps, dve_body, act_body, pe_body, bufs):
        q = Chain(node_chain, base(node_chain), steps)
        b_loaded, b_stored = base(node_loaded), base(node_stored)

        def ready(step, i):
            if step == q.steps[0]:
                return node_loaded, i * (16 * len(loads)) + (b_loaded + 16 * len(loads))
            return q.sem, q.before(step, i)

        block = bufs.enter_context(nc.Block())

        @block.sync
        def _(sp):
            def body(i, first):
                if not first:
                    sp.wait_ge(q.sem, q.end(i - 1))
                    sp.sem_inc(sp_tick, 1)
                    sp.wait_ge(node_stored, i * (16 * len(stores)) + b_stored)
                    sp.sem_inc(sp_tick, 1)
                u = bass.ds(i, 1)
                for tile, rows_ in loads:
                    sp.dma_start(tile, rows_[u].squeeze(0)).then_inc(node_loaded, 16)
                for rows_, tile, step in stores:
                    sp.wait_ge(q.sem, q.at(step, i))
                    sp.sem_inc(sp_tick, 1)
                    sp.dma_start(rows_[u].squeeze(0), tile).then_inc(node_stored, 16)

            rolled(sp, NODE_UNITS, body)
            sp.wait_ge(node_stored, b_stored + 16 * len(stores) * NODE_UNITS)

        @block.vector
        def _(dve):
            rolled(dve, NODE_UNITS, lambda i, first: dve_body(dve, q, ready, i))

        if act_body is not None:
            @block.scalar
            def _(act):
                rolled(act, NODE_UNITS, lambda i, first: act_body(act, q, ready, i))

        if pe_body is not None:
            @block.tensor
            def _(pe):
                rolled(pe, NODE_UNITS, lambda i, first: pe_body(pe, q, ready, i))

        advance(node_chain, q.n * NODE_UNITS)
        advance(node_loaded, 16 * len(loads) * NODE_UNITS)
        advance(node_stored, 16 * len(stores) * NODE_UNITS)

    def ln_relu(dve, q, ready, p, i, x, centered, squares, v, h):
        dve.wait_ge(*ready(f"{p}_sum", i))
        dve.tensor_reduce(v[:, 1, 0:C], x, axis=AX.X, op=ALU.add).then_inc(q.sem, 1)
        dve.wait_ge(*ready(f"{p}_mean", i))
        dve.tensor_scalar(v[:, 1, 0:C], v[:, 1, 0:C], -1.0 / F, None, ALU.mult).then_inc(q.sem, 1)
        dve.wait_ge(*ready(f"{p}_center", i))
        dve.tensor_tensor(centered, x, bc3(v[:, 1, 0:C], [P, C, F]), ALU.add).then_inc(q.sem, 1)
        dve.wait_ge(*ready(f"{p}_square", i))
        dve.tensor_tensor(squares, centered, centered, ALU.mult).then_inc(q.sem, 1)
        norm_stats(dve, q, p, i, squares, F, C, v)
        dve.wait_ge(*ready(f"{p}_norm", i))
        dve.scalar_tensor_tensor(out=h, in0=centered, scalar=0.0, in1=bc3(v[:, 0, 0:C], [P, C, F]),
                                 op0=ALU.max, op1=ALU.mult).then_inc(q.sem, 1)

    def ln_affine(dve, q, ready, p, i, x_ps, squares, v, k, o):
        norm_stats(dve, q, p, i, squares, D, C, v)
        dve.wait_ge(*ready(f"{p}_norm", i))
        dve.tensor_tensor(o, x_ps[0:P, 0:C * D].rearrange("p (c d) -> p c d", d=D), bc3(v[:, 0, 0:C], [P, C, D]),
                          ALU.mult).then_inc(q.sem, 1)
        dve.wait_ge(*ready(f"{p}_gain", i))
        dve.tensor_tensor(o, o, gb[k][:, 0, :].unsqueeze(1).broadcast_to([P, C, D]), ALU.mult).then_inc(q.sem, 1)
        dve.wait_ge(*ready(f"{p}_bias", i))
        dve.tensor_tensor(o, o, gb[k][:, 1, :].unsqueeze(1).broadcast_to([P, C, D]), ALU.add).then_inc(q.sem, 1)

    def flat(ap):
        return ap.rearrange("p a b -> p (a b)")

    def tables_of(agg, tile, width):
        return [(tile[:, t, :], node_rows(agg[t])) for t in range(S)]

    def turn_pairs(pe, ps_, frm):
        for k in range(C // 2):
            last = pe.matmul(ps_[:, k * P:(k + 1) * P], flat(frm[:, 2 * k:2 * k + 2, :]), ident[:, :], start=True, stop=True)
        return last

    def by_node(pe, ps_, turned, w, width, bias=None):
        if bias is not None:
            pe.matmul(ps_[0:P, 0:C * width], ones[:, :], bias[:, 0:C * width], start=True, stop=False)
        for k in range(C // 2):
            last = pe.matmul(ps_[0:P, k * 2 * width:(k + 1) * 2 * width], turned[:, k * P:(k + 1) * P], w,
                             start=bias is None, stop=bias is None or k == C // 2 - 1)
        return last

    TW = C * F
    NORM_UPD = float(1 / np.float32(np.sqrt(F * F)))
    NORM_LIN = float(1 / np.float32(np.sqrt(F)))

    def pass_scope(name, tiles, banks):
        st = ExitStack()
        t = {k: sb(f"{name}_{k}", shape, F32, st) for k, shape in tiles.items()}
        p = {k: st.enter_context(nc.psum_tensor(f"{name}_ps_{k}", [2 * D, 512], F32)) for k in banks}
        return st, t, p


    st, t, ps = pass_scope("n0", dict(x=[P, C, F], c=[P, C, F], sq=[P, C, F], v=[P, 3, 8], h=[P, C, F], ht=[TW, P],
                                      y=[P, 512]), ["t", "y"])
    with st:
        def n0_dve(dve, q, ready, i, t=t):
            ln_relu(dve, q, ready, "x", i, t["x"][:, :, :], t["c"][:, :, :], t["sq"][:, :, :], t["v"], t["h"][:, :, :])

        def n0_act(act, q, ready, i, t=t, ps=ps):
            act.wait_ge(*ready("h_t", i))
            act.activation(t["ht"][:, :], ps["t"][0:TW, 0:P], ACT.Copy).then_inc(q.sem, 1)
            act.wait_ge(*ready("y_out", i))
            act.activation(t["y"][:, :], ps["y"][0:P, :], ACT.Copy).then_inc(q.sem, 1)

        def n0_pe(pe, q, ready, i, t=t, ps=ps):
            pe.wait_ge(*ready("h_turned", i))
            pe.matmul(ps["t"][0:TW, 0:P], flat(t["h"][:, :, :]), ident[:, :], start=True, stop=True).then_inc(q.sem, 1)
            pe.wait_ge(*ready("y", i))
            pe.matmul(ps["y"][0:P, :], t["ht"][:, :], w_msg[:, :], start=True, stop=True).then_inc(q.sem, 1)

        node_pass("n0", [(flat(t["x"][:, :, :]), node_rows(ins["x"]))],
                  [(node_rows(h0_d), flat(t["h"][:, :, :]), "x_norm"), (node_rows(y0), t["y"][:, :], "y_out")],
                  ln_names("x", False) + ["h_turned", "h_t", "y", "y_out"], n0_dve, n0_act, n0_pe, st)

    edge_pass("e0", [(y0, A * F, "dst")], "src", F, agg0, "message")

    st, t, ps = pass_scope("n1", dict(x=[P, C, F], h0=[P, C, F], tab=[P, S, C * F], ag=[P, TW], agt=[TW, P], al=[P, C, F],
                                      h0t=[TW, P], prod=[P, C * F, F], u=[P, C, F], us=[P, C, F], ust=[TW, P],
                                      x1=[P, C, F], c=[P, C, F], sq=[P, C, F], v=[P, 3, 8], h=[P, C, F], ht=[TW, P],
                                      y=[P, 512]), ["agt", "al", "h0t", "up0", "up1", "ut", "ul", "y"])
    with st:
        def n1_dve(dve, q, ready, i, t=t, ps=ps):
            dve.wait_ge(*ready("agg_sum", i))
            dve.tensor_reduce(t["ag"][:, :], t["tab"][:, :, :].rearrange("p t x -> p x t"), axis=AX.X, op=ALU.add).then_inc(q.sem, 1)
            dve.wait_ge(*ready("upd_prod", i))
            for b in range(2):
                last = dve.tensor_tensor(t["prod"][:, b * 32:(b + 1) * 32, :],
                                         ps[f"up{b}"][0:P, :].rearrange("p (a f) -> p a f", f=F),
                                         bc3(flat(t["al"][:, 2 * b:2 * b + 2, :]), [P, 32, F]), ALU.mult)
            last.then_inc(q.sem, 1)
            dve.wait_ge(*ready("upd_sum", i))
            dve.tensor_reduce(t["u"][:, :, :], t["prod"][:, :, :].rearrange("p (c h) k -> p c k h", c=C), axis=AX.X,
                              op=ALU.add).then_inc(q.sem, 1)
            dve.wait_ge(*ready("x_upd", i))
            dve.scalar_tensor_tensor(out=flat(t["x1"][:, :, :]), in0=ps["ul"][0:P, 0:TW], scalar=NORM_LIN,
                                     in1=flat(t["h0"][:, :, :]), op0=ALU.mult, op1=ALU.add).then_inc(q.sem, 1)
            dve.wait_ge(*ready("x_new", i))
            dve.tensor_tensor(t["x1"][:, :, :], t["x1"][:, :, :], t["x"][:, :, :], ALU.add).then_inc(q.sem, 1)
            ln_relu(dve, q, ready, "x", i, t["x1"][:, :, :], t["c"][:, :, :], t["sq"][:, :, :], t["v"], t["h"][:, :, :])

        def n1_act(act, q, ready, i, t=t, ps=ps):
            act.wait_ge(*ready("agg_t", i))
            act.activation(t["agt"][:, :], ps["agt"][0:TW, 0:P], ACT.Copy).then_inc(q.sem, 1)
            act.wait_ge(*ready("agg_scaled", i))
            act.activation(flat(t["al"][:, :, :]), ps["al"][0:P, 0:TW], ACT.Copy, scale=NORM_LIN).then_inc(q.sem, 1)
            act.wait_ge(*ready("h0_t", i))
            act.activation(t["h0t"][:, :], ps["h0t"][0:TW, 0:P], ACT.Copy).then_inc(q.sem, 1)
            act.wait_ge(*ready("upd_silu", i))
            act.activation(t["us"][:, :, :], t["u"][:, :, :], ACT.Silu, scale=NORM_UPD).then_inc(q.sem, 1)
            act.wait_ge(*ready("u_t", i))
            act.activation(t["ust"][:, :], ps["ut"][0:TW, 0:P], ACT.Copy).then_inc(q.sem, 1)
            act.wait_ge(*ready("h_t", i))
            act.activation(t["ht"][:, :], ps["agt"][0:TW, 0:P], ACT.Copy).then_inc(q.sem, 1)
            act.wait_ge(*ready("y_out", i))
            act.activation(t["y"][:, :], ps["y"][0:P, :], ACT.Copy).then_inc(q.sem, 1)

        def n1_pe(pe, q, ready, i, t=t, ps=ps):
            pe.wait_ge(*ready("agg_turned", i))
            pe.matmul(ps["agt"][0:TW, 0:P], t["ag"][:, :], ident[:, :], start=True, stop=True).then_inc(q.sem, 1)
            pe.wait_ge(*ready("agg_lin", i))
            pe.matmul(ps["al"][0:P, 0:TW], t["agt"][:, :], w_msg_lin[:, :], start=True, stop=True).then_inc(q.sem, 1)
            pe.wait_ge(*ready("h0_turned", i))
            pe.matmul(ps["h0t"][0:TW, 0:P], flat(t["h0"][:, :, :]), ident[:, :], start=True, stop=True).then_inc(q.sem, 1)
            pe.wait_ge(*ready("upd", i))
            for b in range(2):
                last = pe.matmul(ps[f"up{b}"][0:P, :], t["h0t"][:, :], w_upd[:, b * 512:(b + 1) * 512], start=True, stop=True)
            last.then_inc(q.sem, 1)
            pe.wait_ge(*ready("u_turned", i))
            pe.matmul(ps["ut"][0:TW, 0:P], flat(t["us"][:, :, :]), ident[:, :], start=True, stop=True).then_inc(q.sem, 1)
            pe.wait_ge(*ready("u_lin", i))
            pe.matmul(ps["ul"][0:P, 0:TW], t["ust"][:, :], w_upd_lin[:, :], start=True, stop=True).then_inc(q.sem, 1)
            pe.wait_ge(*ready("h_turned", i))
            pe.matmul(ps["agt"][0:TW, 0:P], flat(t["h"][:, :, :]), ident[:, :], start=True, stop=True).then_inc(q.sem, 1)
            pe.wait_ge(*ready("y", i))
            pe.matmul(ps["y"][0:P, :], t["ht"][:, :], w_conv[:, :], start=True, stop=True).then_inc(q.sem, 1)

        node_pass("n1", [(flat(t["x"][:, :, :]), node_rows(ins["x"])), (flat(t["h0"][:, :, :]), node_rows(h0_d))]
                  + tables_of(agg0, t["tab"], F),
                  [(node_rows(x1_d), flat(t["x1"][:, :, :]), "x_new"), (node_rows(y1), t["y"][:, :], "y_out")],
                  ["agg_sum", "agg_turned", "agg_t", "agg_lin", "agg_scaled", "h0_turned", "h0_t", "upd", "upd_prod",
                   "upd_sum", "upd_silu", "u_turned", "u_t", "u_lin", "x_upd", "x_new"]
                  + ln_names("x", False) + ["h_turned", "h_t", "y", "y_out"], n1_dve, n1_act, n1_pe, st)

    edge_pass("e1", [(y1, A * F, "src")], "dst", F + 1, agg1, "conv")

    send_recv = ["node_turned", "node_t", "send", "send_out", "recv", "recv_out"]

    def send_recv_act(act, q, ready, i, t, ps):
        act.wait_ge(*ready("node_t", i))
        act.activation(t["nt"][:, :], ps["nt"][:, 0:2 * P], ACT.Copy).then_inc(q.sem, 1)
        act.wait_ge(*ready("send_out", i))
        act.activation(flat(t["send"][:, :, :]), ps["send"][0:P, 0:C * D], ACT.Copy).then_inc(q.sem, 1)
        act.wait_ge(*ready("recv_out", i))
        act.activation(flat(t["recv"][:, :, :]), ps["recv"][0:P, 0:C * D], ACT.Copy).then_inc(q.sem, 1)

    def send_recv_pe(pe, q, ready, i, t, ps, r, node):
        pe.wait_ge(*ready("node_turned", i))
        turn_pairs(pe, ps["nt"], t[node]).then_inc(q.sem, 1)
        pe.wait_ge(*ready("send", i))
        by_node(pe, ps["send"], t["nt"], W[f"eblk_s{r}"][:, :], D).then_inc(q.sem, 1)
        pe.wait_ge(*ready("recv", i))
        by_node(pe, ps["recv"], t["nt"], W[f"eblk_r{r}"][:, :], D, row[f"eblk0_{r}"]).then_inc(q.sem, 1)

    st, t, ps = pass_scope("n2", dict(x=[P, C, F], tab=[P, S, C * (F + 1)], ag=[P, C, F + 1], cv=[P, C, F], deg=[P, 8],
                                      dis=[P, 8], tmp=[P, 8], pos=[P, 8], x2=[P, C, F], c=[P, C, F], sq=[P, C, F],
                                      v=[P, 3, 8], h=[P, C, F], ht=[TW, P], a=[2 * D, 2 * P], sqd=[P, C, D],
                                      n=[P, C, D], nt=[2 * D, 2 * P], send=[P, C, D], recv=[P, C, D]),
                           ["ht", "a", "o", "nt", "send", "recv"])
    with st:
        def n2_dve(dve, q, ready, i, t=t, ps=ps):
            dve.wait_ge(*ready("agg_sum", i))
            dve.tensor_reduce(flat(t["ag"][:, :, :]), t["tab"][:, :, :].rearrange("p t x -> p x t"), axis=AX.X, op=ALU.add).then_inc(q.sem, 1)
            dve.wait_ge(*ready("conv_bias", i))
            dve.tensor_tensor(t["cv"][:, :, :], t["ag"][:, :, 0:F], conv_bias[:, :].unsqueeze(1).broadcast_to([P, C, F]),
                              ALU.add).then_inc(q.sem, 1)
            dve.wait_ge(*ready("x_new", i))
            dve.scalar_tensor_tensor(out=t["x2"][:, :, :], in0=t["cv"][:, :, :], scalar=0.0, in1=t["x"][:, :, :],
                                     op0=ALU.max, op1=ALU.add).then_inc(q.sem, 1)
            deg = t["deg"][:, 0:C]
            dve.wait_ge(*ready("degree", i))
            dve.tensor_scalar(deg, t["ag"][:, :, F], 1.0, None, ALU.add).then_inc(q.sem, 1)
            dve.wait_ge(*ready("degree_positive", i))
            dve.tensor_scalar(t["pos"][:, 0:C], deg, 0.0, None, ALU.is_gt).then_inc(q.sem, 1)
            dve.wait_ge(*ready("dis_rsqrt0", i))
            dve.tensor_scalar(deg, deg, 1e-30, None, ALU.max).then_inc(q.sem, 1)
            newton(dve, q, "dis", i, deg, t["dis"][:, 0:C], t["tmp"][:, 0:C])
            dve.wait_ge(*ready("dis", i))
            dve.tensor_tensor(t["dis"][:, 0:C], t["dis"][:, 0:C], t["pos"][:, 0:C], ALU.mult).then_inc(q.sem, 1)
            ln_relu(dve, q, ready, "x", i, t["x2"][:, :, :], t["c"][:, :, :], t["sq"][:, :, :], t["v"], t["h"][:, :, :])
            ln_affine(dve, q, ready, "enc", i, ps["o"], t["sqd"][:, :, :], t["v"], "nenc", t["n"][:, :, :])

        def n2_act(act, q, ready, i, t=t, ps=ps):
            act.wait_ge(*ready("h_t", i))
            act.activation(t["ht"][:, :], ps["ht"][0:TW, 0:P], ACT.Copy).then_inc(q.sem, 1)
            act.wait_ge(*ready("act", i))
            act.activation(t["a"][:, :], ps["a"][:, 0:2 * P], ACT.Silu, bias=col["nenc0"][:, :]).then_inc(q.sem, 1)
            act.wait_ge(*ready("enc_square", i))
            act.activation(flat(t["sqd"][:, :, :]), ps["o"][0:P, 0:C * D], ACT.Square).then_inc(q.sem, 1)
            send_recv_act(act, q, ready, i, t, ps)

        def n2_pe(pe, q, ready, i, t=t, ps=ps):
            pe.wait_ge(*ready("h_turned", i))
            pe.matmul(ps["ht"][0:TW, 0:P], flat(t["h"][:, :, :]), ident[:, :], start=True, stop=True).then_inc(q.sem, 1)
            pe.wait_ge(*ready("hidden", i))
            for k in range(2):
                last = pe.matmul(ps["a"][:, k * P:(k + 1) * P], w_nenc0[:, k * 2 * D:(k + 1) * 2 * D], t["ht"][:, :],
                                 start=True, stop=True)
            last.then_inc(q.sem, 1)
            pe.wait_ge(*ready("out", i))
            by_node(pe, ps["o"], t["a"], W["nenc1"][:, :], D, row["nenc1"]).then_inc(q.sem, 1)
            send_recv_pe(pe, q, ready, i, t, ps, 0, "n")

        node_pass("n2", [(flat(t["x"][:, :, :]), node_rows(x1_d))] + tables_of(agg1, t["tab"], F + 1),
                  [(node_rows(x2_d), flat(t["x2"][:, :, :]), "x_new"), (node_rows(dis_d), t["dis"][:, 0:C], "dis"),
                   (node_rows(n0_d), flat(t["n"][:, :, :]), "enc_bias"),
                   (node_rows(send_d[0]), flat(t["send"][:, :, :]), "send_out"),
                   (node_rows(recv_d[0]), flat(t["recv"][:, :, :]), "recv_out")],
                  ["agg_sum", "conv_bias", "x_new", "degree", "degree_positive"] + rsqrt_names("dis") + ["dis"]
                  + ln_names("x", False) + ["h_turned", "h_t", "hidden", "act", "out"] + ln_names("enc", True)
                  + ["enc_gain", "enc_bias"] + send_recv, n2_dve, n2_act, n2_pe, st)

    edge_pass("e2", [(send_d[0], D, "src"), (recv_d[0], D, "dst")], "dst", D, agg2, "mlp0", 0)

    node_update = ["agg_sum", "prev_turned", "prev_t", "agg_turned", "agg_t", "hidden", "act", "out"] \
        + ln_names("upd", True) + ["upd_gain", "upd_bias", "node_new"]

    def node_update_dve(dve, q, ready, i, t, ps, r):
        dve.wait_ge(*ready("agg_sum", i))
        dve.tensor_reduce(flat(t["ag"][:, :, :]), t["tab"][:, :, :].rearrange("p t x -> p x t"), axis=AX.X, op=ALU.add).then_inc(q.sem, 1)
        ln_affine(dve, q, ready, "upd", i, ps["o"], t["sqd"][:, :, :], t["v"], f"nblk_{r}", t["n"][:, :, :])
        dve.wait_ge(*ready("node_new", i))
        dve.tensor_tensor(t["n"][:, :, :], t["n"][:, :, :], t["prev"][:, :, :], ALU.add).then_inc(q.sem, 1)

    def node_update_act(act, q, ready, i, t, ps, r):
        act.wait_ge(*ready("prev_t", i))
        act.activation(t["pt"][:, :], ps["nt"][:, 0:2 * P], ACT.Copy).then_inc(q.sem, 1)
        act.wait_ge(*ready("agg_t", i))
        act.activation(t["agt"][:, :], ps["agt"][:, 0:2 * P], ACT.Copy).then_inc(q.sem, 1)
        act.wait_ge(*ready("act", i))
        act.activation(t["a"][:, :], ps["a"][:, 0:2 * P], ACT.Silu, bias=col[f"nblk0_{r}"][:, :]).then_inc(q.sem, 1)
        act.wait_ge(*ready("upd_square", i))
        act.activation(flat(t["sqd"][:, :, :]), ps["o"][0:P, 0:C * D], ACT.Square).then_inc(q.sem, 1)

    def node_update_pe(pe, q, ready, i, t, ps, r):
        pe.wait_ge(*ready("prev_turned", i))
        turn_pairs(pe, ps["nt"], t["prev"]).then_inc(q.sem, 1)
        pe.wait_ge(*ready("agg_turned", i))
        turn_pairs(pe, ps["agt"], t["ag"]).then_inc(q.sem, 1)
        pe.wait_ge(*ready("hidden", i))
        pe.matmul(ps["a"][:, 0:2 * P], W[f"nblk_n{r}"][:, :], t["pt"][:, :], start=True, stop=False)
        pe.matmul(ps["a"][:, 0:2 * P], W[f"nblk_a{r}"][:, :], t["agt"][:, :], start=False, stop=True).then_inc(q.sem, 1)
        pe.wait_ge(*ready("out", i))
        by_node(pe, ps["o"], t["a"], W[f"nblk1{r}"][:, :], D, row[f"nblk1_{r}"]).then_inc(q.sem, 1)

    node_tiles = dict(prev=[P, C, D], tab=[P, S, C * D], ag=[P, C, D], pt=[2 * D, 2 * P], agt=[2 * D, 2 * P],
                      a=[2 * D, 2 * P], sqd=[P, C, D], v=[P, 3, 8], n=[P, C, D], nt=[2 * D, 2 * P])

    st, t, ps = pass_scope("n3", node_tiles | dict(send=[P, C, D], recv=[P, C, D]), ["nt", "agt", "a", "o", "send", "recv"])
    with st:
        def n3_dve(dve, q, ready, i, t=t, ps=ps):
            node_update_dve(dve, q, ready, i, t, ps, 0)

        def n3_act(act, q, ready, i, t=t, ps=ps):
            node_update_act(act, q, ready, i, t, ps, 0)
            send_recv_act(act, q, ready, i, t, ps)

        def n3_pe(pe, q, ready, i, t=t, ps=ps):
            node_update_pe(pe, q, ready, i, t, ps, 0)
            send_recv_pe(pe, q, ready, i, t, ps, 1, "n")

        node_pass("n3", [(flat(t["prev"][:, :, :]), node_rows(n0_d))] + tables_of(agg2, t["tab"], D),
                  [(node_rows(n1_d), flat(t["n"][:, :, :]), "node_new"),
                   (node_rows(send_d[1]), flat(t["send"][:, :, :]), "send_out"),
                   (node_rows(recv_d[1]), flat(t["recv"][:, :, :]), "recv_out")],
                  node_update + send_recv, n3_dve, n3_act, n3_pe, st)

    edge_pass("e3", [(send_d[1], D, "src"), (recv_d[1], D, "dst")], "dst", D, agg2, "mlp1", 1)

    st, t, ps = pass_scope("n4", node_tiles | dict(x=[P, C, F], dis=[P, 8], a2=[2 * D, 2 * P], x3=[P, C, F], c=[P, C, F],
                                                   sq=[P, C, F], h=[P, C, F], g=[P, C, F]),
                           ["nt", "agt", "a", "o", "a2", "dec"])
    with st:
        def n4_dve(dve, q, ready, i, t=t, ps=ps):
            node_update_dve(dve, q, ready, i, t, ps, 1)
            dve.wait_ge(*ready("dec_bias", i))
            dve.tensor_tensor(t["x3"][:, :, :], ps["dec"][0:P, 0:TW].rearrange("p (c f) -> p c f", f=F),
                              dec_b1[:, :].unsqueeze(1).broadcast_to([P, C, F]), ALU.add).then_inc(q.sem, 1)
            dve.wait_ge(*ready("x_new", i))
            dve.tensor_tensor(t["x3"][:, :, :], t["x3"][:, :, :], t["x"][:, :, :], ALU.add).then_inc(q.sem, 1)
            ln_relu(dve, q, ready, "x", i, t["x3"][:, :, :], t["c"][:, :, :], t["sq"][:, :, :], t["v"], t["h"][:, :, :])
            dve.wait_ge(*ready("h_dis", i))
            dve.tensor_tensor(t["g"][:, :, :], t["h"][:, :, :], bc3(t["dis"][:, 0:C], [P, C, F]), ALU.mult).then_inc(q.sem, 1)

        def n4_act(act, q, ready, i, t=t, ps=ps):
            node_update_act(act, q, ready, i, t, ps, 1)
            act.wait_ge(*ready("node_t", i))
            act.activation(t["nt"][:, :], ps["nt"][:, 0:2 * P], ACT.Copy).then_inc(q.sem, 1)
            act.wait_ge(*ready("dec_act", i))
            act.activation(t["a2"][:, :], ps["a2"][:, 0:2 * P], ACT.Silu, bias=col["dec0"][:, :]).then_inc(q.sem, 1)

        def n4_pe(pe, q, ready, i, t=t, ps=ps):
            node_update_pe(pe, q, ready, i, t, ps, 1)
            pe.wait_ge(*ready("node_turned", i))
            turn_pairs(pe, ps["nt"], t["n"]).then_inc(q.sem, 1)
            pe.wait_ge(*ready("dec_hidden", i))
            pe.matmul(ps["a2"][:, 0:2 * P], W["dec0"][:, :], t["nt"][:, :], start=True, stop=True).then_inc(q.sem, 1)
            pe.wait_ge(*ready("dec", i))
            by_node(pe, ps["dec"], t["a2"], w_dec1[:, :], F).then_inc(q.sem, 1)

        node_pass("n4", [(flat(t["prev"][:, :, :]), node_rows(n1_d)), (flat(t["x"][:, :, :]), node_rows(x2_d)),
                         (t["dis"][:, 0:C], node_rows(dis_d))] + tables_of(agg2, t["tab"], D),
                  [(node_rows(x3_d), flat(t["x3"][:, :, :]), "x_new"), (node_rows(g1_d), flat(t["g"][:, :, :]), "h_dis")],
                  node_update + ["node_turned", "node_t", "dec_hidden", "dec_act", "dec", "dec_bias", "x_new"]
                  + ln_names("x", False) + ["h_dis"], n4_dve, n4_act, n4_pe, st)

    edge_pass("e4", [(g1_d, F, "src")], "dst", F, agg3, "gcn")

    def own_loop(dve, q, ready, i, t):
        dve.wait_ge(*ready("own", i))
        dve.tensor_tensor(flat(t["s"][:, :, :]), flat(t["s"][:, :, :]), flat(t["g"][:, :, :]), ALU.add).then_inc(q.sem, 1)
        dve.wait_ge(*ready("s_dis", i))
        dve.tensor_tensor(t["s"][:, :, :], t["s"][:, :, :], bc3(t["dis"][:, 0:C], [P, C, F]), ALU.mult).then_inc(q.sem, 1)

    st, t, ps = pass_scope("n5", dict(tab=[P, S, TW], s=[P, C, F], g=[P, C, F], dis=[P, 8], sT=[TW, P], a=[2 * TW, P],
                                      o=[P, C, F]), ["s", "a", "o"])
    with st:
        def n5_dve(dve, q, ready, i, t=t, ps=ps):
            dve.wait_ge(*ready("agg_sum", i))
            dve.tensor_reduce(flat(t["s"][:, :, :]), t["tab"][:, :, :].rearrange("p t x -> p x t"), axis=AX.X, op=ALU.add).then_inc(q.sem, 1)
            own_loop(dve, q, ready, i, t)
            dve.wait_ge(*ready("o_dis", i))
            dve.tensor_tensor(t["o"][:, :, :], ps["o"][0:P, 0:TW].rearrange("p (c f) -> p c f", f=F),
                              bc3(t["dis"][:, 0:C], [P, C, F]), ALU.mult).then_inc(q.sem, 1)

        def n5_act(act, q, ready, i, t=t, ps=ps):
            act.wait_ge(*ready("s_t", i))
            act.activation(t["sT"][:, :], ps["s"][0:TW, 0:P], ACT.Copy).then_inc(q.sem, 1)
            act.wait_ge(*ready("act", i))
            act.activation(t["a"][:, :], ps["a"][:, 0:P], ACT.Relu, bias=gcn_b1[:, :]).then_inc(q.sem, 1)

        def n5_pe(pe, q, ready, i, t=t, ps=ps):
            pe.wait_ge(*ready("s_turned", i))
            pe.matmul(ps["s"][0:TW, 0:P], flat(t["s"][:, :, :]), ident[:, :], start=True, stop=True).then_inc(q.sem, 1)
            pe.wait_ge(*ready("hidden", i))
            pe.matmul(ps["a"][:, 0:P], w_gcn1[:, :], t["sT"][:, :], start=True, stop=True).then_inc(q.sem, 1)
            pe.wait_ge(*ready("out", i))
            pe.matmul(ps["o"][0:P, 0:TW], t["a"][:, :], w_gcn2[:, :], start=True, stop=True).then_inc(q.sem, 1)

        node_pass("n5", [(flat(t["g"][:, :, :]), node_rows(g1_d)), (t["dis"][:, 0:C], node_rows(dis_d))]
                  + tables_of(agg3, t["tab"], F),
                  [(node_rows(g2_d), flat(t["o"][:, :, :]), "o_dis")],
                  ["agg_sum", "own", "s_dis", "s_turned", "s_t", "hidden", "act", "out", "o_dis"], n5_dve, n5_act, n5_pe, st)

    edge_pass("e5", [(g2_d, F, "src")], "dst", F, agg4, "gcn")

    st, t, ps = pass_scope("n6", dict(tab=[P, S, TW], s=[P, C, F], g=[P, C, F], dis=[P, 8], x=[P, C, F], o=[P, C, F]), [])
    with st:
        def n6_dve(dve, q, ready, i, t=t, ps=ps):
            dve.wait_ge(*ready("agg_sum", i))
            dve.tensor_reduce(flat(t["s"][:, :, :]), t["tab"][:, :, :].rearrange("p t x -> p x t"), axis=AX.X, op=ALU.add).then_inc(q.sem, 1)
            own_loop(dve, q, ready, i, t)
            dve.wait_ge(*ready("s_bias", i))
            dve.tensor_tensor(t["s"][:, :, :], t["s"][:, :, :], gcn_b2[:, :].unsqueeze(1).broadcast_to([P, C, F]),
                              ALU.add).then_inc(q.sem, 1)
            dve.wait_ge(*ready("x_new", i))
            dve.tensor_tensor(t["o"][:, :, :], t["s"][:, :, :], t["x"][:, :, :], ALU.add).then_inc(q.sem, 1)

        node_pass("n6", [(flat(t["g"][:, :, :]), node_rows(g2_d)), (t["dis"][:, 0:C], node_rows(dis_d)),
                         (flat(t["x"][:, :, :]), node_rows(x3_d))] + tables_of(agg4, t["tab"], F),
                  [(node_rows(out), flat(t["o"][:, :, :]), "x_new")],
                  ["agg_sum", "own", "s_dis", "s_bias", "x_new"], n6_dve, None, None, st)


def kernel(**inputs):
    import concourse.bacc as bacc
    from concourse.bass_utils import run_bass_kernel_spmd

    nc = bacc.Bacc("TRN2", target_bir_lowering=False, num_devices=1)
    arrays, aps = {}, {}
    for name, value in inputs.items():
        value = np.ascontiguousarray(value)
        arrays[f"in_{name}"] = value
        aps[name] = nc.dram_tensor(f"in_{name}", value.shape, mybir.dt.from_np(value.dtype), kind="ExternalInput").ap()
    out = nc.dram_tensor("out_0", (N, F), F32, kind="ExternalOutput").ap()
    gnn_kernel(nc, aps, out)
    result = run_bass_kernel_spmd(nc, [arrays], core_ids=[0])
    return result.results[0]["out_0"]
```

```python
from contextlib import ExitStack

import numpy as np
import concourse.bass as bass
from concourse import mybir

F32 = mybir.dt.float32
BF16 = mybir.dt.bfloat16
I32 = mybir.dt.int32
ALU = mybir.AluOpType
ACT = mybir.ActivationFunctionType
AX = mybir.AxisListType

N = 12500
E = 412500
P = 125
WIN = 64
S = 6
UNITS = E // (P * S)
PAIRS = S // 2
C = 4
NODE_UNITS = N // (P * C)
K = 5
NODE_TURNS = NODE_UNITS // K
ROWS = N + P
F = 16
A = 8
D = 64
EPS = 1e-5
RSQRT_STEPS = 12


class Chain:

    def __init__(self, sem, base, steps):
        self.sem, self.base, self.steps = sem, base, list(steps)
        assert len(set(self.steps)) == len(self.steps), self.steps
        self.n = len(self.steps)

    def at(self, step, i):
        return i * self.n + (self.base + self.steps.index(step) + 1)

    def end(self, i):
        return i * self.n + (self.base + self.n)

    def before(self, step, i):
        k = self.steps.index(step)
        assert k, step
        return i * self.n + (self.base + k)


def rsqrt_names(p):
    return [f"{p}_rsqrt{k}" for k in range(RSQRT_STEPS)]


def ln_names(p, centered):
    first = [] if centered else [f"{p}_sum", f"{p}_mean", f"{p}_center"]
    return first + [f"{p}_square", f"{p}_var"] + rsqrt_names(p) + [f"{p}_norm"]


def rolled(eng, n, body):
    body(0, True)
    with eng.Fori(1, n) as i:
        body(i, False)


def in_duos(eng, n, body, ahead=False):
    assert n % 2 and n > 6
    for d in range(3):
        body(d, d % 2, d, False)
    with eng.Fori(1, n // 2 - ahead) as j:
        body(j * 2 + 1, 1, 2, False)
        body(j * 2 + 2, 0, 2, False)
    if ahead:
        body(n - 2, 1, 2, False)
        body(n - 1, 0, 2, True)


def bc3(ap, shape):
    return ap.unsqueeze(2).broadcast_to(shape)


def gnn_kernel(nc, ins, out):
    ctx = ExitStack()
    with ctx:
        _gnn(nc, ctx, ins, out)


def _gnn(nc, ctx, ins, out):
    def sb(name, shape, dt=F32, at=None):
        return (at or ctx).enter_context(nc.sbuf_tensor(name, shape, dt))

    def sem(name):
        return ctx.enter_context(nc.semaphore(name))

    main = [sem("main_chain0"), sem("main_chain1")]
    dedup = [sem("dedup_chain0"), sem("dedup_chain1")]
    loaded = [sem("loaded0"), sem("loaded1")]
    scattered = [sem(f"scattered{t}") for t in range(S)]
    stored = [sem("stored0"), sem("stored1")]
    pool_tick = sem("pool_tick")
    sp_tick = sem("sp_tick")
    node_chain = [sem(f"node_chain{u}") for u in range(K)]
    node_loaded, node_stored = sem("node_loaded"), sem("node_stored")
    half_chain = [sem("half_chain0"), sem("half_chain1")]
    back_chain = [sem("back_chain0"), sem("back_chain1")]
    window_chain = sem("window_chain")
    merge_chain = sem("merge_chain")
    stat_chain = sem("stat_chain")
    full_chain = [sem("full_chain0"), sem("full_chain1")]
    duo_loaded = [sem("duo_loaded0"), sem("duo_loaded1")]
    duo_stored = [sem("duo_stored0"), sem("duo_stored1")]
    full_loaded = [sem("full_loaded0"), sem("full_loaded1")]
    sums_stored = sem("sums_stored")
    duo_scattered = [sem(f"duo_scattered{t}") for t in range(S)]
    count = {}

    def base(s):
        return count.get(s.num, 0)

    def advance(s, by):
        count[s.num] = base(s) + by

    def dram(name, shape):
        return nc.dram_tensor(name, shape, F32).ap()

    y0 = dram("y0", [ROWS, A * F])
    y1 = dram("y1", [N, A * F])
    h0_d = dram("h0", [N, F])
    x1_d, x2_d, x3_d = dram("x1", [N, F]), dram("x2", [N, F]), dram("x3", [N, F])
    n0_d, n1_d = dram("n0", [N, D]), dram("n1", [N, D])
    send_d = [dram("send0", [N, D]), dram("send1", [N, D])]
    recv_d = [dram("recv0", [ROWS, D]), dram("recv1", [ROWS, D])]
    dis_d = dram("dis", [N, 1])
    g1_d, g2_d = dram("g1", [N, F]), dram("g2", [N, F])
    edge_t = dram("edge_t", [UNITS, 2 * D, PAIRS * P])
    unit_t = dram("unit_t", [UNITS, 2 * D, PAIRS * P])
    full_states = dram("full_states", [UNITS, P, S * D])
    agg0 = [dram(f"agg0_{t}", [ROWS, F]) for t in range(S)]
    agg1 = [dram(f"agg1_{t}", [ROWS, F + 1]) for t in range(S)]
    agg2 = [dram(f"agg2_{t}", [ROWS, D]) for t in range(S)]
    agg3 = [dram(f"agg3_{t}", [ROWS, F]) for t in range(S)]
    agg4 = [dram(f"agg4_{t}", [ROWS, F]) for t in range(S)]

    ident = sb("ident", [P, P])
    earlier = sb("earlier", [P, P])
    spare_i = sb("spare_i", [P, 1], I32)
    spare = sb("spare", [P, 1])
    ones = sb("ones", [1, P])
    ones_col = sb("ones_col", [P, 1])
    w_msg = sb("w_msg", [C * F, C * A * F])
    w_msg_lin = sb("w_msg_lin", [C * F, C * F])
    w_upd = sb("w_upd", [C * F, C * F * F])
    w_upd_lin = sb("w_upd_lin", [C * F, C * F])
    w_conv = sb("w_conv", [C * F, C * A * F])
    conv_bias = sb("conv_bias", [P, F])
    w_nenc0 = sb("w_nenc0", [C * F, C * D])
    w_eenc0 = sb("w_eenc0", [S * A, S * D])
    w_gcn1 = sb("w_gcn1", [C * F, C * 32])
    w_gcn2 = sb("w_gcn2", [C * 32, C * F])
    gcn_b1 = sb("gcn_b1", [C * 32, 1])
    gcn_b2 = sb("gcn_b2", [P, F])
    w_dec1 = sb("w_dec1", [2 * D, 2 * F])
    dec_b1 = sb("dec_b1", [P, F])
    iota_row = sb("iota_row", [P, WIN])
    iota_col = sb("iota_col", [2 * D, 1])
    iota_i = sb("iota_i", [P, WIN], I32)
    iota_ci = sb("iota_ci", [2 * D, 1], I32)
    ones3 = sb("ones3", [3, P], BF16)
    row3 = {k: sb(f"row3_{k}", [3, S * D], BF16) for k in ("eenc1", "eblk1_0", "eblk1_1")}
    w_state = sb("w_state", [2 * D, 2 * D])
    col_state = sb("col_state", [2 * D, 1])
    both_bias = sb("both_bias", [P, D])
    disorder = sb("disorder", [1, 1], I32)
    sq = ["nenc1", "eenc1"] + [f"{w}{s}" for s in range(2) for w in
                               ("eblk_e", "eblk_s", "eblk_r", "eblk1", "nblk_n", "nblk_a", "nblk1")] + ["dec0"]
    W = {k: sb(f"w_{k}", [2 * D, 2 * D]) for k in sq}
    col = {k: sb(f"col_{k}", [2 * D, 1]) for k in ("nenc0", "eenc0", "nblk0_0", "nblk0_1", "dec0")}
    row = {k: sb(f"row_{k}", [1, S * D]) for k in ("nenc1", "eenc1", "eblk1_0", "eblk1_1", "nblk1_0", "nblk1_1",
                                                  "eblk0_0", "eblk0_1")}
    gb = {k: sb(f"gb_{k}", [P, 2, D]) for k in ("nenc", "eenc", "eblk_0", "eblk_1", "nblk_0", "nblk_1")}

    with ExitStack() as st:
        zero = sb("zero", [P, ROWS // P * D], F32, st)
        stage = {k: sb(f"stage_{k}", [2 * D, D], F32, st) for k in sq}
        stage_row = sb("stage_row", [1, len(row), D], F32, st)
        mean = sb("mean", [2 * D, len(sq)], F32, st)
        mean_row = sb("mean_row", [1, len(row)], F32, st)
        gain_col = sb("gain_col", [2 * D, 1], F32, st)
        bias_col = sb("bias_col", [2 * D, 1], F32, st)
        parts = {k: sb(f"parts_{k}", [1, 2, S * D], F32, st) for k in row3}
        parts16 = {k: sb(f"parts16_{k}", [1, 3, S * D], BF16, st) for k in row3}
        split = sem("split")
        placed = sem("placed")
        DP = max(k for k in range(1, P + 1) if UNITS // 2 % k == 0)
        DR = UNITS // 2 // DP
        targets = sb("targets", [DP, DR, 2 * P * S], I32, st)
        first_target = sb("first_target", [DP, DR], F32, st)
        extent = sb("extent", [DP, 4, DR], F32, st)
        outside = sb("outside", [DP, 1], F32, st)
        firsts = sb("firsts", [1, UNITS // 2], I32, st)
        back = sb("back", [1, UNITS // 2], F32, st)
        furthest, amiss = sb("furthest", [1, 1], F32, st), sb("amiss", [1, 1], F32, st)
        ps_setup = st.enter_context(nc.psum_tensor("ps_setup", [2 * D, 512], F32))
        ordered, multiplied = sem("ordered"), sem("multiplied")
        cleared, weights, zeroed, wchain, consts = (sem(x) for x in ("cleared", "weights", "zeroed", "wchain", "consts"))
        small = [w_msg, w_msg_lin, w_upd, w_upd_lin, w_conv, w_nenc0, w_eenc0, w_gcn1, w_gcn2, w_dec1]
        square = {
            "nenc1": ins["L2_gnn_node_enc_w1"], "eenc1": ins["L2_gnn_edge_enc_w1"], "dec0": ins["L2_gnn_dec_w0"]}
        for s in range(2):
            w0, w1 = ins["L2_gnn_edge_blk_w0"], ins["L2_gnn_node_blk_w0"]
            square |= {f"eblk_e{s}": w0[s, 0:D, :], f"eblk_s{s}": w0[s, D:2 * D, :], f"eblk_r{s}": w0[s, 2 * D:3 * D, :],
                       f"eblk1{s}": ins["L2_gnn_edge_blk_w1"][s], f"nblk_n{s}": w1[s, 0:D, :],
                       f"nblk_a{s}": w1[s, D:2 * D, :], f"nblk1{s}": ins["L2_gnn_node_blk_w1"][s]}
        rows = {"nenc1": ins["L2_gnn_node_enc_b1"], "eenc1": ins["L2_gnn_edge_enc_b1"],
                "eblk1_0": ins["L2_gnn_edge_blk_b1"][0], "eblk1_1": ins["L2_gnn_edge_blk_b1"][1],
                "nblk1_0": ins["L2_gnn_node_blk_b1"][0], "nblk1_1": ins["L2_gnn_node_blk_b1"][1],
                "eblk0_0": ins["L2_gnn_edge_blk_b0"][0], "eblk0_1": ins["L2_gnn_edge_blk_b0"][1]}
        cols = {"nenc0": ins["L2_gnn_node_enc_b0"], "eenc0": ins["L2_gnn_edge_enc_b0"],
                "nblk0_0": ins["L2_gnn_node_blk_b0"][0], "nblk0_1": ins["L2_gnn_node_blk_b0"][1],
                "dec0": ins["L2_gnn_dec_b0"]}
        gbs = {"nenc": (ins["L2_gnn_node_enc_g"], ins["L2_gnn_node_enc_beta"]),
               "eenc": (ins["L2_gnn_edge_enc_g"], ins["L2_gnn_edge_enc_beta"])}
        for s in range(2):
            gbs[f"eblk_{s}"] = (ins["L2_gnn_edge_blk_g"][s], ins["L2_gnn_edge_blk_beta"][s])
            gbs[f"nblk_{s}"] = (ins["L2_gnn_node_blk_g"][s], ins["L2_gnn_node_blk_beta"][s])
        diagonals = []
        diagonals.append((w_msg, ins["L0_gnn_W_msg_tp"].rearrange("i j h -> i (j h)"), C))
        diagonals.append((w_msg_lin, ins["L0_gnn_W_msg_lin"], C))
        diagonals.append((w_upd, ins["L0_gnn_W_upd_tp"].rearrange("i h k -> i (h k)"), C))
        diagonals.append((w_upd_lin, ins["L0_gnn_W_upd_lin"], C))
        diagonals.append((w_nenc0, ins["L2_gnn_node_enc_w0"], C))
        diagonals.append((w_eenc0, ins["L2_gnn_edge_enc_w0"], S))
        diagonals.append((w_dec1, ins["L2_gnn_dec_w1"], 2))
        gcn_w1_t = ins["L3_gnn_W1"].rearrange("o i -> i o")
        gcn_w2_t = ins["L3_gnn_W2"].rearrange("o i -> i o")
        diagonals.append((w_gcn1, gcn_w1_t, C))
        diagonals.append((w_gcn2, gcn_w2_t, C))
        n_loads = [0]

        block = st.enter_context(nc.Block())

        @block.sync
        def _(sp):
            def load(dst, src):
                sp.dma_start(dst, src).then_inc(weights, 16)
                n_loads[0] += 1

            sp.wait_ge(cleared, 2)
            with nc.allow_non_contiguous_dma(reason="small weights, transposed once"):
                for dst, src, copies in diagonals:
                    k, m = src.shape
                    for t in range(copies):
                        load(dst[t * k:(t + 1) * k, t * m:(t + 1) * m], src)
                for t in range(C):
                    for a in range(A):
                        load(w_conv[t * F:(t + 1) * F, (t * A + a) * F:(t * A + a + 1) * F],
                             ins["L1_gnn_weight_matrix"][a].rearrange("o i -> i o"))
            for k, src in square.items():
                for half in range(2):
                    load(stage[k][half * D:(half + 1) * D, :], src)
            for n, k in enumerate(row):
                load(stage_row[:, n, :], rows[k].unsqueeze(0))
            with nc.allow_non_contiguous_dma(reason="biases as columns"):
                for k in col:
                    for half in range(2):
                        load(col[k][half * D:(half + 1) * D, :], cols[k].unsqueeze(1))
                for t in range(C):
                    load(gcn_b1[t * 32:(t + 1) * 32, :], ins["L3_gnn_b1"].unsqueeze(1))
            for k in gb:
                for n in range(2):
                    load(gb[k][:, n, :], gbs[k][n].unsqueeze(0).broadcast_to([P, D]))
            with nc.allow_non_contiguous_dma(reason="gain and bias as columns"):
                for half in range(2):
                    load(gain_col[half * D:(half + 1) * D, :], ins["L2_gnn_edge_enc_g"].unsqueeze(1))
                    load(bias_col[half * D:(half + 1) * D, :], ins["L2_gnn_edge_enc_beta"].unsqueeze(1))
            with nc.allow_non_contiguous_dma(reason="the first target of each duo of units"):
                load(firsts[:, :], ins["dst"].rearrange("(r e) -> e r", e=2 * P * S)[0:1, :])
            load(targets[:, :, :], ins["dst"].rearrange("(p r e) -> p r e", r=DR, e=2 * P * S))
            load(conv_bias[:, :], ins["L1_gnn_bias"].unsqueeze(0).broadcast_to([P, F]))
            load(gcn_b2[:, :], ins["L3_gnn_b2"].unsqueeze(0).broadcast_to([P, F]))
            load(dec_b1[:, :], ins["L2_gnn_dec_b1"].unsqueeze(0).broadcast_to([P, F]))

        @block.scalar
        def _(act):
            act.wait_ge(cleared, 2)
            n = 0
            for tables, width in ((agg0, F), (agg1, F + 1), (agg2, D), (agg3, F), (agg4, F)):
                for table in tables:
                    act.dma_start(table.rearrange("(p r) f -> p (r f)", p=P),
                                  zero[:, 0:ROWS // P * width]).then_inc(zeroed, 16)
                    n += 1
            for table in recv_d:
                act.dma_start(table[N:ROWS, :], zero[:, 0:D]).then_inc(zeroed, 16)
                n += 1
            act.dma_start(y0[N:ROWS, :], zero[:, 0:A * F]).then_inc(zeroed, 16)
            n += 1
            act.wait_ge(split, 5 * len(row3))
            n_placed = 0
            for k in row3:
                for part in range(3):
                    act.dma_start(row3[k][part:part + 1, :], parts16[k][:, part, :]).then_inc(placed, 16)
                    n_placed += 1
            act.wait_ge(placed, 16 * n_placed)
            act.wait_ge(zeroed, 16 * n)

        @block.gpsimd
        def _(pool):
            pool.memset(ident[:, :], 0.0).then_inc(consts, 1)
            pool.memset(earlier[:, :], 1.0).then_inc(consts, 1)
            pool.memset(ones[:, :], 1.0).then_inc(consts, 1)
            pool.iota(spare_i[:, :], pattern=[[0, 1]], base=N, channel_multiplier=1).then_inc(consts, 1)
            pool.iota(iota_i[:, :], pattern=[[1, WIN]], base=0, channel_multiplier=0).then_inc(consts, 1)
            for half in range(2):
                pool.wait_ge(consts, 5 + half)
                pool.iota(iota_ci[half * D:(half + 1) * D, :], pattern=[[0, 1]], base=0, channel_multiplier=1).then_inc(consts, 1)
            pool.wait_ge(consts, 7)
            pool.memset(ones3[:, :], 1.0).then_inc(consts, 1)
            pool.memset(ones_col[:, :], 1.0).then_inc(consts, 1)
            pool.wait_ge(consts, 9)
            pool.tensor_copy(iota_row[:, :], iota_i[:, :]).then_inc(consts, 1)
            pool.tensor_copy(iota_col[:, :], iota_ci[:, :]).then_inc(consts, 1)
            pool.affine_select(out=ident[:, :], in_=ident[:, :], compare_op=ALU.not_equal, fill=1.0,
                               base=0, pattern=[[-1, P]], channel_multiplier=1).then_inc(consts, 1)
            pool.affine_select(out=earlier[:, :], in_=earlier[:, :], compare_op=ALU.is_gt, fill=0.0,
                               base=0, pattern=[[-1, P]], channel_multiplier=1).then_inc(consts, 1)
            pool.tensor_copy(spare[:, :], spare_i[:, :]).then_inc(consts, 1)
            pool.wait_ge(consts, 14)

        @block.vector
        def _(dve):
            dve.memset(zero[:, :], 0.0).then_inc(cleared, 1)
            for w in small:
                last = dve.memset(w[:, :], 0.0)
            last.then_inc(cleared, 1)
            for k in sq:
                last = dve.memset(W[k][:, :], 0.0)
            last.then_inc(wchain, 1)
            dve.wait_ge(weights, 16 * n_loads[0])
            dve.wait_ge(wchain, 1)
            centered = ["nenc1", "eenc1"] + [f"{w}1{s}" for s in range(2) for w in ("eblk", "nblk")]
            for n, k in enumerate(sq):
                last = dve.tensor_reduce(mean[:, n:n + 1], stage[k][:, :], axis=AX.X, op=ALU.add)
            last = dve.tensor_reduce(mean_row[:, :], stage_row[:, :, :], axis=AX.X, op=ALU.add)
            last.then_inc(wchain, 1)
            dve.wait_ge(wchain, 2)
            dve.tensor_scalar(mean[:, :], mean[:, :], -1.0 / D, None, ALU.mult).then_inc(wchain, 1)
            dve.tensor_scalar(mean_row[:, :], mean_row[:, :], -1.0 / D, None, ALU.mult).then_inc(wchain, 1)
            dve.wait_ge(wchain, 4)
            for n, k in enumerate(sq):
                for half in range(2):
                    q = slice(half * D, (half + 1) * D)
                    if k in centered:
                        last = dve.tensor_scalar(W[k][q, q], stage[k][q, :], mean[q, n:n + 1], None, ALU.add)
                    else:
                        last = dve.tensor_copy(W[k][q, q], stage[k][q, :])
            for n, k in enumerate(row):
                for t in range(S):
                    q = slice(t * D, (t + 1) * D)
                    if k.startswith("eblk0"):
                        last = dve.tensor_copy(row[k][:, q], stage_row[:, n, :])
                    else:
                        last = dve.tensor_scalar(row[k][:, q], stage_row[:, n, :], mean_row[:, n:n + 1], None, ALU.add)
            last.then_inc(wchain, 1)
            dve.wait_ge(wchain, 5)
            dve.tensor_scalar(w_state[:, :], W["eblk_e0"][:, :], gain_col[:, :], None, ALU.mult).then_inc(wchain, 1)
            dve.tensor_tensor(both_bias[:, :], gb["eenc"][:, 1, :], gb["eblk_0"][:, 1, :], ALU.add).then_inc(wchain, 1)
            dve.wait_ge(multiplied, 1)
            dve.tensor_copy(col_state[:, :], ps_setup[:, 0:1]).then_inc(wchain, 1)
            n = 0
            for k in row3:
                lo, hi = parts[k], parts16[k]
                for part in range(3):
                    frm = row[k][:, :] if part == 0 else lo[:, part - 1, :]
                    dve.tensor_copy(hi[:, part, :], frm).then_inc(split, 1)
                    n += 1
                    dve.wait_ge(split, n)
                    if part < 2:
                        dve.tensor_tensor(lo[:, part, :], frm, hi[:, part, :], ALU.subtract).then_inc(split, 1)
                        n += 1
                        dve.wait_ge(split, n)
            dve.tensor_copy(first_target[:, :], targets[:, :, 0]).then_inc(ordered, 1)
            dve.tensor_reduce(extent[:, 0, :], targets[:, :, :], axis=AX.X, op=ALU.max).then_inc(ordered, 1)
            dve.tensor_reduce(extent[:, 1, :], targets[:, :, :], axis=AX.X, op=ALU.min).then_inc(ordered, 1)
            dve.tensor_tensor(back[:, 1:], firsts[:, 0:UNITS // 2 - 1], firsts[:, 1:], ALU.subtract).then_inc(ordered, 1)
            dve.wait_ge(ordered, 4)
            dve.tensor_reduce(furthest[:, :], back[:, 1:], axis=AX.X, op=ALU.max).then_inc(ordered, 1)
            dve.tensor_tensor(extent[:, 2, :], extent[:, 0, :], first_target[:, :], ALU.subtract).then_inc(ordered, 1)
            dve.tensor_tensor(extent[:, 3, :], first_target[:, :], extent[:, 1, :], ALU.subtract).then_inc(ordered, 1)
            dve.wait_ge(ordered, 7)
            dve.tensor_scalar(extent[:, 2, :], extent[:, 2, :], float(1 - WIN), 0.0, ALU.add, ALU.max).then_inc(ordered, 1)
            dve.tensor_scalar(extent[:, 3, :], extent[:, 3, :], 0.0, None, ALU.max).then_inc(ordered, 1)
            dve.wait_ge(ordered, 9)
            dve.tensor_reduce(outside[:, :], extent[:, 2:4, :], axis=AX.XY, op=ALU.max).then_inc(ordered, 1)
            dve.wait_ge(multiplied, 2)
            dve.scalar_tensor_tensor(out=amiss[:, :], in0=furthest[:, :], scalar=0.0, in1=ps_setup[0:1, 2:3],
                                     op0=ALU.max, op1=ALU.add).then_inc(ordered, 1)
            dve.wait_ge(ordered, 11)
            dve.tensor_scalar(disorder[:, :], amiss[:, :], 1.0, None, ALU.min).then_inc(ordered, 1)
            dve.wait_ge(ordered, 12)

        @block.tensor
        def _(pe):
            pe.wait_ge(weights, 16 * n_loads[0])
            pe.wait_ge(wchain, 5)
            pe.matmul(ps_setup[:, 0:1], W["eblk_e0"][:, :], bias_col[:, :], start=True, stop=True).then_inc(multiplied, 1)
            pe.wait_ge(consts, 14)
            pe.wait_ge(ordered, 10)
            pe.wait_ge(wchain, 8)
            pe.matmul(ps_setup[0:1, 2:3], outside[:, :], ones_col[0:DP, :], start=True, stop=True).then_inc(multiplied, 1)

    def norm_stats(dve, chain, p, i, squares, width, n, v):
        dve.wait_ge(chain.sem, chain.at(f"{p}_square", i))
        dve.tensor_reduce(v[:, 1, 0:n], squares, axis=AX.X, op=ALU.add).then_inc(chain.sem, 1)
        dve.wait_ge(chain.sem, chain.at(f"{p}_var", i))
        dve.tensor_scalar(v[:, 1, 0:n], v[:, 1, 0:n], 1.0 / width, EPS, ALU.mult, ALU.add).then_inc(chain.sem, 1)
        newton(dve, chain, p, i, v[:, 1, 0:n], v[:, 0, 0:n], v[:, 2, 0:n])

    def newton(dve, chain, p, i, value, out_, t):
        names = rsqrt_names(p)

        dve.wait_ge(chain.sem, chain.at(names[0], i))
        dve.tensor_scalar(t.bitcast(I32), value.bitcast(I32), 1, None, ALU.logical_shift_right).then_inc(chain.sem, 1)
        dve.wait_ge(chain.sem, chain.at(names[1], i))
        dve.tensor_scalar(out_.bitcast(I32), t.bitcast(I32), -1.0, float(0x5F3759DF), ALU.mult, ALU.add).then_inc(chain.sem, 1)
        for r in range(3):
            dve.wait_ge(chain.sem, chain.at(names[2 + 3 * r], i))
            dve.scalar_tensor_tensor(out=t, in0=out_, scalar=-0.5, in1=value, op0=ALU.mult, op1=ALU.mult).then_inc(chain.sem, 1)
            dve.wait_ge(chain.sem, chain.at(names[3 + 3 * r], i))
            dve.tensor_tensor(t, t, out_, ALU.mult).then_inc(chain.sem, 1)
            dve.wait_ge(chain.sem, chain.at(names[4 + 3 * r], i))
            dve.scalar_tensor_tensor(out=out_, in0=t, scalar=1.5, in1=out_, op0=ALU.add, op1=ALU.mult).then_inc(chain.sem, 1)

    def edge_rows(ap):
        return ap.rearrange("(u p s) k -> u p (s k)", p=P, s=S)

    def node_rows(ap):
        return ap[0:N, :].rearrange("(v u p c) k -> v p u (c k)", u=K, p=P, c=C)

    attr_u = edge_rows(ins["edge_attr_8"])
    src_u = edge_rows(ins["src"].unsqueeze(1))
    dst_u = edge_rows(ins["dst"].unsqueeze(1))
    weight_u = edge_rows(ins["edge_weight"].unsqueeze(1))

    DUO = 2 * P * S
    DUOS = UNITS // 2
    src_d = ins["src"].rearrange("(d h p s) -> d p h s", h=2, p=P, s=S)
    dst_d = ins["dst"].rearrange("(d h p s) -> d p h s", h=2, p=P, s=S)
    weight_d = ins["edge_weight"].rearrange("(d h p s) -> d p h s", h=2, p=P, s=S)
    attr_d = ins["edge_attr_8"].rearrange("(d h p s) k -> d p h (s k)", h=2, p=P, s=S)
    edge_t_d = edge_t.rearrange("(d h) p n -> d p h n", h=2)
    src_duo = ins["src"].rearrange("(d e) -> d e", e=DUO)
    unit_t_d = unit_t.rearrange("(d h) p n -> d p h n", h=2)
    full_d = full_states.rearrange("(d h) p n -> d p h n", h=2)
    dst_duo = ins["dst"].rearrange("(d e) -> d e", e=DUO)

    def store_sums(sp, g, agg, tile, d, b_sums, again):
        sp.wait_ge(g.sem, g.at("merged_out", d))
        sp.sem_inc(sp_tick, 1)
        if again:
            sp.wait_ge(sums_stored, d * 16 + b_sums)
            sp.sem_inc(sp_tick, 1)
        at = sp.value_load(dst_duo[bass.ds(d, 1), 0:1], min_val=0, max_val=N - 1)
        sp.dma_start(agg[bass.ds(at, WIN), :], tile[:, :]).then_inc(sums_stored, 16)

    def windowed_pass(st, name, tables, width, agg, kind, gathered, into, enc_banks):
        conv = kind == "conv"
        steps = ["product", "summed", "weight"] if conv else ["product"]
        q = [Chain(half_chain[h], base(half_chain[h]), steps) for h in range(2)]
        g = Chain(merge_chain, base(merge_chain), ["merged", "merged_out"])
        w = Chain(window_chain, base(window_chain), ["row", "pick0", "pick1", "col", "shift"])
        b_loaded = [base(x) for x in duo_loaded]
        b_sums = base(sums_stored)
        n_loads = 4 + conv
        e = [Chain(back_chain[h], base(back_chain[h]), ["attr_turned", "attr_t", "hidden0", "act0", "out0", "enc_square",
                                                        "enc_var", "enc_norm", "state_turned", "state_t"]) for h in range(2)]
        r = Chain(stat_chain, base(stat_chain), rsqrt_names("dev"))
        f = [Chain(full_chain[h], base(full_chain[h]), ["full_gain", "full_bias"]) for h in range(2)]
        b_stored = [base(x) for x in duo_stored]

        def tiles(k, shape, dt=F32, n=2):
            return [sb(f"{name}_w_{k}{x}", shape, dt, st) for x in range(n)]

        Jsrc, Jdst = tiles("src", [P, 2, S], I32), tiles("dst", [P, 2, S], I32)
        first = tiles("first", [2 * D, 1], I32)
        G = tiles("g", [P, S, tables[0][1]], F32, 4)
        attr = tiles("attr", [P, 2, S * A]) if conv else None
        wt = tiles("wt", [P, 2, S])
        row_ids, col_ids = tiles("row_ids", [P, WIN]), tiles("col_ids", [2 * D, 1])
        shift = tiles("shift", [WIN, WIN])
        pick = tiles("pick", [P, S, WIN], F32, 4)
        merged = tiles("merged", [WIN, width])
        V = tiles("v", [P, S, width], F32, 4)
        prod = tiles("prod", [P, S * A, F]) if conv else None

        if conv:
            O0, H0 = enc_banks[0:2], enc_banks[2:4]
            attr_t, act0 = tiles("attr_t", [S * A, P]), tiles("act0", [2 * D, PAIRS * P])
            sq0, unit = tiles("sq0", [P, S, D]), tiles("unit", [P, S, D])
            state_t, full = tiles("state_t", [2 * D, 2, PAIRS * P]), tiles("full", [P, 2, S * D])
            stat = tiles("stat", [P, 3, 2 * S], F32, 1)[0]
            for h in range(2):
                advance(back_chain[h], e[h].n * DUOS)
                advance(full_chain[h], 2 * DUOS)
                advance(duo_stored[h], 16 * DUOS)
            advance(stat_chain, r.n * DUOS)

        def three(ap):
            return ap.rearrange("p (s d) -> p s d", d=D)

        for h in range(2):
            advance(half_chain[h], q[h].n * DUOS)
        advance(merge_chain, 2 * DUOS)
        advance(window_chain, w.n * DUOS)
        advance(sums_stored, 16 * DUOS)
        for x in range(2):
            advance(duo_loaded[x], 16 * n_loads * (DUOS // 2 + 1 - x))

        def by_parity(d, x, each, b):
            if isinstance(d, int):
                return (d // 2 + 1) * each + b
            return (d - x) * (each // 2) + (each + b)

        def loads_of(d, x):
            return by_parity(d, x, 16 * n_loads, b_loaded[x])

        def gathers_of(d, x):
            return by_parity(d, x, 16 * S, 0)

        def sums_to(d):
            return d * 16 + b_sums

        def sync(sp):
            def body(d, x, before, last):
                if before >= 2:
                    for h in range(2):
                        sp.wait_ge(q[h].sem, q[h].end(d - 2))
                        sp.sem_inc(sp_tick, 1)
                        if conv:
                            sp.wait_ge(e[h].sem, e[h].at("attr_turned", d - 2))
                            sp.sem_inc(sp_tick, 1)
                u = bass.ds(d, 1)
                sp.dma_start(Jsrc[x][:, :, :], src_d[u].squeeze(0)).then_inc(duo_loaded[x], 16)
                sp.dma_start(Jdst[x][:, :, :], dst_d[u].squeeze(0)).then_inc(duo_loaded[x], 16)
                sp.dma_start(first[x][:, :], dst_duo[u, 0:1].broadcast_to([2 * D, 1])).then_inc(duo_loaded[x], 16)
                sp.dma_start(wt[x][:, :, :], weight_d[u].squeeze(0)).then_inc(duo_loaded[x], 16)
                if conv:
                    sp.dma_start(attr[x][:, :, :], attr_d[u].squeeze(0)).then_inc(duo_loaded[x], 16)
                if before >= 2:
                    store_sums(sp, g, agg, merged[x], d - 2, b_sums, before >= 3 or not isinstance(d, int))

            in_duos(sp, DUOS, body)
            for d in (DUOS - 2, DUOS - 1):
                store_sums(sp, g, agg, merged[d % 2], d, b_sums, True)
            sp.wait_ge(sums_stored, sums_to(DUOS))

        def gpsimd(pool):
            def gathers(d, x, before):
                pool.wait_ge(duo_loaded[x], loads_of(d, x))
                pool.sem_inc(pool_tick, 1)
                for h in range(2):
                    if before >= 2:
                        pool.wait_ge(q[h].sem, q[h].at("product", d - 2))
                        pool.sem_inc(pool_tick, 1)
                    for t in range(S):
                        pool.indirect_dma_start(
                            G[2 * x + h][:, t, :], None, tables[0][0],
                            bass.IndirectOffsetOnAxis(ap=Jsrc[x][:, h, t:t + 1], axis=0),
                        ).then_inc(gathered[2 * x + h], 16)

            def body(d, x, before, last):
                if not last:
                    gathers(d + 1, 1 - x, before + 1)

            gathers(0, 0, 0)
            in_duos(pool, DUOS, body, ahead=True)

        def vector(dve):
            def body(d, x, before, last):
                dve.wait_ge(duo_loaded[x], loads_of(d, x))
                if before:
                    dve.wait_ge(w.sem, w.end(d - 1))
                dve.tensor_tensor(row_ids[x][:, :], iota_row[:, :], first[x][0:P, :].broadcast_to([P, WIN]), ALU.add).then_inc(w.sem, 1)
                dve.wait_ge(w.sem, w.at("row", d))
                if before >= 2:
                    dve.wait_ge(g.sem, g.at("merged", d - 2))
                for h in range(2):
                    dve.tensor_tensor(pick[2 * x + h][:, :, :], bc3(Jdst[x][:, h, :], [P, S, WIN]),
                                      row_ids[x][:, :].unsqueeze(1).broadcast_to([P, S, WIN]), ALU.is_equal).then_inc(w.sem, 1)
                dve.tensor_tensor(col_ids[x][:, :], iota_col[:, :], first[x][:, :], ALU.add).then_inc(w.sem, 1)
                dve.wait_ge(w.sem, w.at("col", d))
                dve.tensor_scalar(shift[x][:, :], row_ids[x][0:WIN, :], col_ids[1 - x if before else x][0:WIN, :], None,
                                  ALU.is_equal).then_inc(w.sem, 1)
                dve.wait_ge(w.sem, w.end(d))
                for h in range(2):
                    k = 2 * x + h
                    dve.wait_ge(gathered[k], gathers_of(d, x))
                    if conv:
                        if before:
                            dve.wait_ge(q[h].sem, q[h].end(d - 1))
                        dve.tensor_tensor(prod[h][:, :, :], G[k][:, :, :].rearrange("p s (a f) -> p (s a) f", f=F),
                                          bc3(attr[x][:, h, :], [P, S * A, F]), ALU.mult).then_inc(q[h].sem, 1)
                    else:
                        dve.tensor_tensor(V[k][:, :, :], G[k][:, :, :], bc3(wt[x][:, h, :], [P, S, F]),
                                          ALU.mult).then_inc(q[h].sem, 1)
                if conv:
                    for h in range(2):
                        dve.wait_ge(q[h].sem, q[h].at("product", d))
                        dve.tensor_reduce(V[2 * x + h][:, :, 0:F], prod[h][:, :, :].rearrange("p (s a) f -> p s f a", a=A),
                                          axis=AX.X, op=ALU.add).then_inc(q[h].sem, 1)
                    for h in range(2):
                        dve.wait_ge(q[h].sem, q[h].at("summed", d))
                        dve.tensor_copy(V[2 * x + h][:, :, F:F + 1], wt[x][:, h, :].unsqueeze(2)).then_inc(q[h].sem, 1)
                    for h in range(2):
                        if before:
                            dve.wait_ge(e[h].sem, e[h].at("enc_norm", d - 1))
                        dve.wait_ge(e[h].sem, e[h].at("enc_square", d))
                        dve.tensor_reduce(stat[:, 1, h * S:(h + 1) * S], sq0[h][:, :, :], axis=AX.X, op=ALU.add).then_inc(e[h].sem, 1)
                    for h in range(2):
                        dve.wait_ge(e[h].sem, e[h].at("enc_var", d))
                    if before:
                        dve.wait_ge(r.sem, r.end(d - 1))
                    dve.tensor_scalar(stat[:, 1, :], stat[:, 1, :], 1.0 / D, EPS, ALU.mult, ALU.add).then_inc(r.sem, 1)
                    newton(dve, r, "dev", d, stat[:, 1, :], stat[:, 0, :], stat[:, 2, :])
                    dve.wait_ge(r.sem, r.end(d))
                    for h in range(2):
                        if before:
                            dve.wait_ge(f[h].sem, f[h].at("full_gain", d - 1))
                        dve.tensor_tensor(unit[h][:, :, :], three(O0[h][0:P, 0:S * D]), bc3(stat[:, 0, h * S:(h + 1) * S], [P, S, D]),
                                          ALU.mult).then_inc(e[h].sem, 1)
                    if before >= 2:
                        dve.wait_ge(duo_stored[1], (d - 1) * 16 + b_stored[1])
                    for h in range(2):
                        dve.wait_ge(e[h].sem, e[h].at("enc_norm", d))
                        dve.tensor_tensor(three(full[x][:, h, :]), unit[h][:, :, :],
                                          gb["eenc"][:, 0, :].unsqueeze(1).broadcast_to([P, S, D]), ALU.mult).then_inc(f[h].sem, 1)
                    for h in range(2):
                        dve.wait_ge(f[h].sem, f[h].at("full_gain", d))
                        dve.tensor_tensor(three(full[x][:, h, :]), three(full[x][:, h, :]),
                                          both_bias[:, :].unsqueeze(1).broadcast_to([P, S, D]), ALU.add).then_inc(f[h].sem, 1)

            in_duos(dve, DUOS, body)

        def scalar(act):
            def store(d, x, before):
                for h in range(2):
                    act.wait_ge(e[h].sem, e[h].end(d))
                if before:
                    act.wait_ge(duo_stored[0], d * 16 + b_stored[0])
                    act.wait_ge(duo_stored[1], d * 16 + b_stored[1])
                act.dma_start(unit_t_d[bass.ds(d, 1)].squeeze(0), state_t[x][:, :, :]).then_inc(duo_stored[0], 16)
                for h in range(2):
                    act.wait_ge(f[h].sem, f[h].end(d))
                act.dma_start(full_d[bass.ds(d, 1)].squeeze(0), full[x][:, :, :]).then_inc(duo_stored[1], 16)

            def body(d, x, before, last):
                if conv:
                    for h in range(2):
                        act.wait_ge(e[h].sem, e[h].at("attr_turned", d))
                        act.activation(attr_t[h][:, :], O0[h][0:S * A, 0:P], ACT.Copy).then_inc(e[h].sem, 1)
                    for h in range(2):
                        act.wait_ge(e[h].sem, e[h].at("hidden0", d))
                        act.activation(act0[h][:, :], H0[h][:, 0:PAIRS * P], ACT.Silu, bias=col["eenc0"][:, :]).then_inc(e[h].sem, 1)
                    for h in range(2):
                        act.wait_ge(e[h].sem, e[h].at("out0", d))
                        act.activation(sq0[h][:, :, :], three(O0[h][0:P, 0:S * D]), ACT.Square).then_inc(e[h].sem, 1)
                    if before:
                        store(d - 1, 1 - x, before - 1)
                act.wait_ge(g.sem, g.at("merged", d))
                if before >= 2:
                    act.wait_ge(sums_stored, sums_to(d - 1))
                act.activation(merged[x][:, :], into[0:WIN, 0:width], ACT.Copy).then_inc(g.sem, 1)
                if conv:
                    if before >= 2:
                        act.wait_ge(duo_stored[0], (d - 1) * 16 + b_stored[0])
                    for h in range(2):
                        act.wait_ge(e[h].sem, e[h].at("state_turned", d))
                        act.activation(state_t[x][:, h, :], H0[h][:, 0:PAIRS * P], ACT.Copy).then_inc(e[h].sem, 1)

            in_duos(act, DUOS, body)
            if conv:
                store(DUOS - 1, 0, 2)
                for k in range(2):
                    act.wait_ge(duo_stored[k], 16 * DUOS + b_stored[k])

        def tensor(pe):
            def body(d, x, before, last):
                if conv:
                    for h in range(2):
                        pe.wait_ge(duo_loaded[x], loads_of(d, x))
                        if before:
                            pe.wait_ge(e[h].sem, e[h].end(d - 1))
                        pe.matmul(O0[h][0:S * A, 0:P], attr[x][:, h, :], ident[:, :], start=True, stop=True).then_inc(e[h].sem, 1)
                    for h in range(2):
                        pe.wait_ge(e[h].sem, e[h].at("attr_t", d))
                        for k in range(PAIRS):
                            mm = pe.matmul(H0[h][:, k * P:(k + 1) * P], w_eenc0[:, k * 2 * D:(k + 1) * 2 * D],
                                           attr_t[h][:, :], start=True, stop=True)
                        mm.then_inc(e[h].sem, 1)
                    for h in range(2):
                        pe.wait_ge(e[h].sem, e[h].at("act0", d))
                        pe.matmul(O0[h][0:P, 0:S * D], ones3[:, :], row3["eenc1"][:, :], start=True, stop=False)
                        for k in range(PAIRS):
                            mm = pe.matmul(O0[h][0:P, k * 2 * D:(k + 1) * 2 * D], act0[h][:, k * P:(k + 1) * P],
                                           W["eenc1"][:, :], start=False, stop=k == PAIRS - 1)
                        mm.then_inc(e[h].sem, 1)
                pe.wait_ge(w.sem, w.end(d))
                if before:
                    pe.wait_ge(g.sem, g.end(d - 1))
                for h in range(2):
                    pe.wait_ge(q[h].sem, q[h].end(d))
                    for t in range(S):
                        mm = pe.matmul(into[0:WIN, 0:width], pick[2 * x + h][:, t, :], V[2 * x + h][:, t, :],
                                       start=h == 0 and t == 0, stop=not before and h == 1 and t == S - 1)
                if before:
                    mm = pe.matmul(into[0:WIN, 0:width], shift[x][:, :], merged[1 - x][:, :], start=False, stop=True)
                mm.then_inc(g.sem, 1)
                if conv:
                    for h in range(2):
                        pe.wait_ge(e[h].sem, e[h].at("enc_norm", d))
                        for k in range(PAIRS):
                            mm = pe.matmul(H0[h][:, k * P:(k + 1) * P], flat2(unit[h][:, 2 * k:2 * k + 2, :]), ident[:, :],
                                           start=True, stop=True)
                        mm.then_inc(e[h].sem, 1)

            in_duos(pe, DUOS, body)

        return dict(sync=sync, gpsimd=gpsimd, vector=vector, scalar=scalar, tensor=tensor)

    def windowed_mlp(st, name, tables, agg, rnd, gathered, banks):
        enc = rnd == 0
        front_steps = ["hidden1", "act1", "out1", "upd_square"]
        back_steps = ["upd_var", "upd_norm", "upd_gain", "values"] + (["next_turned", "next_t"] if enc else [])
        a = [Chain(half_chain[h], base(half_chain[h]), front_steps) for h in range(2)]
        b = [Chain(back_chain[h], base(back_chain[h]), back_steps) for h in range(2)]
        w = Chain(window_chain, base(window_chain), ["row", "pick0", "pick1", "col", "shift", "spread0", "spread1"])
        r = Chain(stat_chain, base(stat_chain), rsqrt_names("dev"))
        g = Chain(merge_chain, base(merge_chain), ["merged", "merged_out"])
        b_loaded = [base(x) for x in duo_loaded]
        b_stored = [base(x) for x in duo_stored]
        b_filled = [base(x) for x in full_loaded]
        b_sums = base(sums_stored)
        n_loads = 7

        def tiles(k, shape, dt=F32, n=2):
            return [sb(f"{name}_w_{k}{x}", shape, dt, st) for x in range(n)]

        Jsrc, Jdst = tiles("src", [P, 2, S], I32), tiles("dst", [P, 2, S], I32)
        first = tiles("first", [2 * D, 1], I32)
        G = tiles("g", [P, S, D], F32, 4)
        row_ids, col_ids = tiles("row_ids", [P, WIN]), tiles("col_ids", [2 * D, 1])
        shift = tiles("shift", [WIN, WIN])
        trow = tiles("row", [2 * D, DUO], I32)
        pick = tiles("pick", [P, S, WIN], F32, 4)
        spread = tiles("spread", [2 * D, PAIRS, P], F32, 4)
        window = tiles("window", [2 * D, 2 * D])
        merged = tiles("merged", [WIN, D])
        act1 = tiles("act1", [2 * D, PAIRS * P])
        sq1 = tiles("sq1", [P, S, D], F32, 4)
        stat = tiles("stat", [P, 3, 2 * S], F32, 1)[0]
        V = tiles("v", [P, S, D])
        state2 = tiles("state", [2 * D, 2, PAIRS * P])
        H1, O4, into = banks[0:2], banks[2:6], banks[6]
        if enc:
            full = tiles("full", [P, 2, S * D])
            next_t = tiles("next_t", [2 * D, PAIRS * P])

        for h in range(2):
            advance(half_chain[h], a[h].n * DUOS)
            advance(back_chain[h], b[h].n * DUOS)
            if enc:
                advance(duo_stored[h], 16 * DUOS)
        advance(window_chain, w.n * DUOS)
        advance(merge_chain, 2 * DUOS)
        advance(sums_stored, 16 * DUOS)
        advance(stat_chain, r.n * (DUOS + 1))
        for x in range(2):
            if enc:
                advance(full_loaded[x], 16 * (DUOS // 2 + 1 - x))
            advance(duo_loaded[x], 16 * n_loads * (DUOS // 2 + 1 - x))

        def by_parity(d, x, each, start):
            if isinstance(d, int):
                return (d // 2 + 1) * each + start
            return (d - x) * (each // 2) + (each + start)

        def loads_of(d, x):
            return by_parity(d, x, 16 * n_loads, b_loaded[x])

        def gathers_of(d, x):
            return by_parity(d, x, 16 * S, 0)

        def sums_to(d):
            return d * 16 + b_sums

        def three(bank):
            return bank[0:P, 0:S * D].rearrange("p (s d) -> p s d", d=D)

        def fills_of(d, x):
            return by_parity(d, x, 16, b_filled[x])

        def sync(sp):
            sp.wait_ge(cleared_windows[name], 2)

            def body(d, x, before, last):
                if before >= 2:
                    for h in range(2):
                        sp.wait_ge(a[h].sem, a[h].at("hidden1", d - 2))
                        sp.sem_inc(sp_tick, 1)
                u = bass.ds(d, 1)
                sp.dma_start(state2[x][:, :, :], (unit_t_d if enc else edge_t_d)[u].squeeze(0)).then_inc(duo_loaded[x], 16)
                sp.dma_start(first[x][:, :], dst_duo[u, 0:1].broadcast_to([2 * D, 1])).then_inc(duo_loaded[x], 16)
                sp.dma_start(Jsrc[x][:, :, :], src_d[u].squeeze(0)).then_inc(duo_loaded[x], 16)
                sp.dma_start(Jdst[x][:, :, :], dst_d[u].squeeze(0)).then_inc(duo_loaded[x], 16)
                sp.dma_start(trow[x][:, :], dst_duo[u, :].broadcast_to([2 * D, DUO])).then_inc(duo_loaded[x], 16)
                at = sp.value_load(dst_duo[u, 0:1], min_val=0, max_val=N - 1)
                for h in range(2):
                    sp.dma_start(window[x][h * D:h * D + WIN, h * D:(h + 1) * D], tables[1][0][bass.ds(at, WIN), :])\
                      .then_inc(duo_loaded[x], 16)
                if not isinstance(d, int) or d >= 3:
                    store_sums(sp, g, agg, merged[1 - x], d - 3, b_sums, not isinstance(d, int) or d > 3)

            in_duos(sp, DUOS, body)
            for d in (DUOS - 3, DUOS - 2, DUOS - 1):
                store_sums(sp, g, agg, merged[d % 2], d, b_sums, True)
            sp.wait_ge(sums_stored, sums_to(DUOS))

        def gpsimd(pool):
            def gathers(d, x, before):
                pool.wait_ge(duo_loaded[x], loads_of(d, x))
                pool.sem_inc(pool_tick, 1)
                for h in range(2):
                    if before >= 2:
                        pool.wait_ge(a[h].sem, a[h].at("hidden1", d - 2))
                        pool.sem_inc(pool_tick, 1)
                    for t in range(S):
                        pool.indirect_dma_start(
                            G[2 * x + h][:, t, :], None, tables[0][0],
                            bass.IndirectOffsetOnAxis(ap=Jsrc[x][:, h, t:t + 1], axis=0),
                        ).then_inc(gathered[2 * x + h], 16)

            def body(d, x, before, last):
                if not last:
                    gathers(d + 1, 1 - x, before + 1)

            gathers(0, 0, 0)
            in_duos(pool, DUOS, body, ahead=True)

        def vector(dve):
            for x in range(2):
                dve.memset(window[x][:, :], 0.0).then_inc(cleared_windows[name], 1)
            dve.memset(stat[:, :, :], 1.0).then_inc(cleared_windows[name], 1)
            dve.wait_ge(cleared_windows[name], 3)

            def body(d, x, before, last, front=True):
                y = 1 - x
                if front:
                    dve.wait_ge(duo_loaded[x], loads_of(d, x))
                    if before:
                        dve.wait_ge(w.sem, w.end(d - 1))
                    dve.tensor_tensor(row_ids[x][:, :], iota_row[:, :], first[x][0:P, :].broadcast_to([P, WIN]), ALU.add).then_inc(w.sem, 1)
                    dve.wait_ge(w.sem, w.at("row", d))
                    if before >= 2:
                        dve.wait_ge(g.sem, g.at("merged", d - 2))
                    for h in range(2):
                        dve.tensor_tensor(pick[2 * x + h][:, :, :], bc3(Jdst[x][:, h, :], [P, S, WIN]),
                                          row_ids[x][:, :].unsqueeze(1).broadcast_to([P, S, WIN]), ALU.is_equal).then_inc(w.sem, 1)
                    dve.tensor_tensor(col_ids[x][:, :], iota_col[:, :], first[x][:, :], ALU.add).then_inc(w.sem, 1)
                    dve.wait_ge(w.sem, w.at("col", d))
                    dve.tensor_scalar(shift[x][:, :], row_ids[x][0:WIN, :], col_ids[y if before else x][0:WIN, :], None,
                                      ALU.is_equal).then_inc(w.sem, 1)
                    for h in range(2):
                        targets_ = trow[x][:, h * P * S:(h + 1) * P * S].rearrange("p (q k two) -> p two k q", two=2, k=PAIRS)
                        if before >= 2:
                            dve.wait_ge(a[h].sem, a[h].at("hidden1", d - 2))
                        dve.tensor_scalar(spread[2 * x + h][0:D, :, :], targets_[0:D, 0], col_ids[x][0:D, :], None, ALU.is_equal)
                        dve.tensor_scalar(spread[2 * x + h][D:2 * D, :, :], targets_[D:2 * D, 1], col_ids[x][D:2 * D, :], None,
                                          ALU.is_equal).then_inc(w.sem, 1)
                if before:
                    for h in range(2):
                        if before >= 2:
                            dve.wait_ge(b[h].sem, b[h].end(d - 2))
                        dve.wait_ge(a[h].sem, a[h].at("upd_square", d - 1))
                        dve.tensor_reduce(stat[:, 1, h * S:(h + 1) * S], sq1[2 * y + h][:, :, :], axis=AX.X, op=ALU.add).then_inc(b[h].sem, 1)
                    for h in range(2):
                        dve.wait_ge(b[h].sem, b[h].at("upd_var", d - 1))
                    dve.wait_ge(r.sem, r.end(d - 1))
                dve.tensor_scalar(stat[:, 1, :], stat[:, 1, :], 1.0 / D, EPS, ALU.mult, ALU.add).then_inc(r.sem, 1)
                newton(dve, r, "dev", d, stat[:, 1, :], stat[:, 0, :], stat[:, 2, :])
                dve.wait_ge(r.sem, r.end(d))
                if before:
                    if before >= 2:
                        dve.wait_ge(g.sem, g.at("merged", d - 2))
                    for h in range(2):
                        dve.tensor_tensor(V[h][:, :, :], three(O4[2 * y + h]), bc3(stat[:, 0, h * S:(h + 1) * S], [P, S, D]),
                                          ALU.mult).then_inc(b[h].sem, 1)
                    for h in range(2):
                        dve.wait_ge(b[h].sem, b[h].at("upd_norm", d - 1))
                        dve.tensor_tensor(V[h][:, :, :], V[h][:, :, :],
                                          gb[f"eblk_{rnd}"][:, 0, :].unsqueeze(1).broadcast_to([P, S, D]), ALU.mult).then_inc(b[h].sem, 1)
                    if enc:
                        dve.wait_ge(full_loaded[y], fills_of(d - 1, y))
                    for h in range(2):
                        more = full[y][:, h, :].rearrange("p (s d) -> p s d", d=D) if enc \
                            else gb[f"eblk_{rnd}"][:, 1, :].unsqueeze(1).broadcast_to([P, S, D])
                        dve.wait_ge(b[h].sem, b[h].at("upd_gain", d - 1))
                        dve.tensor_tensor(V[h][:, :, :], V[h][:, :, :], more, ALU.add).then_inc(b[h].sem, 1)

            in_duos(dve, DUOS, body)
            body(DUOS, 1, 2, True, front=False)

        def scalar(act):
            def body(d, x, before, last, front=True):
                y = 1 - x
                if front:
                    for h in range(2):
                        act.wait_ge(a[h].sem, a[h].at("hidden1", d))
                        act.activation(act1[h][:, :], H1[h][:, 0:PAIRS * P], ACT.Silu,
                                       bias=col_state[:, :] if enc else 0.0).then_inc(a[h].sem, 1)
                    for h in range(2):
                        act.wait_ge(a[h].sem, a[h].at("out1", d))
                        if before >= 2:
                            act.wait_ge(b[h].sem, b[h].at("upd_var", d - 2))
                        act.activation(sq1[2 * x + h][:, :, :], three(O4[2 * x + h]), ACT.Square).then_inc(a[h].sem, 1)
                    if enc:
                        if before >= 2:
                            for h in range(2):
                                act.wait_ge(b[h].sem, b[h].at("values", d - 2))
                        act.dma_start(full[x][:, :, :], full_d[bass.ds(d, 1)].squeeze(0)).then_inc(full_loaded[x], 16)
                if enc and before:
                    for h in range(2):
                        act.wait_ge(b[h].sem, b[h].at("next_turned", d - 1))
                        if before >= 2:
                            act.wait_ge(duo_stored[h], (d - 1) * 16 + b_stored[h])
                        act.activation(next_t[h][:, :], O4[2 * y + h][:, 0:PAIRS * P], ACT.Copy).then_inc(b[h].sem, 1)
                    for h in range(2):
                        act.wait_ge(b[h].sem, b[h].at("next_t", d - 1))
                        act.dma_start(edge_t[bass.ds(d * 2 - 2 + h, 1), :, :].squeeze(0), next_t[h][:, :]).then_inc(duo_stored[h], 16)
                if before:
                    act.wait_ge(g.sem, g.at("merged", d - 1))
                    if before >= 2:
                        act.wait_ge(sums_stored, sums_to(d - 2))
                    act.activation(merged[y][:, :], into[0:WIN, 0:D], ACT.Copy).then_inc(g.sem, 1)

            in_duos(act, DUOS, body)
            body(DUOS, 1, 2, True, front=False)
            if enc:
                for h in range(2):
                    act.wait_ge(duo_stored[h], 16 * DUOS + b_stored[h])

        def tensor(pe):
            def hidden1(d, x, before):
                for h in range(2):
                    k4 = 2 * x + h
                    if before:
                        pe.wait_ge(a[h].sem, a[h].end(d - 1))
                    pe.wait_ge(duo_loaded[x], loads_of(d, x))
                    pe.matmul(H1[h][:, 0:PAIRS * P], w_state[:, :] if enc else W[f"eblk_e{rnd}"][:, :], state2[x][:, h, :],
                              start=True, stop=False)
                    pe.wait_ge(gathered[k4], gathers_of(d, x))
                    pe.wait_ge(w.sem, w.at(f"spread{h}", d))
                    for k in range(PAIRS):
                        pe.matmul(H1[h][:, k * P:(k + 1) * P], flat2(G[k4][:, 2 * k:2 * k + 2, :]), ident[:, :],
                                  start=False, stop=False)
                    pe.matmul(H1[h][:, 0:PAIRS * P], window[x][:, :], spread[k4][:, :, :].rearrange("p k q -> p (k q)"),
                              start=False, stop=True).then_inc(a[h].sem, 1)

            def out1(d, x, before):
                for h in range(2):
                    pe.wait_ge(a[h].sem, a[h].at("act1", d))
                    if enc and before >= 2:
                        pe.wait_ge(b[h].sem, b[h].end(d - 2))
                    o = O4[2 * x + h]
                    pe.matmul(o[0:P, 0:S * D], ones3[:, :], row3[f"eblk1_{rnd}"][:, :], start=True, stop=False)
                    for k in range(PAIRS):
                        mm = pe.matmul(o[0:P, k * 2 * D:(k + 1) * 2 * D], act1[h][:, k * P:(k + 1) * P],
                                       W[f"eblk1{rnd}"][:, :], start=False, stop=k == PAIRS - 1)
                    mm.then_inc(a[h].sem, 1)

            def body(d, x, before, last, front=True):
                y = 1 - x
                if front:
                    hidden1(d, x, before)
                    out1(d, x, before)
                if before:
                    if enc:
                        for h in range(2):
                            pe.wait_ge(b[h].sem, b[h].at("values", d - 1))
                            for k in range(PAIRS):
                                mm = pe.matmul(O4[2 * y + h][:, k * P:(k + 1) * P], flat2(V[h][:, 2 * k:2 * k + 2, :]), ident[:, :],
                                               start=True, stop=True)
                            mm.then_inc(b[h].sem, 1)
                    if before >= 2:
                        pe.wait_ge(g.sem, g.end(d - 2))
                    for h in range(2):
                        pe.wait_ge(b[h].sem, b[h].at("values", d - 1))
                        for t in range(S):
                            mm = pe.matmul(into[0:WIN, 0:D], pick[2 * y + h][:, t, :], V[h][:, t, :],
                                           start=h == 0 and t == 0, stop=before < 2 and h == 1 and t == S - 1)
                    if before >= 2:
                        mm = pe.matmul(into[0:WIN, 0:D], shift[y][:, :], merged[x][:, :], start=False, stop=True)
                    mm.then_inc(g.sem, 1)

            in_duos(pe, DUOS, body)
            body(DUOS, 1, 2, True, front=False)

        return dict(sync=sync, gpsimd=gpsimd, vector=vector, scalar=scalar, tensor=tensor)

    def windowed_message(st, name, tables, agg, merged_banks):
        q = [Chain(half_chain[h], base(half_chain[h]), ["product", "summed", "silu", "merged", "merged_out"]) for h in range(2)]
        u = [Chain(back_chain[h], base(back_chain[h]), ["equal", "masked", "repeated", "to_spare", "if_repeated", "index"])
             for h in range(2)]
        w = Chain(window_chain, base(window_chain), ["col", "spread0", "spread1", "picked0", "picked1"])
        b_loaded = [base(x) for x in duo_loaded]
        b_scattered = base(duo_scattered[0])
        n_loads = 7
        AF = A * F

        def tiles(k, shape, dt=F32, n=2):
            return [sb(f"{name}_w_{k}{x}", shape, dt, st) for x in range(n)]

        Jsrc = tiles("src", [P, 2, S], I32)
        srow, trow = tiles("src_row", [P, DUO], I32), tiles("dst_row", [2 * D, DUO], I32)
        first, col_ids = tiles("first", [2 * D, 1], I32), tiles("col_ids", [2 * D, 1])
        attr = tiles("attr", [P, 2, S * A])
        window = tiles("window", [2 * D, 2 * AF])
        spread = tiles("spread", [2 * D, PAIRS, P], F32, 4)
        same, masked = tiles("same", [P, S, P], F32, 4), tiles("masked", [P, S, P])
        rep, alt = tiles("rep", [P, S]), tiles("alt", [P, S])
        index = tiles("index", [P, S], I32, 4)
        prod, summed, V = tiles("prod", [P, S * A, F]), tiles("summed", [P, S, F]), tiles("v", [P, S, F])
        SV = tiles("sv", [P, S, F], F32, 4)
        picked = [st.enter_context(nc.psum_tensor(f"{name}_w_picked{h}", [2 * D, 1024], F32)) for h in range(2)]

        for h in range(2):
            advance(half_chain[h], q[h].n * DUOS)
            advance(back_chain[h], u[h].n * DUOS)
        advance(window_chain, w.n * DUOS)
        for t in range(S):
            advance(duo_scattered[t], 32 * DUOS)
        for x in range(2):
            advance(duo_loaded[x], 16 * n_loads * (DUOS // 2 + 1 - x))

        def loads_of(d, x):
            each = 16 * n_loads
            if isinstance(d, int):
                return (d // 2 + 1) * each + b_loaded[x]
            return (d - x) * (each // 2) + (each + b_loaded[x])

        def scatters_to(d, h):
            return d * 32 + (b_scattered + 16 * h)

        def sync(sp):
            sp.wait_ge(cleared_windows[name], 2)

            def body(d, x, before, last):
                if before >= 2:
                    for h in range(2):
                        sp.wait_ge(q[h].sem, q[h].at("product", d - 2))
                        sp.sem_inc(sp_tick, 1)
                at_duo = bass.ds(d, 1)
                sp.dma_start(trow[x][:, :], dst_duo[at_duo, :].broadcast_to([2 * D, DUO])).then_inc(duo_loaded[x], 16)
                sp.dma_start(first[x][:, :], dst_duo[at_duo, 0:1].broadcast_to([2 * D, 1])).then_inc(duo_loaded[x], 16)
                sp.dma_start(srow[x][:, :], src_duo[at_duo, :].broadcast_to([P, DUO])).then_inc(duo_loaded[x], 16)
                sp.dma_start(Jsrc[x][:, :, :], src_d[at_duo].squeeze(0)).then_inc(duo_loaded[x], 16)
                sp.dma_start(attr[x][:, :, :], attr_d[at_duo].squeeze(0)).then_inc(duo_loaded[x], 16)
                at = sp.value_load(dst_duo[at_duo, 0:1], min_val=0, max_val=N - 1)
                for h in range(2):
                    sp.dma_start(window[x][h * D:h * D + WIN, h * AF:(h + 1) * AF], tables[0][0][bass.ds(at, WIN), :])\
                      .then_inc(duo_loaded[x], 16)

            in_duos(sp, DUOS, body)

        def gpsimd(pool):
            def body(d, x, before, last):
                for h in range(2):
                    pool.wait_ge(q[h].sem, q[h].at("merged_out", d))
                    pool.sem_inc(pool_tick, 1)
                    for t in range(S):
                        if before or h:
                            pool.wait_ge(duo_scattered[t], scatters_to(d, h))
                            pool.sem_inc(pool_tick, 1)
                        pool.indirect_dma_start(
                            agg[t], bass.IndirectOffsetOnAxis(ap=index[2 * x + h][:, t:t + 1], axis=0), SV[2 * x + h][:, t, :],
                            None, compute_op=ALU.add).then_inc(duo_scattered[t], 16)

            in_duos(pool, DUOS, body)
            for t in range(S):
                pool.wait_ge(duo_scattered[t], scatters_to(DUOS, 0))

        def vector(dve):
            for x in range(2):
                dve.memset(window[x][:, :], 0.0).then_inc(cleared_windows[name], 1)

            def body(d, x, before, last):
                dve.wait_ge(duo_loaded[x], loads_of(d, x))
                if before:
                    dve.wait_ge(w.sem, w.end(d - 1))
                dve.tensor_tensor(col_ids[x][:, :], iota_col[:, :], first[x][:, :], ALU.add).then_inc(w.sem, 1)
                dve.wait_ge(w.sem, w.at("col", d))
                for h in range(2):
                    targets_ = trow[x][:, h * P * S:(h + 1) * P * S].rearrange("p (q k two) -> p two k q", two=2, k=PAIRS)
                    dve.tensor_scalar(spread[2 * x + h][0:D, :, :], targets_[0:D, 0], col_ids[x][0:D, :], None, ALU.is_equal)
                    dve.tensor_scalar(spread[2 * x + h][D:2 * D, :, :], targets_[D:2 * D, 1], col_ids[x][D:2 * D, :], None,
                                      ALU.is_equal).then_inc(w.sem, 1)
                for h in range(2):
                    if before:
                        dve.wait_ge(u[h].sem, u[h].end(d - 1))
                    if before >= 2:
                        dve.wait_ge(q[h].sem, q[h].at("merged", d - 2))
                    dve.tensor_tensor(same[2 * x + h][:, :, :], bc3(Jsrc[x][:, h, :], [P, S, P]),
                                      srow[x][:, h * P * S:(h + 1) * P * S].rearrange("p (q s) -> p s q", s=S),
                                      ALU.is_equal).then_inc(u[h].sem, 1)
                for h in range(2):
                    dve.wait_ge(u[h].sem, u[h].at("equal", d))
                    dve.tensor_tensor(masked[h][:, :, :], same[2 * x + h][:, :, :],
                                      earlier[:, :].unsqueeze(1).broadcast_to([P, S, P]), ALU.mult).then_inc(u[h].sem, 1)
                for h in range(2):
                    dve.wait_ge(u[h].sem, u[h].at("masked", d))
                    dve.tensor_reduce(rep[h][:, :], masked[h][:, :, :], axis=AX.X, op=ALU.max).then_inc(u[h].sem, 1)
                for h in range(2):
                    dve.wait_ge(u[h].sem, u[h].at("repeated", d))
                    dve.tensor_scalar(alt[h][:, :], Jsrc[x][:, h, :], -1.0, spare[:, :], ALU.mult, ALU.add).then_inc(u[h].sem, 1)
                for h in range(2):
                    dve.wait_ge(u[h].sem, u[h].at("to_spare", d))
                    dve.tensor_tensor(alt[h][:, :], alt[h][:, :], rep[h][:, :], ALU.mult).then_inc(u[h].sem, 1)
                for h in range(2):
                    dve.wait_ge(u[h].sem, u[h].at("if_repeated", d))
                    if before >= 2:
                        for t in range(S):
                            dve.wait_ge(duo_scattered[t], scatters_to(d - 2, h) + 16)
                    dve.tensor_tensor(index[2 * x + h][:, :], alt[h][:, :], Jsrc[x][:, h, :], ALU.add).then_inc(u[h].sem, 1)
                for h in range(2):
                    dve.wait_ge(w.sem, w.at(f"picked{h}", d))
                    if before:
                        dve.wait_ge(q[h].sem, q[h].end(d - 1))
                    dve.tensor_tensor(prod[h][:, :, :], picked[h][0:P, 0:S * AF].rearrange("p (s f) -> p s f", f=F),
                                      bc3(attr[x][:, h, :], [P, S * A, F]), ALU.mult).then_inc(q[h].sem, 1)
                for h in range(2):
                    dve.wait_ge(q[h].sem, q[h].at("product", d))
                    dve.tensor_reduce(summed[h][:, :, :], prod[h][:, :, :].rearrange("p (s a) f -> p s f a", a=A), axis=AX.X,
                                      op=ALU.add).then_inc(q[h].sem, 1)

            in_duos(dve, DUOS, body)

        def scalar(act):
            def body(d, x, before, last):
                for h in range(2):
                    act.wait_ge(q[h].sem, q[h].at("summed", d))
                    act.activation(V[h][:, :, :], summed[h][:, :, :], ACT.Silu,
                                   scale=float(1 / np.float32(np.sqrt(F * A)))).then_inc(q[h].sem, 1)
                for h in range(2):
                    act.wait_ge(q[h].sem, q[h].at("merged", d))
                    act.wait_ge(u[h].sem, u[h].at("index", d))
                    act.activation(flat2(SV[2 * x + h][:, :, :]), merged_banks[h][0:P, 0:S * F], ACT.Copy).then_inc(q[h].sem, 1)

            in_duos(act, DUOS, body)

        def tensor(pe):
            def body(d, x, before, last):
                for h in range(2):
                    pe.wait_ge(w.sem, w.before(f"picked{h}", d))
                    if before:
                        pe.wait_ge(q[h].sem, q[h].at("product", d - 1))
                    for k in range(PAIRS):
                        mm = pe.matmul(picked[h][0:P, k * 2 * AF:(k + 1) * 2 * AF], spread[2 * x + h][:, k, :], window[x][:, :],
                                       start=True, stop=True)
                    mm.then_inc(w.sem, 1)
                for h in range(2):
                    pe.wait_ge(q[h].sem, q[h].at("silu", d))
                    for t in range(S):
                        mm = pe.matmul(merged_banks[h][0:P, t * F:(t + 1) * F], same[2 * x + h][:, t, :], V[h][:, t, :],
                                       start=True, stop=True)
                    mm.then_inc(q[h].sem, 1)

            in_duos(pe, DUOS, body)

        return dict(sync=sync, gpsimd=gpsimd, vector=vector, scalar=scalar, tensor=tensor)

    def flat2(ap):
        return ap.rearrange("p a b -> p (a b)")

    cleared_windows = {"e0": sem("cleared_windows2"), "e2": sem("cleared_windows0"), "e3": sem("cleared_windows1")}

    def edge_pass(name, tables, target, width, agg, kind, rnd=0):
        table_widths = [w for _, w, _ in tables]
        ends = {"src": src_u, "dst": dst_u}
        used = sorted({e for _, _, e in tables} | {target})
        mlp = kind in ("mlp0", "mlp1")
        takes_attr = kind in ("message", "conv", "mlp0")
        takes_weight = kind in ("conv", "gcn")
        from_table = "attr" if takes_attr else None

        dedup_steps = ["equal", "masked", "repeated", "to_spare", "if_repeated", "index"]
        if kind in ("message", "conv"):
            steps = ["product", "summed"] + (["silu"] if kind == "message" else ["weight"])
        elif kind == "gcn":
            steps = ["product"]
        else:
            steps = []
            if kind == "mlp0":
                steps += ["attr_turned", "attr_t", "hidden0", "act0", "out0"] + ln_names("enc", True) + \
                         ["enc_gain", "enc_bias", "state_turned", "state_t"]
            steps += ["hidden1", "act1", "out1"] + ln_names("upd", True) + ["upd_gain", "upd_bias"]
            if kind == "mlp0":
                steps += ["state_added", "next_turned", "next_t"]
        steps += ["merged", "merged_out"]

        with ExitStack() as st:
            J = {e: [sb(f"{name}_{e}{h}", [P, S], I32, st) for h in range(2)] for e in used}
            B = [sb(f"{name}_row{h}", [P, P * S], I32, st) for h in range(2)]
            G = [[sb(f"{name}_g{n}{h}", [P, S, w], F32, st) for h in range(2)] for n, w in enumerate(table_widths)]
            attr = [sb(f"{name}_attr{h}", [P, S * A], F32, st) for h in range(2)] if takes_attr else None
            wt = [sb(f"{name}_wt{h}", [P, S], F32, st) for h in range(2)] if takes_weight else None
            same = [sb(f"{name}_same{h}", [P, S, P], F32, st) for h in range(2)]
            masked = sb(f"{name}_masked", [P, S, P], F32, st)
            rep = sb(f"{name}_rep", [P, S], F32, st)
            alt = sb(f"{name}_alt", [P, S], F32, st)
            index = [sb(f"{name}_index{h}", [P, S], I32, st) for h in range(2)]
            V = [sb(f"{name}_v{h}", [P, S, width], F32, st) for h in range(2)]
            SV = [sb(f"{name}_sv{h}", [P, S, width], F32, st) for h in range(2)]
            if takes_attr and not mlp:
                prod = sb(f"{name}_prod", [P, S * A, F], F32, st)
                summed = sb(f"{name}_summed", [P, S, F], F32, st)
            if mlp:
                attr_t = sb(f"{name}_attr_t", [S * A, P], F32, st)
                act0 = sb(f"{name}_act0", [2 * D, PAIRS * P], F32, st)
                act1 = sb(f"{name}_act1", [2 * D, PAIRS * P], F32, st)
                squares = sb(f"{name}_squares", [P, S, D], F32, st)
                stat = sb(f"{name}_stat", [P, 3, 8], F32, st)
                state = sb(f"{name}_state", [P, S, D], F32, st)
                state_t = [sb(f"{name}_state_t{h}", [2 * D, PAIRS * P], F32, st) for h in range(2)]
                next_t = [sb(f"{name}_next_t{h}", [2 * D, PAIRS * P], F32, st) for h in range(2)]

            def ps(k):
                return st.enter_context(nc.psum_tensor(f"{name}_ps_{k}", [2 * D, 512], F32))

            ps_merged = ps("merged")
            if mlp:
                ps_attr, ps_h0, ps_o0, ps_st, ps_h1, ps_o1, ps_nt = [ps(k) for k in ("attr", "h0", "o0", "st", "h1", "o1", "nt")]

            gathered = [sem(f"{name}_gathered{h}") for h in range(4)]
            m = [Chain(main[h], base(main[h]), steps) for h in range(2)]
            d = [Chain(dedup[h], base(dedup[h]), dedup_steps) for h in range(2)]
            n_loads = len(used) + 1 + takes_attr + takes_weight + (kind == "mlp1")
            n_gathers = S * len(tables)
            consumed = "product" if not mlp else "hidden1"
            b_loaded = [base(x) for x in loaded]
            b_scattered = [base(x) for x in scattered]
            b_stored = [base(x) for x in stored]
            half = UNITS // 2

            def loads_of(h, i):
                return i * (16 * n_loads) + (b_loaded[h] + 16 * n_loads)

            def gathers_of(h, i):
                return i * (16 * n_gathers) + 16 * n_gathers

            def scatters_of(t, i, h, ago):
                return i * 32 + (b_scattered[t] + 16 * (h - ago + 1))

            def stores_of(h, i):
                return i * 16 + (b_stored[h] + 16)

            if mlp:
                windowed = windowed_mlp(st, name, tables, agg[rnd], rnd, gathered,
                                        [ps_h0, ps_attr, ps_h1, ps_merged, ps_o0, ps_o1, ps_st, ps_nt])
            elif kind == "message":
                windowed = windowed_message(st, name, tables, agg, [ps_merged, ps("merged1")])
            else:
                windowed = windowed_pass(st, name, tables, width, agg[0], kind, gathered, ps_merged,
                                         [ps(f"enc{k}") for k in range(4)] if kind == "conv" else None)

            def either(eng, engine, general):
                unordered = eng.value_load(disorder[0:1, 0:1], min_val=0, max_val=1)
                with eng.If_eq(eng.to_reg(unordered), 0):
                    windowed[engine](eng)
                with eng.Else():
                    general()

            block = st.enter_context(nc.Block())

            @block.sync
            def _(sp):
                def store_state(i, h):
                    sp.wait_ge(m[h].sem, m[h].at("next_t", i))
                    sp.sem_inc(sp_tick, 1)
                    sp.dma_start(edge_t[bass.ds(i * 2 + h, 1), :, :].squeeze(0), next_t[h][:, :]).then_inc(stored[h], 16)

                def unit(i, h, first):
                    u = bass.ds(i * 2 + h, 1)
                    if not first:
                        sp.wait_ge(m[h].sem, m[h].end(i - 1))
                        sp.sem_inc(sp_tick, 1)
                        sp.wait_ge(d[h].sem, d[h].end(i - 1))
                        sp.sem_inc(sp_tick, 1)
                        sp.wait_ge(gathered[h], gathers_of(h, i - 1))
                        sp.sem_inc(sp_tick, 1)
                        if kind == "mlp0":
                            store_state(i - 1, h)
                    for e in used:
                        sp.dma_start(J[e][h][:, :], ends[e][u].squeeze(0)).then_inc(loaded[h], 16)
                    sp.dma_start(B[h][:, :], ends[target][u].rearrange("u p s -> u (p s)").broadcast_to([P, P * S]))\
                      .then_inc(loaded[h], 16)
                    if takes_attr:
                        sp.dma_start(attr[h][:, :], attr_u[u].squeeze(0)).then_inc(loaded[h], 16)
                    if takes_weight:
                        sp.dma_start(wt[h][:, :], weight_u[u].squeeze(0)).then_inc(loaded[h], 16)
                    if kind == "mlp1":
                        sp.dma_start(state_t[h][:, :], edge_t[u].squeeze(0)).then_inc(loaded[h], 16)

                def body(i, first):
                    for h in range(2):
                        unit(i, h, first)

                def general():
                    rolled(sp, half, body)
                    if kind == "mlp0":
                        for h in range(2):
                            store_state(half - 1, h)
                        for h in range(2):
                            sp.wait_ge(stored[h], stores_of(h, half - 1))

                either(sp, "sync", general)

            @block.gpsimd
            def _(pool):
                def gathers(i, h, first):
                    pool.wait_ge(loaded[h], loads_of(h, i))
                    pool.sem_inc(pool_tick, 1)
                    if not first:
                        pool.wait_ge(m[h].sem, m[h].at(consumed, i - 1))
                        pool.sem_inc(pool_tick, 1)
                    for n, (table, _, end) in enumerate(tables):
                        for t in range(S):
                            pool.indirect_dma_start(
                                G[n][h][:, t, :], None, table,
                                bass.IndirectOffsetOnAxis(ap=J[end][h][:, t:t + 1], axis=0),
                            ).then_inc(gathered[h], 16)

                def scatters(i, h, first):
                    pool.wait_ge(m[h].sem, m[h].at("merged_out", i))
                    pool.sem_inc(pool_tick, 1)
                    for t in range(S):
                        if not (first and h == 0):
                            pool.wait_ge(scattered[t], scatters_of(t, i, h, 1))
                            pool.sem_inc(pool_tick, 1)
                        pool.indirect_dma_start(
                            agg[t], bass.IndirectOffsetOnAxis(ap=index[h][:, t:t + 1], axis=0), SV[h][:, t, :], None,
                            compute_op=ALU.add).then_inc(scattered[t], 16)

                def general():
                    gathers(0, 0, True)

                    def body(i, first, last=False):
                        gathers(i, 1, first)
                        scatters(i, 0, first)
                        if not last:
                            gathers(i + 1, 0, False)
                        scatters(i, 1, first)

                    body(0, True)
                    with pool.Fori(1, half - 1) as i:
                        body(i, False)
                    body(half - 1, False, True)
                    for t in range(S):
                        pool.wait_ge(scattered[t], scatters_of(t, half, 0, 1))

                either(pool, "gpsimd", general)

            @block.vector
            def _(dve):
                def targets(i, h, first):
                    q = d[h]
                    Jt = J[target][h]
                    dve.wait_ge(loaded[h], loads_of(h, i))
                    if not first or h == 1:
                        dve.wait_ge(d[1 - h].sem, d[1 - h].end(i - (1 - h)))
                    if not first:
                        dve.wait_ge(m[h].sem, m[h].at("merged", i - 1))
                    dve.tensor_tensor(same[h][:, :, :], bc3(Jt[:, :], [P, S, P]),
                                      B[h][:, :].rearrange("p (q s) -> p s q", s=S), ALU.is_equal).then_inc(q.sem, 1)
                    dve.wait_ge(q.sem, q.at("equal", i))
                    dve.tensor_tensor(masked[:, :, :], same[h][:, :, :],
                                      earlier[:, :].unsqueeze(1).broadcast_to([P, S, P]), ALU.mult).then_inc(q.sem, 1)
                    dve.wait_ge(q.sem, q.at("masked", i))
                    dve.tensor_reduce(rep[:, :], masked[:, :, :], axis=AX.X, op=ALU.max).then_inc(q.sem, 1)
                    dve.wait_ge(q.sem, q.at("repeated", i))
                    dve.tensor_scalar(alt[:, :], Jt[:, :], -1.0, spare[:, :], ALU.mult, ALU.add).then_inc(q.sem, 1)
                    dve.wait_ge(q.sem, q.at("to_spare", i))
                    dve.tensor_tensor(alt[:, :], alt[:, :], rep[:, :], ALU.mult).then_inc(q.sem, 1)
                    dve.wait_ge(q.sem, q.at("if_repeated", i))
                    if not first:
                        for t in range(S):
                            dve.wait_ge(scattered[t], scatters_of(t, i, h, 2))
                    dve.tensor_tensor(index[h][:, :], alt[:, :], Jt[:, :], ALU.add).then_inc(q.sem, 1)

                def body(i, first):
                    for h in range(2):
                        q = m[h]
                        targets(i, h, first)
                        if kind in ("message", "conv"):
                            dve.wait_ge(loaded[h], loads_of(h, i))
                            dve.wait_ge(gathered[h], gathers_of(h, i))
                            if not first or h == 1:
                                dve.wait_ge(m[1 - h].sem, m[1 - h].at("summed", i - (1 - h)))
                            dve.tensor_tensor(prod[:, :, :], G[0][h][:, :, :].rearrange("p s (a f) -> p (s a) f", f=F),
                                              bc3(attr[h][:, :], [P, S * A, F]), ALU.mult).then_inc(q.sem, 1)
                            dve.wait_ge(q.sem, q.at("product", i))
                            if kind == "message":
                                if not first or h == 1:
                                    dve.wait_ge(m[1 - h].sem, m[1 - h].at("silu", i - (1 - h)))
                                to = summed[:, :, :]
                            else:
                                if not first:
                                    dve.wait_ge(m[h].sem, m[h].at("merged", i - 1))
                                to = V[h][:, :, 0:F]
                            dve.tensor_reduce(to, prod[:, :, :].rearrange("p (s a) f -> p s f a", a=A), axis=AX.X,
                                              op=ALU.add).then_inc(q.sem, 1)
                            if kind == "conv":
                                dve.wait_ge(q.sem, q.at("summed", i))
                                dve.tensor_copy(V[h][:, :, F:F + 1], wt[h][:, :].unsqueeze(2)).then_inc(q.sem, 1)
                        if kind == "gcn":
                            dve.wait_ge(loaded[h], loads_of(h, i))
                            dve.wait_ge(gathered[h], gathers_of(h, i))
                            if not first:
                                dve.wait_ge(m[h].sem, m[h].at("merged", i - 1))
                            dve.tensor_tensor(V[h][:, :, :], G[0][h][:, :, :], bc3(wt[h][:, :], [P, S, F]),
                                              ALU.mult).then_inc(q.sem, 1)
                        if kind == "mlp0":
                            dve.wait_ge(q.sem, q.at("attr_turned", i))
                            dve.tensor_copy(attr_t[:, :], ps_attr[0:S * A, 0:P]).then_inc(q.sem, 1)
                            norm_stats(dve, q, "enc", i, squares[:, :, :], D, S, stat)
                            dve.wait_ge(q.sem, q.at(rsqrt_names("enc")[-1], i))
                            dve.tensor_tensor(state[:, :, :], ps_o0[0:P, 0:S * D].rearrange("p (s d) -> p s d", d=D),
                                              bc3(stat[:, 0, 0:S], [P, S, D]), ALU.mult).then_inc(q.sem, 1)
                            dve.wait_ge(q.sem, q.at("enc_norm", i))
                            dve.tensor_tensor(state[:, :, :], state[:, :, :],
                                              gb["eenc"][:, 0, :].unsqueeze(1).broadcast_to([P, S, D]), ALU.mult).then_inc(q.sem, 1)
                            dve.wait_ge(q.sem, q.at("enc_gain", i))
                            dve.tensor_tensor(state[:, :, :], state[:, :, :],
                                              gb["eenc"][:, 1, :].unsqueeze(1).broadcast_to([P, S, D]), ALU.add).then_inc(q.sem, 1)
                        if mlp:
                            norm_stats(dve, q, "upd", i, squares[:, :, :], D, S, stat)
                            if not first:
                                dve.wait_ge(m[h].sem, m[h].at("merged", i - 1))
                            dve.wait_ge(q.sem, q.at(rsqrt_names("upd")[-1], i))
                            dve.tensor_tensor(V[h][:, :, :], ps_o1[0:P, 0:S * D].rearrange("p (s d) -> p s d", d=D),
                                              bc3(stat[:, 0, 0:S], [P, S, D]), ALU.mult).then_inc(q.sem, 1)
                            dve.wait_ge(q.sem, q.at("upd_norm", i))
                            dve.tensor_tensor(V[h][:, :, :], V[h][:, :, :],
                                              gb[f"eblk_{rnd}"][:, 0, :].unsqueeze(1).broadcast_to([P, S, D]), ALU.mult).then_inc(q.sem, 1)
                            dve.wait_ge(q.sem, q.at("upd_gain", i))
                            dve.tensor_tensor(V[h][:, :, :], V[h][:, :, :],
                                              gb[f"eblk_{rnd}"][:, 1, :].unsqueeze(1).broadcast_to([P, S, D]), ALU.add).then_inc(q.sem, 1)
                        if kind == "mlp0":
                            dve.wait_ge(q.sem, q.at("upd_bias", i))
                            dve.tensor_tensor(V[h][:, :, :], V[h][:, :, :], state[:, :, :], ALU.add).then_inc(q.sem, 1)

                def general():
                    rolled(dve, half, body)

                either(dve, "vector", general)

            @block.scalar
            def _(act):
                def body(i, first):
                    for h in range(2):
                        q = m[h]
                        if kind == "message":
                            act.wait_ge(q.sem, q.at("summed", i))
                            if not first:
                                act.wait_ge(m[h].sem, m[h].at("merged", i - 1))
                            act.activation(V[h][:, :, :], summed[:, :, :], ACT.Silu,
                                           scale=float(1 / np.float32(np.sqrt(F * A)))).then_inc(q.sem, 1)
                        if kind == "mlp0":
                            act.wait_ge(q.sem, q.at("hidden0", i))
                            act.activation(act0[:, :], ps_h0[:, 0:PAIRS * P], ACT.Silu, bias=col["eenc0"][:, :]).then_inc(q.sem, 1)
                            act.wait_ge(q.sem, q.at("out0", i))
                            act.activation(squares[:, :, :].rearrange("p s d -> p (s d)"), ps_o0[0:P, 0:S * D], ACT.Square).then_inc(q.sem, 1)
                            act.wait_ge(q.sem, q.at("state_turned", i))
                            act.activation(state_t[0][:, :], ps_st[:, 0:PAIRS * P], ACT.Copy).then_inc(q.sem, 1)
                        if mlp:
                            act.wait_ge(q.sem, q.at("hidden1", i))
                            act.activation(act1[:, :], ps_h1[:, 0:PAIRS * P], ACT.Silu).then_inc(q.sem, 1)
                            act.wait_ge(q.sem, q.at("out1", i))
                            act.activation(squares[:, :, :].rearrange("p s d -> p (s d)"), ps_o1[0:P, 0:S * D], ACT.Square).then_inc(q.sem, 1)
                        if kind == "mlp0":
                            act.wait_ge(q.sem, q.at("next_turned", i))
                            if not first:
                                act.wait_ge(stored[h], stores_of(h, i - 1))
                            act.activation(next_t[h][:, :], ps_nt[:, 0:PAIRS * P], ACT.Copy).then_inc(q.sem, 1)
                        act.wait_ge(q.sem, q.at("merged", i))
                        act.wait_ge(d[h].sem, d[h].at("index", i))
                        act.activation(SV[h][:, :, :].rearrange("p s w -> p (s w)"), ps_merged[0:P, 0:S * width], ACT.Copy).then_inc(q.sem, 1)

                def general():
                    rolled(act, half, body)

                either(act, "scalar", general)

            @block.tensor
            def _(pe):
                def body(i, first):
                    for h in range(2):
                        q = m[h]
                        if kind == "mlp0":
                            pe.wait_ge(loaded[h], loads_of(h, i))
                            if not first or h == 1:
                                pe.wait_ge(m[1 - h].sem, m[1 - h].end(i - (1 - h)))
                            pe.matmul(ps_attr[0:S * A, 0:P], attr[h][:, :], ident[:, :], start=True, stop=True).then_inc(q.sem, 1)
                            pe.wait_ge(q.sem, q.at("attr_t", i))
                            for k in range(PAIRS):
                                last = pe.matmul(ps_h0[:, k * P:(k + 1) * P], w_eenc0[:, k * 2 * D:(k + 1) * 2 * D],
                                                 attr_t[:, :], start=True, stop=True)
                            last.then_inc(q.sem, 1)
                            pe.wait_ge(q.sem, q.at("act0", i))
                            pe.matmul(ps_o0[0:P, 0:S * D], ones[:, :], row["eenc1"][:, :], start=True, stop=False)
                            for k in range(PAIRS):
                                last = pe.matmul(ps_o0[0:P, k * 2 * D:(k + 1) * 2 * D], act0[:, k * P:(k + 1) * P],
                                                 W["eenc1"][:, :], start=False, stop=k == PAIRS - 1)
                            last.then_inc(q.sem, 1)
                            pe.wait_ge(q.sem, q.at("enc_bias", i))
                            for k in range(PAIRS):
                                last = pe.matmul(ps_st[:, k * P:(k + 1) * P],
                                                 state[:, 2 * k:2 * k + 2, :].rearrange("p s d -> p (s d)"), ident[:, :],
                                                 start=True, stop=True)
                            last.then_inc(q.sem, 1)
                            pe.wait_ge(q.sem, q.at("state_t", i))
                        elif mlp:
                            pe.wait_ge(loaded[h], loads_of(h, i))
                            if not first or h == 1:
                                pe.wait_ge(m[1 - h].sem, m[1 - h].end(i - (1 - h)))
                        if mlp:
                            pe.wait_ge(gathered[h], gathers_of(h, i))
                            pe.matmul(ps_h1[:, 0:PAIRS * P], W[f"eblk_e{rnd}"][:, :],
                                      state_t[0 if kind == "mlp0" else h][:, :], start=True, stop=False)
                            for n in range(2):
                                for k in range(PAIRS):
                                    last = pe.matmul(ps_h1[:, k * P:(k + 1) * P],
                                                     G[n][h][:, 2 * k:2 * k + 2, :].rearrange("p s d -> p (s d)"),
                                                     ident[:, :], start=False, stop=n == 1 and k == PAIRS - 1)
                            last.then_inc(q.sem, 1)
                            pe.wait_ge(q.sem, q.at("act1", i))
                            pe.matmul(ps_o1[0:P, 0:S * D], ones[:, :], row[f"eblk1_{rnd}"][:, :], start=True, stop=False)
                            for k in range(PAIRS):
                                last = pe.matmul(ps_o1[0:P, k * 2 * D:(k + 1) * 2 * D], act1[:, k * P:(k + 1) * P],
                                                 W[f"eblk1{rnd}"][:, :], start=False, stop=k == PAIRS - 1)
                            last.then_inc(q.sem, 1)
                        if kind == "mlp0":
                            pe.wait_ge(q.sem, q.at("state_added", i))
                            for k in range(PAIRS):
                                last = pe.matmul(ps_nt[:, k * P:(k + 1) * P],
                                                 V[h][:, 2 * k:2 * k + 2, :].rearrange("p s d -> p (s d)"), ident[:, :],
                                                 start=True, stop=True)
                            last.then_inc(q.sem, 1)
                        pe.wait_ge(q.sem, q.before("merged", i))
                        pe.wait_ge(d[h].sem, d[h].at("equal", i))
                        if not first or h == 1:
                            pe.wait_ge(m[1 - h].sem, m[1 - h].end(i - (1 - h)))
                        for t in range(S):
                            last = pe.matmul(ps_merged[0:P, t * width:(t + 1) * width], same[h][:, t, :], V[h][:, t, :],
                                             start=True, stop=True)
                        last.then_inc(q.sem, 1)

                def general():
                    rolled(pe, half, body)

                either(pe, "tensor", general)

        for h in range(2):
            advance(main[h], m[h].n * half)
            advance(dedup[h], d[h].n * half)
            advance(loaded[h], 16 * n_loads * half)
            if kind == "mlp0":
                advance(stored[h], 16 * half)
        for t in range(S):
            advance(scattered[t], 16 * UNITS)

    def node_pass(name, loads, tables, stores, steps, dve_body, act_body, pe_body, bufs, big):
        q = [Chain(node_chain[u], base(node_chain[u]), steps) for u in range(K)]
        b_loaded, b_stored = base(node_loaded), base(node_stored)
        n_loads = len(loads) + S * (tables is not None)

        def ready(u, step, i):
            if step == steps[0]:
                return node_loaded, i * (16 * n_loads) + (b_loaded + 16 * n_loads)
            return q[u].sem, q[u].before(step, i)

        block = bufs.enter_context(nc.Block())

        @block.sync
        def _(sp):
            if tables is not None:
                agg, in_use = tables
                sp.wait_ge(tables_cleared[name], 1)
                unordered = sp.to_reg(sp.value_load(disorder[0:1, 0:1], min_val=0, max_val=1))

                def load_table(i, k):
                    sp.dma_start(big["tab"][:, :, k, :], node_rows(agg[k])[bass.ds(i, 1)].squeeze(0)).then_inc(node_loaded, 16)

                def load_tables(i):
                    for k in range(in_use):
                        load_table(i, k)
                    if in_use < S:
                        with sp.If_eq(unordered, 0):
                            sp.sem_inc(node_loaded, 16 * (S - in_use))
                        with sp.Else():
                            for k in range(in_use, S):
                                load_table(i, k)

                load_tables(0)

            def body(i, first, last=False):
                if not first:
                    for u in range(K):
                        sp.wait_ge(q[u].sem, q[u].end(i - 1))
                        sp.sem_inc(sp_tick, 1)
                    sp.wait_ge(node_stored, i * (16 * len(stores)) + b_stored)
                    sp.sem_inc(sp_tick, 1)
                for tile, rows_ in loads:
                    sp.dma_start(tile, node_rows(rows_)[bass.ds(i, 1)].squeeze(0)).then_inc(node_loaded, 16)
                if tables is not None and not last:
                    for u in range(K):
                        sp.wait_ge(q[u].sem, q[u].at("agg_sum", i))
                        sp.sem_inc(sp_tick, 1)
                    load_tables(i + 1)
                for rows_, tile, step in stores:
                    for u in range(K):
                        sp.wait_ge(q[u].sem, q[u].at(step, i))
                        sp.sem_inc(sp_tick, 1)
                    sp.dma_start(node_rows(rows_)[bass.ds(i, 1)].squeeze(0), by_unit(big[tile])).then_inc(node_stored, 16)

            body(0, True)
            with sp.Fori(1, NODE_TURNS - 1) as i:
                body(i, False)
            body(NODE_TURNS - 1, False, True)
            sp.wait_ge(node_stored, b_stored + 16 * len(stores) * NODE_TURNS)

        @block.vector
        def _(dve):
            if tables is not None:
                dve.memset(big["tab"][:, :, :, :], 0.0).then_inc(tables_cleared[name], 1)
            rolled(dve, NODE_TURNS, lambda i, first: dve_body(dve, q, ready, i))

        if act_body is not None:
            @block.scalar
            def _(act):
                rolled(act, NODE_TURNS, lambda i, first: act_body(act, q, ready, i))

        if pe_body is not None:
            @block.tensor
            def _(pe):
                rolled(pe, NODE_TURNS, lambda i, first: pe_body(pe, q, ready, i))

        for u in range(K):
            advance(node_chain[u], q[u].n * NODE_TURNS)
        advance(node_loaded, 16 * n_loads * NODE_TURNS)
        advance(node_stored, 16 * len(stores) * NODE_TURNS)

    tables_cleared = {f"n{k}": sem(f"tables_cleared{k}") for k in range(1, 7)}

    def node_newton(dve, q, ready, p, i, value, out_, t):
        names = rsqrt_names(p)

        for u in range(K):
            dve.wait_ge(*ready(u, names[1], i))
            dve.tensor_scalar(t(u).bitcast(I32), value(u).bitcast(I32), 1, None, ALU.logical_shift_right).then_inc(q[u].sem, 1)
        for u in range(K):
            dve.wait_ge(*ready(u, names[2], i))
            dve.tensor_scalar(out_(u).bitcast(I32), t(u).bitcast(I32), -1.0, float(0x5F3759DF), ALU.mult, ALU.add).then_inc(q[u].sem, 1)
        for r in range(3):
            for u in range(K):
                dve.wait_ge(*ready(u, names[3 + 3 * r], i))
                dve.scalar_tensor_tensor(out=t(u), in0=out_(u), scalar=-0.5, in1=value(u), op0=ALU.mult, op1=ALU.mult).then_inc(q[u].sem, 1)
            for u in range(K):
                dve.wait_ge(*ready(u, names[4 + 3 * r], i))
                dve.tensor_tensor(t(u), t(u), out_(u), ALU.mult).then_inc(q[u].sem, 1)
            for u in range(K):
                dve.wait_ge(q[u].sem, q[u].at(names[4 + 3 * r], i))
                dve.scalar_tensor_tensor(out=out_(u), in0=t(u), scalar=1.5, in1=out_(u), op0=ALU.add, op1=ALU.mult).then_inc(q[u].sem, 1)

    def node_norm_stats(dve, q, ready, p, i, squares, width, v):
        for u in range(K):
            dve.wait_ge(*ready(u, f"{p}_var", i))
            dve.tensor_reduce(v[u][:, 1, 0:C], squares[u], axis=AX.X, op=ALU.add).then_inc(q[u].sem, 1)
        for u in range(K):
            dve.wait_ge(*ready(u, f"{p}_rsqrt0", i))
            dve.tensor_scalar(v[u][:, 1, 0:C], v[u][:, 1, 0:C], 1.0 / width, EPS, ALU.mult, ALU.add).then_inc(q[u].sem, 1)
        node_newton(dve, q, ready, p, i, lambda u: v[u][:, 1, 0:C], lambda u: v[u][:, 0, 0:C], lambda u: v[u][:, 2, 0:C])

    def ln_relu(dve, q, ready, p, i, x, centered, squares, v, h):
        for u in range(K):
            dve.wait_ge(*ready(u, f"{p}_sum", i))
            dve.tensor_reduce(v[u][:, 1, 0:C], x[u], axis=AX.X, op=ALU.add).then_inc(q[u].sem, 1)
        for u in range(K):
            dve.wait_ge(*ready(u, f"{p}_mean", i))
            dve.tensor_scalar(v[u][:, 1, 0:C], v[u][:, 1, 0:C], -1.0 / F, None, ALU.mult).then_inc(q[u].sem, 1)
        for u in range(K):
            dve.wait_ge(*ready(u, f"{p}_center", i))
            dve.tensor_tensor(centered[u], x[u], bc3(v[u][:, 1, 0:C], [P, C, F]), ALU.add).then_inc(q[u].sem, 1)
        for u in range(K):
            dve.wait_ge(*ready(u, f"{p}_square", i))
            dve.tensor_tensor(squares[u], centered[u], centered[u], ALU.mult).then_inc(q[u].sem, 1)
        node_norm_stats(dve, q, ready, p, i, squares, F, v)
        for u in range(K):
            dve.wait_ge(*ready(u, f"{p}_norm", i))
            dve.scalar_tensor_tensor(out=h[u], in0=centered[u], scalar=0.0, in1=bc3(v[u][:, 0, 0:C], [P, C, F]),
                                     op0=ALU.max, op1=ALU.mult).then_inc(q[u].sem, 1)

    def ln_affine(dve, q, ready, p, i, x_ps, squares, v, k, o):
        node_norm_stats(dve, q, ready, p, i, squares, D, v)
        for u in range(K):
            dve.wait_ge(*ready(u, f"{p}_norm", i))
            dve.tensor_tensor(o[u], x_ps[u][0:P, 0:C * D].rearrange("p (c d) -> p c d", d=D), bc3(v[u][:, 0, 0:C], [P, C, D]),
                              ALU.mult).then_inc(q[u].sem, 1)
        for u in range(K):
            dve.wait_ge(*ready(u, f"{p}_gain", i))
            dve.tensor_tensor(o[u], o[u], gb[k][:, 0, :].unsqueeze(1).broadcast_to([P, C, D]), ALU.mult).then_inc(q[u].sem, 1)
        for u in range(K):
            dve.wait_ge(*ready(u, f"{p}_bias", i))
            dve.tensor_tensor(o[u], o[u], gb[k][:, 1, :].unsqueeze(1).broadcast_to([P, C, D]), ALU.add).then_inc(q[u].sem, 1)

    def flat(ap):
        return ap.rearrange("p a b -> p (a b)")

    def by_unit(ap):
        return ap[:, :, :] if len(ap.shape) == 3 else ap[:, :, :, :].rearrange("p u a b -> p u (a b)")

    def turn_pairs(pe, ps_, frm):
        for k in range(C // 2):
            last = pe.matmul(ps_[:, k * P:(k + 1) * P], flat(frm[:, 2 * k:2 * k + 2, :]), ident[:, :], start=True, stop=True)
        return last

    def by_node(pe, ps_, turned, w, width, bias=None):
        if bias is not None:
            pe.matmul(ps_[0:P, 0:C * width], ones[:, :], bias[:, 0:C * width], start=True, stop=False)
        for k in range(C // 2):
            last = pe.matmul(ps_[0:P, k * 2 * width:(k + 1) * 2 * width], turned[:, k * P:(k + 1) * P], w,
                             start=bias is None, stop=bias is None or k == C // 2 - 1)
        return last

    TW = C * F
    NORM_UPD = float(1 / np.float32(np.sqrt(F * F)))
    NORM_LIN = float(1 / np.float32(np.sqrt(F)))

    def pass_scope(name, tiles):
        st = ExitStack()
        big = {k: sb(f"{name}_{k}", [shape[0], K] + shape[1:], F32, st) for k, shape in tiles.items()}
        t = {k: [tile[:, u] for u in range(K)] for k, tile in big.items()}
        ps = [st.enter_context(nc.psum_tensor(f"{name}_ps{u}", [2 * D, 512], F32)) for u in range(K)]
        return st, t, ps, big

    st, t, ps, big = pass_scope("n0", dict(x=[P, C, F], c=[P, C, F], sq=[P, C, F], v=[P, 3, 8], h=[P, C, F], ht=[TW, P],
                                      y=[P, 512]))
    with st:
        def n0_dve(dve, q, ready, i, t=t):
            ln_relu(dve, q, ready, "x", i, t["x"], t["c"], t["sq"], t["v"], t["h"])

        def n0_act(act, q, ready, i, t=t, ps=ps):
            for u in range(K):
                act.wait_ge(*ready(u, "h_t", i))
                act.activation(t["ht"][u], ps[u][0:TW, 0:P], ACT.Copy).then_inc(q[u].sem, 1)
            for u in range(K):
                act.wait_ge(*ready(u, "y_out", i))
                act.activation(t["y"][u], ps[u][0:P, :], ACT.Copy).then_inc(q[u].sem, 1)

        def n0_pe(pe, q, ready, i, t=t, ps=ps):
            for u in range(K):
                pe.wait_ge(*ready(u, "h_turned", i))
                pe.matmul(ps[u][0:TW, 0:P], flat(t["h"][u]), ident[:, :], start=True, stop=True).then_inc(q[u].sem, 1)
            for u in range(K):
                pe.wait_ge(*ready(u, "y", i))
                pe.matmul(ps[u][0:P, :], t["ht"][u], w_msg[:, :], start=True, stop=True).then_inc(q[u].sem, 1)

        node_pass("n0", [(by_unit(big["x"]), ins["x"])], None,
                  [(h0_d, "h", "x_norm"), (y0, "y", "y_out")],
                  ln_names("x", False) + ["h_turned", "h_t", "y", "y_out"], n0_dve, n0_act, n0_pe, st, big)

    edge_pass("e0", [(y0, A * F, "dst")], "src", F, agg0, "message")

    st, t, ps, big = pass_scope("n1", dict(x=[P, C, F], h0=[P, C, F], tab=[P, S, C * F], ag=[P, TW], agt=[TW, P], al=[P, C, F],
                                      h0t=[TW, P], prod=[P, C * F, F], u=[P, C, F], us=[P, C, F], ust=[TW, P],
                                      x1=[P, C, F], c=[P, C, F], sq=[P, C, F], v=[P, 3, 8], h=[P, C, F], ht=[TW, P],
                                      y=[P, 512]))
    with st:
        def n1_dve(dve, q, ready, i, t=t, ps=ps):
            for u in range(K):
                dve.wait_ge(*ready(u, "agg_sum", i))
                dve.tensor_reduce(t["ag"][u], t["tab"][u].rearrange("p t x -> p x t"), axis=AX.X, op=ALU.add).then_inc(q[u].sem, 1)
            for u in range(K):
                dve.wait_ge(*ready(u, "upd_prod0", i))
                dve.tensor_tensor(t["prod"][u][:, 0:2 * F, :], ps[u][0:P, :].rearrange("p (a f) -> p a f", f=F),
                                  bc3(flat(t["al"][u][:, 0:2, :]), [P, 2 * F, F]), ALU.mult).then_inc(q[u].sem, 1)
            for u in range(K):
                dve.wait_ge(*ready(u, "upd_prod1", i))
                dve.tensor_tensor(t["prod"][u][:, 2 * F:4 * F, :], ps[u][0:P, :].rearrange("p (a f) -> p a f", f=F),
                                  bc3(flat(t["al"][u][:, 2:4, :]), [P, 2 * F, F]), ALU.mult).then_inc(q[u].sem, 1)
            for u in range(K):
                dve.wait_ge(*ready(u, "upd_sum", i))
                dve.tensor_reduce(t["u"][u], t["prod"][u].rearrange("p (c h) k -> p c k h", c=C), axis=AX.X,
                                  op=ALU.add).then_inc(q[u].sem, 1)
            for u in range(K):
                dve.wait_ge(*ready(u, "x_upd", i))
                dve.scalar_tensor_tensor(out=flat(t["x1"][u]), in0=ps[u][0:P, 0:TW], scalar=NORM_LIN,
                                         in1=flat(t["h0"][u]), op0=ALU.mult, op1=ALU.add).then_inc(q[u].sem, 1)
            for u in range(K):
                dve.wait_ge(*ready(u, "x_new", i))
                dve.tensor_tensor(t["x1"][u], t["x1"][u], t["x"][u], ALU.add).then_inc(q[u].sem, 1)
            ln_relu(dve, q, ready, "x", i, t["x1"], t["c"], t["sq"], t["v"], t["h"])

        def n1_act(act, q, ready, i, t=t, ps=ps):
            for u in range(K):
                act.wait_ge(*ready(u, "agg_t", i))
                act.activation(t["agt"][u], ps[u][0:TW, 0:P], ACT.Copy).then_inc(q[u].sem, 1)
            for u in range(K):
                act.wait_ge(*ready(u, "agg_scaled", i))
                act.activation(flat(t["al"][u]), ps[u][0:P, 0:TW], ACT.Copy, scale=NORM_LIN).then_inc(q[u].sem, 1)
            for u in range(K):
                act.wait_ge(*ready(u, "h0_t", i))
                act.activation(t["h0t"][u], ps[u][0:TW, 0:P], ACT.Copy).then_inc(q[u].sem, 1)
            for u in range(K):
                act.wait_ge(*ready(u, "upd_silu", i))
                act.activation(t["us"][u], t["u"][u], ACT.Silu, scale=NORM_UPD).then_inc(q[u].sem, 1)
            for u in range(K):
                act.wait_ge(*ready(u, "u_t", i))
                act.activation(t["ust"][u], ps[u][0:TW, 0:P], ACT.Copy).then_inc(q[u].sem, 1)
            for u in range(K):
                act.wait_ge(*ready(u, "h_t", i))
                act.activation(t["ht"][u], ps[u][0:TW, 0:P], ACT.Copy).then_inc(q[u].sem, 1)
            for u in range(K):
                act.wait_ge(*ready(u, "y_out", i))
                act.activation(t["y"][u], ps[u][0:P, :], ACT.Copy).then_inc(q[u].sem, 1)

        def n1_pe(pe, q, ready, i, t=t, ps=ps):
            for u in range(K):
                pe.wait_ge(*ready(u, "agg_turned", i))
                pe.matmul(ps[u][0:TW, 0:P], t["ag"][u], ident[:, :], start=True, stop=True).then_inc(q[u].sem, 1)
            for u in range(K):
                pe.wait_ge(*ready(u, "agg_lin", i))
                pe.matmul(ps[u][0:P, 0:TW], t["agt"][u], w_msg_lin[:, :], start=True, stop=True).then_inc(q[u].sem, 1)
            for u in range(K):
                pe.wait_ge(*ready(u, "h0_turned", i))
                pe.matmul(ps[u][0:TW, 0:P], flat(t["h0"][u]), ident[:, :], start=True, stop=True).then_inc(q[u].sem, 1)
            for u in range(K):
                pe.wait_ge(*ready(u, "upd0", i))
                pe.matmul(ps[u][0:P, :], t["h0t"][u], w_upd[:, 0:C * F * F // 2], start=True, stop=True).then_inc(q[u].sem, 1)
            for u in range(K):
                pe.wait_ge(*ready(u, "upd1", i))
                pe.matmul(ps[u][0:P, :], t["h0t"][u], w_upd[:, C * F * F // 2:C * F * F], start=True, stop=True).then_inc(q[u].sem, 1)
            for u in range(K):
                pe.wait_ge(*ready(u, "u_turned", i))
                pe.matmul(ps[u][0:TW, 0:P], flat(t["us"][u]), ident[:, :], start=True, stop=True).then_inc(q[u].sem, 1)
            for u in range(K):
                pe.wait_ge(*ready(u, "u_lin", i))
                pe.matmul(ps[u][0:P, 0:TW], t["ust"][u], w_upd_lin[:, :], start=True, stop=True).then_inc(q[u].sem, 1)
            for u in range(K):
                pe.wait_ge(*ready(u, "h_turned", i))
                pe.matmul(ps[u][0:TW, 0:P], flat(t["h"][u]), ident[:, :], start=True, stop=True).then_inc(q[u].sem, 1)
            for u in range(K):
                pe.wait_ge(*ready(u, "y", i))
                pe.matmul(ps[u][0:P, :], t["ht"][u], w_conv[:, :], start=True, stop=True).then_inc(q[u].sem, 1)

        node_pass("n1", [(by_unit(big["x"]), ins["x"]), (by_unit(big["h0"]), h0_d)], (agg0, S),
                  [(x1_d, "x1", "x_new"), (y1, "y", "y_out")],
                  ["agg_sum", "agg_turned", "agg_t", "agg_lin", "agg_scaled", "h0_turned", "h0_t", "upd0", "upd_prod0", "upd1", "upd_prod1",
                   "upd_sum", "upd_silu", "u_turned", "u_t", "u_lin", "x_upd", "x_new"]
                  + ln_names("x", False) + ["h_turned", "h_t", "y", "y_out"], n1_dve, n1_act, n1_pe, st, big)

    edge_pass("e1", [(y1, A * F, "src")], "dst", F + 1, agg1, "conv")

    send_recv = ["node_turned", "node_t", "send", "send_out", "recv", "recv_out"]

    def send_recv_act(act, q, ready, i, t, ps):
        for u in range(K):
            act.wait_ge(*ready(u, "node_t", i))
            act.activation(t["nt"][u], ps[u][:, 0:2 * P], ACT.Copy).then_inc(q[u].sem, 1)
        for u in range(K):
            act.wait_ge(*ready(u, "send_out", i))
            act.activation(flat(t["send"][u]), ps[u][0:P, 0:C * D], ACT.Copy).then_inc(q[u].sem, 1)
        for u in range(K):
            act.wait_ge(*ready(u, "recv_out", i))
            act.activation(flat(t["recv"][u]), ps[u][0:P, 0:C * D], ACT.Copy).then_inc(q[u].sem, 1)

    def send_recv_pe(pe, q, ready, i, t, ps, r, node):
        for u in range(K):
            pe.wait_ge(*ready(u, "node_turned", i))
            turn_pairs(pe, ps[u], t[node][u]).then_inc(q[u].sem, 1)
        for u in range(K):
            pe.wait_ge(*ready(u, "send", i))
            by_node(pe, ps[u], t["nt"][u], W[f"eblk_s{r}"][:, :], D).then_inc(q[u].sem, 1)
        for u in range(K):
            pe.wait_ge(*ready(u, "recv", i))
            by_node(pe, ps[u], t["nt"][u], W[f"eblk_r{r}"][:, :], D, row[f"eblk0_{r}"]).then_inc(q[u].sem, 1)

    st, t, ps, big = pass_scope("n2", dict(x=[P, C, F], tab=[P, S, C * (F + 1)], ag=[P, C, F + 1], cv=[P, C, F], deg=[P, C],
                                      dis=[P, C], tmp=[P, C], pos=[P, C], x2=[P, C, F], c=[P, C, F], sq=[P, C, F],
                                      v=[P, 3, 8], h=[P, C, F], ht=[TW, P], a=[2 * D, 2 * P], sqd=[P, C, D],
                                      n=[P, C, D], nt=[2 * D, 2 * P], send=[P, C, D], recv=[P, C, D]))
    with st:
        def n2_dve(dve, q, ready, i, t=t, ps=ps):
            for u in range(K):
                dve.wait_ge(*ready(u, "agg_sum", i))
                dve.tensor_reduce(flat(t["ag"][u]), t["tab"][u].rearrange("p t x -> p x t"), axis=AX.X, op=ALU.add).then_inc(q[u].sem, 1)
            for u in range(K):
                dve.wait_ge(*ready(u, "conv_bias", i))
                dve.tensor_tensor(t["cv"][u], t["ag"][u][:, :, 0:F], conv_bias[:, :].unsqueeze(1).broadcast_to([P, C, F]),
                                  ALU.add).then_inc(q[u].sem, 1)
            for u in range(K):
                dve.wait_ge(*ready(u, "x_new", i))
                dve.scalar_tensor_tensor(out=t["x2"][u], in0=t["cv"][u], scalar=0.0, in1=t["x"][u],
                                         op0=ALU.max, op1=ALU.add).then_inc(q[u].sem, 1)
            for u in range(K):
                dve.wait_ge(*ready(u, "degree", i))
                dve.tensor_scalar(t["deg"][u], t["ag"][u][:, :, F], 1.0, None, ALU.add).then_inc(q[u].sem, 1)
            for u in range(K):
                dve.wait_ge(*ready(u, "degree_positive", i))
                dve.tensor_scalar(t["pos"][u], t["deg"][u], 0.0, None, ALU.is_gt).then_inc(q[u].sem, 1)
            for u in range(K):
                dve.wait_ge(*ready(u, "dis_rsqrt0", i))
                dve.tensor_scalar(t["deg"][u], t["deg"][u], 1e-30, None, ALU.max).then_inc(q[u].sem, 1)
            node_newton(dve, q, ready, "dis", i, lambda u: t["deg"][u], lambda u: t["dis"][u], lambda u: t["tmp"][u])
            for u in range(K):
                dve.wait_ge(*ready(u, "dis", i))
                dve.tensor_tensor(t["dis"][u], t["dis"][u], t["pos"][u], ALU.mult).then_inc(q[u].sem, 1)
            ln_relu(dve, q, ready, "x", i, t["x2"], t["c"], t["sq"], t["v"], t["h"])
            ln_affine(dve, q, ready, "enc", i, ps, t["sqd"], t["v"], "nenc", t["n"])

        def n2_act(act, q, ready, i, t=t, ps=ps):
            for u in range(K):
                act.wait_ge(*ready(u, "h_t", i))
                act.activation(t["ht"][u], ps[u][0:TW, 0:P], ACT.Copy).then_inc(q[u].sem, 1)
            for u in range(K):
                act.wait_ge(*ready(u, "act", i))
                act.activation(t["a"][u], ps[u][:, 0:2 * P], ACT.Silu, bias=col["nenc0"][:, :]).then_inc(q[u].sem, 1)
            for u in range(K):
                act.wait_ge(*ready(u, "enc_square", i))
                act.activation(flat(t["sqd"][u]), ps[u][0:P, 0:C * D], ACT.Square).then_inc(q[u].sem, 1)
            send_recv_act(act, q, ready, i, t, ps)

        def n2_pe(pe, q, ready, i, t=t, ps=ps):
            for u in range(K):
                pe.wait_ge(*ready(u, "h_turned", i))
                pe.matmul(ps[u][0:TW, 0:P], flat(t["h"][u]), ident[:, :], start=True, stop=True).then_inc(q[u].sem, 1)
            for u in range(K):
                pe.wait_ge(*ready(u, "hidden", i))
                for k in range(2):
                    last = pe.matmul(ps[u][:, k * P:(k + 1) * P], w_nenc0[:, k * 2 * D:(k + 1) * 2 * D], t["ht"][u],
                                     start=True, stop=True)
                last.then_inc(q[u].sem, 1)
            for u in range(K):
                pe.wait_ge(*ready(u, "out", i))
                by_node(pe, ps[u], t["a"][u], W["nenc1"][:, :], D, row["nenc1"]).then_inc(q[u].sem, 1)
            send_recv_pe(pe, q, ready, i, t, ps, 0, "n")

        node_pass("n2", [(by_unit(big["x"]), x1_d)], (agg1, 1),
                  [(x2_d, "x2", "x_new"), (dis_d, "dis", "dis"),
                   (n0_d, "n", "enc_bias"),
                   (send_d[0], "send", "send_out"),
                   (recv_d[0], "recv", "recv_out")],
                  ["agg_sum", "conv_bias", "x_new", "degree", "degree_positive"] + rsqrt_names("dis") + ["dis"]
                  + ln_names("x", False) + ["h_turned", "h_t", "hidden", "act", "out"] + ln_names("enc", True)
                  + ["enc_gain", "enc_bias"] + send_recv, n2_dve, n2_act, n2_pe, st, big)

    edge_pass("e2", [(send_d[0], D, "src"), (recv_d[0], D, "dst")], "dst", D, agg2, "mlp0", 0)

    node_update = ["agg_sum", "prev_turned", "prev_t", "agg_turned", "agg_t", "hidden", "act", "out"] \
        + ln_names("upd", True) + ["upd_gain", "upd_bias", "node_new"]

    def node_update_dve(dve, q, ready, i, t, ps, r):
        for u in range(K):
            dve.wait_ge(*ready(u, "agg_sum", i))
            dve.tensor_reduce(flat(t["ag"][u]), t["tab"][u].rearrange("p t x -> p x t"), axis=AX.X, op=ALU.add).then_inc(q[u].sem, 1)
        ln_affine(dve, q, ready, "upd", i, ps, t["sqd"], t["v"], f"nblk_{r}", t["n"])
        for u in range(K):
            dve.wait_ge(*ready(u, "node_new", i))
            dve.tensor_tensor(t["n"][u], t["n"][u], t["prev"][u], ALU.add).then_inc(q[u].sem, 1)

    def node_update_act(act, q, ready, i, t, ps, r):
        for u in range(K):
            act.wait_ge(*ready(u, "prev_t", i))
            act.activation(t["pt"][u], ps[u][:, 0:2 * P], ACT.Copy).then_inc(q[u].sem, 1)
        for u in range(K):
            act.wait_ge(*ready(u, "agg_t", i))
            act.activation(t["agt"][u], ps[u][:, 0:2 * P], ACT.Copy).then_inc(q[u].sem, 1)
        for u in range(K):
            act.wait_ge(*ready(u, "act", i))
            act.activation(t["a"][u], ps[u][:, 0:2 * P], ACT.Silu, bias=col[f"nblk0_{r}"][:, :]).then_inc(q[u].sem, 1)
        for u in range(K):
            act.wait_ge(*ready(u, "upd_square", i))
            act.activation(flat(t["sqd"][u]), ps[u][0:P, 0:C * D], ACT.Square).then_inc(q[u].sem, 1)

    def node_update_pe(pe, q, ready, i, t, ps, r):
        for u in range(K):
            pe.wait_ge(*ready(u, "prev_turned", i))
            turn_pairs(pe, ps[u], t["prev"][u]).then_inc(q[u].sem, 1)
        for u in range(K):
            pe.wait_ge(*ready(u, "agg_turned", i))
            turn_pairs(pe, ps[u], t["ag"][u]).then_inc(q[u].sem, 1)
        for u in range(K):
            pe.wait_ge(*ready(u, "hidden", i))
            pe.matmul(ps[u][:, 0:2 * P], W[f"nblk_n{r}"][:, :], t["pt"][u], start=True, stop=False)
            pe.matmul(ps[u][:, 0:2 * P], W[f"nblk_a{r}"][:, :], t["agt"][u], start=False, stop=True).then_inc(q[u].sem, 1)
        for u in range(K):
            pe.wait_ge(*ready(u, "out", i))
            by_node(pe, ps[u], t["a"][u], W[f"nblk1{r}"][:, :], D, row[f"nblk1_{r}"]).then_inc(q[u].sem, 1)

    node_tiles = dict(prev=[P, C, D], tab=[P, S, C * D], ag=[P, C, D], pt=[2 * D, 2 * P], agt=[2 * D, 2 * P],
                      a=[2 * D, 2 * P], sqd=[P, C, D], v=[P, 3, 8], n=[P, C, D], nt=[2 * D, 2 * P])

    st, t, ps, big = pass_scope("n3", node_tiles | dict(send=[P, C, D], recv=[P, C, D]))
    with st:
        def n3_dve(dve, q, ready, i, t=t, ps=ps):
            node_update_dve(dve, q, ready, i, t, ps, 0)

        def n3_act(act, q, ready, i, t=t, ps=ps):
            node_update_act(act, q, ready, i, t, ps, 0)
            send_recv_act(act, q, ready, i, t, ps)

        def n3_pe(pe, q, ready, i, t=t, ps=ps):
            node_update_pe(pe, q, ready, i, t, ps, 0)
            send_recv_pe(pe, q, ready, i, t, ps, 1, "n")

        node_pass("n3", [(by_unit(big["prev"]), n0_d)], (agg2, 1),
                  [(n1_d, "n", "node_new"),
                   (send_d[1], "send", "send_out"),
                   (recv_d[1], "recv", "recv_out")],
                  node_update + send_recv, n3_dve, n3_act, n3_pe, st, big)

    edge_pass("e3", [(send_d[1], D, "src"), (recv_d[1], D, "dst")], "dst", D, agg2, "mlp1", 1)

    st, t, ps, big = pass_scope("n4", node_tiles | dict(x=[P, C, F], dis=[P, C], a2=[2 * D, 2 * P], x3=[P, C, F], c=[P, C, F],
                                                   sq=[P, C, F], h=[P, C, F], g=[P, C, F]))
    with st:
        def n4_dve(dve, q, ready, i, t=t, ps=ps):
            node_update_dve(dve, q, ready, i, t, ps, 1)
            for u in range(K):
                dve.wait_ge(*ready(u, "dec_bias", i))
                dve.tensor_tensor(t["x3"][u], ps[u][0:P, 0:TW].rearrange("p (c f) -> p c f", f=F),
                                  dec_b1[:, :].unsqueeze(1).broadcast_to([P, C, F]), ALU.add).then_inc(q[u].sem, 1)
            for u in range(K):
                dve.wait_ge(*ready(u, "x_new", i))
                dve.tensor_tensor(t["x3"][u], t["x3"][u], t["x"][u], ALU.add).then_inc(q[u].sem, 1)
            ln_relu(dve, q, ready, "x", i, t["x3"], t["c"], t["sq"], t["v"], t["h"])
            for u in range(K):
                dve.wait_ge(*ready(u, "h_dis", i))
                dve.tensor_tensor(t["g"][u], t["h"][u], bc3(t["dis"][u], [P, C, F]), ALU.mult).then_inc(q[u].sem, 1)

        def n4_act(act, q, ready, i, t=t, ps=ps):
            node_update_act(act, q, ready, i, t, ps, 1)
            for u in range(K):
                act.wait_ge(*ready(u, "node_t", i))
                act.activation(t["nt"][u], ps[u][:, 0:2 * P], ACT.Copy).then_inc(q[u].sem, 1)
            for u in range(K):
                act.wait_ge(*ready(u, "dec_act", i))
                act.activation(t["a2"][u], ps[u][:, 0:2 * P], ACT.Silu, bias=col["dec0"][:, :]).then_inc(q[u].sem, 1)

        def n4_pe(pe, q, ready, i, t=t, ps=ps):
            node_update_pe(pe, q, ready, i, t, ps, 1)
            for u in range(K):
                pe.wait_ge(*ready(u, "node_turned", i))
                turn_pairs(pe, ps[u], t["n"][u]).then_inc(q[u].sem, 1)
            for u in range(K):
                pe.wait_ge(*ready(u, "dec_hidden", i))
                pe.matmul(ps[u][:, 0:2 * P], W["dec0"][:, :], t["nt"][u], start=True, stop=True).then_inc(q[u].sem, 1)
            for u in range(K):
                pe.wait_ge(*ready(u, "dec", i))
                by_node(pe, ps[u], t["a2"][u], w_dec1[:, :], F).then_inc(q[u].sem, 1)

        node_pass("n4", [(by_unit(big["prev"]), n1_d), (by_unit(big["x"]), x2_d),
                         (by_unit(big["dis"]), dis_d)], (agg2, 2),
                  [(x3_d, "x3", "x_new"), (g1_d, "g", "h_dis")],
                  node_update + ["node_turned", "node_t", "dec_hidden", "dec_act", "dec", "dec_bias", "x_new"]
                  + ln_names("x", False) + ["h_dis"], n4_dve, n4_act, n4_pe, st, big)

    edge_pass("e4", [(g1_d, F, "src")], "dst", F, agg3, "gcn")

    def own_loop(dve, q, ready, i, t):
        for u in range(K):
            dve.wait_ge(*ready(u, "own", i))
            dve.tensor_tensor(flat(t["s"][u]), flat(t["s"][u]), flat(t["g"][u]), ALU.add).then_inc(q[u].sem, 1)
        for u in range(K):
            dve.wait_ge(*ready(u, "s_dis", i))
            dve.tensor_tensor(t["s"][u], t["s"][u], bc3(t["dis"][u], [P, C, F]), ALU.mult).then_inc(q[u].sem, 1)

    st, t, ps, big = pass_scope("n5", dict(tab=[P, S, TW], s=[P, C, F], g=[P, C, F], dis=[P, C], sT=[TW, P], a=[2 * TW, P],
                                      o=[P, C, F]))
    with st:
        def n5_dve(dve, q, ready, i, t=t, ps=ps):
            for u in range(K):
                dve.wait_ge(*ready(u, "agg_sum", i))
                dve.tensor_reduce(flat(t["s"][u]), t["tab"][u].rearrange("p t x -> p x t"), axis=AX.X, op=ALU.add).then_inc(q[u].sem, 1)
            own_loop(dve, q, ready, i, t)
            for u in range(K):
                dve.wait_ge(*ready(u, "o_dis", i))
                dve.tensor_tensor(t["o"][u], ps[u][0:P, 0:TW].rearrange("p (c f) -> p c f", f=F),
                                  bc3(t["dis"][u], [P, C, F]), ALU.mult).then_inc(q[u].sem, 1)

        def n5_act(act, q, ready, i, t=t, ps=ps):
            for u in range(K):
                act.wait_ge(*ready(u, "s_t", i))
                act.activation(t["sT"][u], ps[u][0:TW, 0:P], ACT.Copy).then_inc(q[u].sem, 1)
            for u in range(K):
                act.wait_ge(*ready(u, "act", i))
                act.activation(t["a"][u], ps[u][:, 0:P], ACT.Relu, bias=gcn_b1[:, :]).then_inc(q[u].sem, 1)

        def n5_pe(pe, q, ready, i, t=t, ps=ps):
            for u in range(K):
                pe.wait_ge(*ready(u, "s_turned", i))
                pe.matmul(ps[u][0:TW, 0:P], flat(t["s"][u]), ident[:, :], start=True, stop=True).then_inc(q[u].sem, 1)
            for u in range(K):
                pe.wait_ge(*ready(u, "hidden", i))
                pe.matmul(ps[u][:, 0:P], w_gcn1[:, :], t["sT"][u], start=True, stop=True).then_inc(q[u].sem, 1)
            for u in range(K):
                pe.wait_ge(*ready(u, "out", i))
                pe.matmul(ps[u][0:P, 0:TW], t["a"][u], w_gcn2[:, :], start=True, stop=True).then_inc(q[u].sem, 1)

        node_pass("n5", [(by_unit(big["g"]), g1_d), (by_unit(big["dis"]), dis_d)], (agg3, 1),
                  [(g2_d, "o", "o_dis")],
                  ["agg_sum", "own", "s_dis", "s_turned", "s_t", "hidden", "act", "out", "o_dis"], n5_dve, n5_act, n5_pe, st, big)

    edge_pass("e5", [(g2_d, F, "src")], "dst", F, agg4, "gcn")

    st, t, ps, big = pass_scope("n6", dict(tab=[P, S, TW], s=[P, C, F], g=[P, C, F], dis=[P, C], x=[P, C, F], o=[P, C, F]))
    with st:
        def n6_dve(dve, q, ready, i, t=t, ps=ps):
            for u in range(K):
                dve.wait_ge(*ready(u, "agg_sum", i))
                dve.tensor_reduce(flat(t["s"][u]), t["tab"][u].rearrange("p t x -> p x t"), axis=AX.X, op=ALU.add).then_inc(q[u].sem, 1)
            own_loop(dve, q, ready, i, t)
            for u in range(K):
                dve.wait_ge(*ready(u, "s_bias", i))
                dve.tensor_tensor(t["s"][u], t["s"][u], gcn_b2[:, :].unsqueeze(1).broadcast_to([P, C, F]),
                                  ALU.add).then_inc(q[u].sem, 1)
            for u in range(K):
                dve.wait_ge(*ready(u, "x_new", i))
                dve.tensor_tensor(t["o"][u], t["s"][u], t["x"][u], ALU.add).then_inc(q[u].sem, 1)

        node_pass("n6", [(by_unit(big["g"]), g2_d), (by_unit(big["dis"]), dis_d),
                         (by_unit(big["x"]), x3_d)], (agg4, 1),
                  [(out, "o", "x_new")],
                  ["agg_sum", "own", "s_dis", "s_bias", "x_new"], n6_dve, None, None, st, big)


def kernel(**inputs):
    import concourse.bacc as bacc
    from concourse.bass_utils import run_bass_kernel_spmd

    nc = bacc.Bacc("TRN2", target_bir_lowering=False, num_devices=1)
    arrays, aps = {}, {}
    for name, value in inputs.items():
        value = np.ascontiguousarray(value)
        arrays[f"in_{name}"] = value
        aps[name] = nc.dram_tensor(f"in_{name}", value.shape, mybir.dt.from_np(value.dtype), kind="ExternalInput").ap()
    out = nc.dram_tensor("out_0", (N, F), F32, kind="ExternalOutput").ap()
    gnn_kernel(nc, aps, out)
    result = run_bass_kernel_spmd(nc, [arrays], core_ids=[0])
    return result.results[0]["out_0"]
```
